# Optimizing a Trainium2 kernel written in Bass

```python
import numpy as np
import jax
import jax.numpy as jnp

def _softmax(x, axis=-1):
    return jax.nn.softmax(x, axis=axis)

def _gelu(x):
    return jax.nn.gelu(x, approximate=True)

def _silu(x):
    return jax.nn.silu(x)

def _sigmoid(x):
    return jax.nn.sigmoid(x)

def _layernorm(x, axis=-1, eps=1e-05):
    m = jnp.mean(x, axis=axis, keepdims=True)
    v = jnp.var(x, axis=axis, keepdims=True)
    return (x - m) / jnp.sqrt(v + eps)

def _scatter_add(tgt, idx, src, axis=0):
    return tgt.at[idx].add(src)

def _segment_sum(src, seg, n):
    return jax.ops.segment_sum(src, seg, n)
kernel_name = 'mk_gps_d2_gnn_r8_bffd5e'

def setup_inputs(seed: int=0):
    np.random.seed(seed)
    _w = jnp.asarray

    def _rec_inputs():
        import jax
        import jax.numpy as jnp
        _gk = jax.random.key(seed)
        x = -0.0002928 + 1 * jax.random.normal(jax.random.fold_in(_gk, 1), (1024, 512), jnp.float32)
        src = jax.random.randint(jax.random.fold_in(_gk, 2), (16384,), 0, 1024, jnp.int32)
        dst = jax.random.randint(jax.random.fold_in(_gk, 3), (16384,), 0, 1024, jnp.int32)
        _o = jnp.argsort(dst, stable=True)
        src = src[_o]
        dst = dst[_o]
        return (x, src, dst)
    x, src, dst = _rec_inputs()

    def _L0_gnn_setup():
        import jax, jax.numpy as jnp
        import numpy as np
        NUM_NODES = 1024
        NUM_EDGES = 32768
        IN_C = 512
        OUT_C = 512
        key = jax.random.key(seed)
        k1, k2, k3, k4 = jax.random.split(key, 4)
        x = jax.random.normal(k1, (NUM_NODES, IN_C), dtype=jnp.float32)
        edge_index = jax.random.randint(k2, (2, NUM_EDGES), 0, NUM_NODES, dtype=jnp.int64)
        W = jax.random.normal(k3, (OUT_C, IN_C), dtype=jnp.float32) * (1.0 / np.sqrt(IN_C))
        b = jax.random.normal(k4, (OUT_C,), dtype=jnp.float32) * 0.01
        return {'x': x, 'edge_index': edge_index, 'W': W, 'b': b}
    _L0_gnn_all = _L0_gnn_setup()
    _L0_gnn_in = {k: v for k, v in _L0_gnn_all.items() if k in ('W', 'b')}
    del _L0_gnn_all

    def _L0_mix_setup():
        import jax, jax.numpy as jnp
        import numpy as np
        DIM = 512
        HEADS = 8
        DIM_HEAD = 64
        SLICE = 32
        INNER = HEADS * DIM_HEAD
        key = jax.random.key(seed)
        ks = jax.random.split(key, 8)
        B, N = (8, 1024)
        s = 0.02
        return {'x': jax.random.normal(ks[0], (B, N, DIM), dtype=jnp.float32), 'W_in': jax.random.normal(ks[1], (DIM, INNER), dtype=jnp.float32) * s, 'b_in': jnp.zeros((INNER,), dtype=jnp.float32), 'Wq': jax.random.normal(ks[2], (DIM_HEAD, SLICE), dtype=jnp.float32) * s, 'Wk': jax.random.normal(ks[3], (DIM_HEAD, SLICE), dtype=jnp.float32) * s, 'Wv': jax.random.normal(ks[4], (DIM_HEAD, DIM_HEAD), dtype=jnp.float32) * s, 'W_out': jax.random.normal(ks[5], (INNER, DIM), dtype=jnp.float32) * s, 'b_out': jnp.zeros((DIM,), dtype=jnp.float32)}
    _L0_mix_all = _L0_mix_setup()
    _L0_mix_in = {k: v for k, v in _L0_mix_all.items() if k in ('W_in', 'b_in', 'Wq', 'Wk', 'Wv', 'W_out', 'b_out')}
    del _L0_mix_all

    def _L0_ffn_setup():
        import jax, jax.numpy as jnp
        import numpy as np
        D, H, E, B, S = (512, 256, 16, 8, 1024)
        MAX_GROUP_SIZE = 512
        MIN_CAPACITY = 8
        CAPACITY_FACTOR = 1.0

        def _group_dims(num_tokens, num_experts):
            num_groups = -(-num_tokens // MAX_GROUP_SIZE)
            while num_tokens % num_groups != 0 or num_groups % num_experts != 0:
                num_groups += 1
            return (num_tokens // num_groups, num_groups)
        key = jax.random.key(seed)
        ks = jax.random.split(key, 6)
        s = 0.02
        return {'x': jax.random.normal(ks[0], (B, S, D), jnp.float32), 'gate_w': jax.random.normal(ks[1], (D, E), jnp.float32) * s, 'w1': jax.random.normal(ks[2], (E, D, H), jnp.float32) * s, 'b1': jnp.zeros((E, H), jnp.float32), 'w2': jax.random.normal(ks[3], (E, H, D), jnp.float32) * s, 'b2': jnp.zeros((E, D), jnp.float32), 'sw1': jax.random.normal(ks[4], (D, H), jnp.float32) * s, 'sb1': jnp.zeros((H,), jnp.float32), 'sw2': jax.random.normal(ks[5], (H, D), jnp.float32) * s, 'sb2': jnp.zeros((D,), jnp.float32)}
    _L0_ffn_all = _L0_ffn_setup()
    _L0_ffn_in = {k: v for k, v in _L0_ffn_all.items() if k in ('gate_w', 'w1', 'b1', 'w2', 'b2', 'sw1', 'sb1', 'sw2', 'sb2')}
    del _L0_ffn_all

    def _L1_gnn_setup():
        import jax, jax.numpy as jnp
        import numpy as np
        N = 6250
        IN_CH = 512
        OUT_CH = 512
        DEG = 32
        E = N * DEG
        key = jax.random.key(seed)
        kx, kwc, kwn, kb, ke = jax.random.split(key, 5)
        x = jax.random.normal(kx, (N, IN_CH), dtype=jnp.float32)
        bound = 1.0 / np.sqrt(IN_CH)
        wc = jax.random.uniform(kwc, (IN_CH, OUT_CH), minval=-bound, maxval=bound, dtype=jnp.float32)
        wn = jax.random.uniform(kwn, (IN_CH, OUT_CH), minval=-bound, maxval=bound, dtype=jnp.float32)
        bias = jax.random.uniform(kb, (OUT_CH,), minval=-bound, maxval=bound, dtype=jnp.float32)
        src = jnp.repeat(jnp.arange(N, dtype=jnp.int64), DEG)
        dst = jax.random.randint(ke, (E,), 0, N, dtype=jnp.int64)
        edge_index = jnp.stack([src, dst], axis=0)
        return {'x': x, 'wc': wc, 'wn': wn, 'bias': bias, 'edge_index': edge_index}
    _L1_gnn_all = _L1_gnn_setup()
    _L1_gnn_in = {k: v for k, v in _L1_gnn_all.items() if k in ('wc', 'wn', 'bias')}
    del _L1_gnn_all

    def _L1_mix_setup():
        import jax, jax.numpy as jnp
        import numpy as np
        NUM_HEADS = 8
        key = jax.random.key(seed)
        k1, k2, k3 = jax.random.split(key, 3)
        B, N, C = (4, 512, 512)
        x = jax.random.normal(k1, (B, N, C), dtype=jnp.float32)
        w_qkv = jax.random.normal(k2, (C, 3 * C), dtype=jnp.float32) * (1.0 / np.sqrt(C))
        w_proj = jax.random.normal(k3, (C, C), dtype=jnp.float32) * (1.0 / np.sqrt(C))
        b_proj = jnp.zeros((C,), dtype=jnp.float32)
        return {'x': x, 'w_qkv': w_qkv, 'w_proj': w_proj, 'b_proj': b_proj}
    _L1_mix_all = _L1_mix_setup()
    _L1_mix_in = {k: v for k, v in _L1_mix_all.items() if k in ('w_qkv', 'w_proj', 'b_proj')}
    del _L1_mix_all

    def _L1_ffn_setup():
        import jax, jax.numpy as jnp
        import numpy as np
        B, S, D, H, E, K = (2, 1024, 512, 256, 64, 2)
        EPS = 1e-05
        key = jax.random.key(seed)
        ks = jax.random.split(key, 5)
        s = 0.02
        return {'x': jax.random.normal(ks[0], (B, S, D), dtype=jnp.float32), 'Wg': jax.random.normal(ks[1], (D, E), dtype=jnp.float32) * s, 'bg': jnp.zeros((E,), dtype=jnp.float32), 'W1': jax.random.normal(ks[2], (E, D, H), dtype=jnp.float32) * s, 'b1': jnp.zeros((E, H), dtype=jnp.float32), 'W2': jax.random.normal(ks[3], (E, H, D), dtype=jnp.float32) * s, 'b2': jnp.zeros((E, D), dtype=jnp.float32), 'gamma': jnp.ones((D,), dtype=jnp.float32), 'beta': jnp.zeros((D,), dtype=jnp.float32)}
    _L1_ffn_all = _L1_ffn_setup()
    _L1_ffn_in = {k: v for k, v in _L1_ffn_all.items() if k in ('Wg', 'bg', 'W1', 'b1', 'W2', 'b2', 'gamma', 'beta')}
    del _L1_ffn_all
    return {'x': x, 'src': src, 'dst': dst, 'L0_gnn_W': _L0_gnn_in['W'], 'L0_gnn_b': _L0_gnn_in['b'], 'L0_mix_W_in': _L0_mix_in['W_in'], 'L0_mix_b_in': _L0_mix_in['b_in'], 'L0_mix_Wq': _L0_mix_in['Wq'], 'L0_mix_Wk': _L0_mix_in['Wk'], 'L0_mix_Wv': _L0_mix_in['Wv'], 'L0_mix_W_out': _L0_mix_in['W_out'], 'L0_mix_b_out': _L0_mix_in['b_out'], 'L0_ffn_gate_w': _L0_ffn_in['gate_w'], 'L0_ffn_w1': _L0_ffn_in['w1'], 'L0_ffn_b1': _L0_ffn_in['b1'], 'L0_ffn_w2': _L0_ffn_in['w2'], 'L0_ffn_b2': _L0_ffn_in['b2'], 'L0_ffn_sw1': _L0_ffn_in['sw1'], 'L0_ffn_sb1': _L0_ffn_in['sb1'], 'L0_ffn_sw2': _L0_ffn_in['sw2'], 'L0_ffn_sb2': _L0_ffn_in['sb2'], 'L1_gnn_wc': _L1_gnn_in['wc'], 'L1_gnn_wn': _L1_gnn_in['wn'], 'L1_gnn_bias': _L1_gnn_in['bias'], 'L1_mix_w_qkv': _L1_mix_in['w_qkv'], 'L1_mix_w_proj': _L1_mix_in['w_proj'], 'L1_mix_b_proj': _L1_mix_in['b_proj'], 'L1_ffn_Wg': _L1_ffn_in['Wg'], 'L1_ffn_bg': _L1_ffn_in['bg'], 'L1_ffn_W1': _L1_ffn_in['W1'], 'L1_ffn_b1': _L1_ffn_in['b1'], 'L1_ffn_W2': _L1_ffn_in['W2'], 'L1_ffn_b2': _L1_ffn_in['b2'], 'L1_ffn_gamma': _L1_ffn_in['gamma'], 'L1_ffn_beta': _L1_ffn_in['beta']}

def reference(x, src, dst, L0_gnn_W, L0_gnn_b, L0_mix_W_in, L0_mix_b_in, L0_mix_Wq, L0_mix_Wk, L0_mix_Wv, L0_mix_W_out, L0_mix_b_out, L0_ffn_gate_w, L0_ffn_w1, L0_ffn_b1, L0_ffn_w2, L0_ffn_b2, L0_ffn_sw1, L0_ffn_sb1, L0_ffn_sw2, L0_ffn_sb2, L1_gnn_wc, L1_gnn_wn, L1_gnn_bias, L1_mix_w_qkv, L1_mix_w_proj, L1_mix_b_proj, L1_ffn_Wg, L1_ffn_bg, L1_ffn_W1, L1_ffn_b1, L1_ffn_W2, L1_ffn_b2, L1_ffn_gamma, L1_ffn_beta):
    import jax
    import jax.numpy as jnp

    def _L0_gnn_ref(x, edge_index, W, b):
        import jax, jax.numpy as jnp
        import numpy as np
        NUM_NODES = 1024
        NUM_EDGES = 32768
        IN_C = 512
        OUT_C = 512
        n = x.shape[0]
        loop = jnp.arange(n, dtype=edge_index.dtype)
        rows = jnp.concatenate([edge_index[0], loop])
        cols = jnp.concatenate([edge_index[1], loop])
        adj = jnp.zeros((n, n), dtype=jnp.float32).at[rows, cols].set(1.0)
        deg = adj.sum(axis=1)
        deg_inv_sqrt = jnp.where(deg > 0, jax.lax.rsqrt(jnp.maximum(deg, 1e-30)), 0.0)
        norm = deg_inv_sqrt[:, None] * adj * deg_inv_sqrt[None, :]
        h = x @ W.T + b
        return norm @ h

    def _L0_mix_ref(x, W_in, b_in, Wq, Wk, Wv, W_out, b_out):
        import jax, jax.numpy as jnp
        import numpy as np
        DIM = 512
        HEADS = 8
        DIM_HEAD = 64
        SLICE = 32
        INNER = HEADS * DIM_HEAD
        B, N, C = x.shape
        x_mid = (x @ W_in + b_in).reshape(B, N, HEADS, DIM_HEAD).transpose(0, 2, 1, 3)
        q = x_mid @ Wq
        k = x_mid @ Wk
        v = x_mid @ Wv
        q = jax.nn.softmax(q, axis=-1)
        k = jax.nn.softmax(k, axis=-2)
        kv = jnp.einsum('bhns,bhnc->bhsc', k, v)
        qkv = jnp.einsum('bhns,bhsc->bhnc', q, kv)
        qkv = qkv.transpose(0, 2, 1, 3).reshape(B, N, INNER)
        return qkv @ W_out + b_out

    def _L0_ffn_ref(x, gate_w, w1, b1, w2, b2, sw1, sb1, sw2, sb2):
        import jax, jax.numpy as jnp
        import numpy as np
        D, H, E, B, S = (512, 256, 16, 8, 1024)
        MAX_GROUP_SIZE = 512
        MIN_CAPACITY = 8
        CAPACITY_FACTOR = 1.0

        def _group_dims(num_tokens, num_experts):
            num_groups = -(-num_tokens // MAX_GROUP_SIZE)
            while num_tokens % num_groups != 0 or num_groups % num_experts != 0:
                num_groups += 1
            return (num_tokens // num_groups, num_groups)
        Bn, Sn, Dn = x.shape
        En = gate_w.shape[1]
        T = Bn * Sn
        group_size, num_groups = _group_dims(T, En)
        cap = max(int(round(CAPACITY_FACTOR * group_size * num_groups / En)), MIN_CAPACITY)
        xg = x.reshape(num_groups, group_size, Dn)
        logits = jnp.einsum('gsd,de->gse', xg, gate_w)
        probs = jax.nn.softmax(logits, axis=-1)
        flat_probs = probs.transpose(2, 0, 1).reshape(En, T)
        scores, tok_idx = jax.lax.top_k(flat_probs, cap)
        xf = x.reshape(T, Dn)
        toks = xf[tok_idx]
        h = jax.nn.gelu(jnp.einsum('ecd,edh->ech', toks, w1) + b1[:, None, :])
        y = jnp.einsum('ech,ehd->ecd', h, w2) + b2[:, None, :]
        y = y * scores[..., None]
        routed = jnp.zeros_like(xf).at[tok_idx.reshape(-1)].add(y.reshape(-1, Dn))
        shared = jax.nn.gelu(xf @ sw1 + sb1) @ sw2 + sb2
        out = (routed + shared).reshape(Bn, Sn, Dn)
        return out

    def _L1_gnn_ref(x, wc, wn, bias, edge_index):
        import jax, jax.numpy as jnp
        import numpy as np
        N = 6250
        IN_CH = 512
        OUT_CH = 512
        DEG = 32
        E = N * DEG
        alpha = x @ wc
        beta = x @ wn
        src, dst = (edge_index[0], edge_index[1])
        sums = jax.ops.segment_sum(beta[dst], src, num_segments=x.shape[0])
        counts = jax.ops.segment_sum(jnp.ones_like(src, dtype=beta.dtype), src, num_segments=x.shape[0])
        gamma = sums / counts[:, None]
        return alpha + gamma + bias

    def _L1_mix_ref(x, w_qkv, w_proj, b_proj):
        import jax, jax.numpy as jnp
        import numpy as np
        NUM_HEADS = 8
        B, N, C = x.shape
        H = NUM_HEADS
        D = C // H
        qkv = (x @ w_qkv).reshape(B, N, 3, H, D)
        qkv = jnp.transpose(qkv, (2, 0, 3, 1, 4))
        q, k, v = (qkv[0], qkv[1], qkv[2])
        q = jax.nn.softmax(q, axis=-1)
        k = jax.nn.softmax(jax.nn.elu(k) + 1.0, axis=-2)
        context = jnp.einsum('bhnd,bhne->bhde', k, v)
        out = jnp.einsum('bhnd,bhde->bhne', q, context)
        out = jnp.transpose(out, (0, 2, 1, 3)).reshape(B, N, C)
        return out @ w_proj + b_proj

    def _L1_ffn_ref(x, Wg, bg, W1, b1, W2, b2, gamma, beta):
        import jax, jax.numpy as jnp
        import numpy as np
        B, S, D, H, E, K = (2, 1024, 512, 256, 64, 2)
        EPS = 1e-05
        probs = jax.nn.softmax(x @ Wg + bg, axis=-1)
        topk_vals, topk_idx = jax.lax.top_k(probs, K)
        sparse_w = jnp.sum(jax.nn.one_hot(topk_idx, E, dtype=probs.dtype) * topk_vals[..., None], axis=-2)
        h = jax.nn.relu(jnp.einsum('bsd,edh->bseh', x, W1) + b1)
        expert_out = jnp.einsum('bseh,ehd->bsed', h, W2) + b2
        out = jnp.einsum('bse,bsed->bsd', sparse_w, expert_out) + x
        mu = out.mean(-1, keepdims=True)
        var = ((out - mu) ** 2).mean(-1, keepdims=True)
        return (out - mu) * jax.lax.rsqrt(var + EPS) * gamma + beta
    edge_index = jnp.stack([src, dst])
    xn = _layernorm(x, axis=-1)
    x = x + _L0_gnn_ref(xn, edge_index, L0_gnn_W, L0_gnn_b) + _L0_mix_ref(xn[None], L0_mix_W_in, L0_mix_b_in, L0_mix_Wq, L0_mix_Wk, L0_mix_Wv, L0_mix_W_out, L0_mix_b_out)[0]
    x = x + _L0_ffn_ref(_layernorm(x, axis=-1)[None], L0_ffn_gate_w, L0_ffn_w1, L0_ffn_b1, L0_ffn_w2, L0_ffn_b2, L0_ffn_sw1, L0_ffn_sb1, L0_ffn_sw2, L0_ffn_sb2)[0]
    xn = _layernorm(x, axis=-1)
    x = x + _L1_gnn_ref(xn, L1_gnn_wc, L1_gnn_wn, L1_gnn_bias, edge_index) + _L1_mix_ref(xn[None], L1_mix_w_qkv, L1_mix_w_proj, L1_mix_b_proj)[0]
    x = x + _L1_ffn_ref(_layernorm(x, axis=-1)[None], L1_ffn_Wg, L1_ffn_bg, L1_ffn_W1, L1_ffn_b1, L1_ffn_W2, L1_ffn_b2, L1_ffn_gamma, L1_ffn_beta)[0]
    return x

_drawn_inputs = setup_inputs


def setup_inputs(seed=0):
    import zlib

    import numpy as np

    out = dict(_drawn_inputs(seed))
    spreads = {'L0_mix_b_in': (0.0, 0.794),
     'L0_mix_b_out': (0.0, 0.1),
     'L0_ffn_b1': (0.0, 0.8),
     'L0_ffn_b2': (0.0, 0.607),
     'L0_ffn_sb1': (0.0, 1.474),
     'L0_ffn_sb2': (0.0, 0.279),
     'L1_mix_b_proj': (0.0, 0.285),
     'L1_ffn_bg': (0.0, 0.8),
     'L1_ffn_b1': (0.0, 0.8),
     'L1_ffn_b2': (0.0, 2.0),
     'L1_ffn_gamma': (1.0, 0.2),
     'L1_ffn_beta': (0.0, 0.454)}
    factors = {'L0_gnn_b': 16.344,
     'L0_mix_W_in': 8.0,
     'L0_mix_Wq': 8.0,
     'L0_mix_Wk': 8.0,
     'L0_mix_Wv': 5.595,
     'L0_mix_W_out': 5.85,
     'L0_ffn_gate_w': 3.491,
     'L0_ffn_w1': 5.534,
     'L0_ffn_w2': 5.169,
     'L1_gnn_bias': 7.957,
     'L1_ffn_Wg': 8.0,
     'L1_ffn_W1': 8.0,
     'L1_ffn_W2': 8.0}
    for name, (base, spread) in spreads.items():
        noise = np.random.default_rng([zlib.crc32(name.encode()), seed]).standard_normal(out[name].shape)
        drawn = base * np.exp(spread * noise) if base else spread * noise
        out[name] = jnp.asarray(drawn.astype(out[name].dtype))
    for name, factor in factors.items():
        out[name] = (out[name] * factor).astype(out[name].dtype)
    return out
```

```python
from contextlib import ExitStack

import concourse.bass as bass
from concourse import mybir

ALU = mybir.AluOpType
ACT = mybir.ActivationFunctionType
AX_X = mybir.AxisListType.X
F32 = mybir.dt.float32
F32R = mybir.dt.float32r
F16 = mybir.dt.float16
BF16 = mybir.dt.bfloat16
I32 = mybir.dt.int32
U32 = mybir.dt.uint32
RMAX = bass.bass_isa.ReduceOp.max
ds = bass.ds

P = 128
N = 1024
D = 512
NE = 16384
T = N // P
K = D // P
HEADS = 8
DH = D // HEADS
SLICE = 32
GRP = 4 * P
NG = NE // GRP
SHIFT = NG * T
HID = 256
HJ = HID // P
E0 = 16
CAP = N // E0
E1 = 64
C = 128
U = 4
MAXT = E1 + (2 * N - E1) // C + U
MAXT -= MAXT % U
EPS = 1e-5


def build(nc, A, out):
    with ExitStack() as ctx:
        def sb(name, shape, dt=F32):
            return ctx.enter_context(nc.sbuf_tensor(name, shape, dt))

        def rounded(name, shape):
            return nc.alloc_sbuf_tensor_at(name, shape, F32R, offset=-(-nc.sbuf_base // 32) * 32)

        norms = dict(var_ready=1, sd_ready=1, xn_ready=T, xT_ready=2 * K, xT_done=2 * K)
        layers = dict(h_ready=T, h_done=T, gnn_ready=T, gnn_done=T, k_ready=4, k_done=4, v_ready=T, v_done=T,
                      q_ready=T, q_done=T, q_shifted=T, q_exp=T, q_soft=T, kmax_ready=2, k_exp=2, kr_ready=4,
                      kr_done=4, qT_ready=4, qT_done=4, kv_ready=2, kv_done=2, oT_ready=2 * K, oT_done=2 * K,
                      mix_ready=T, mix_done=T, logit_ready=1, logit_shifted=1, logit_exp=1, probs_ready=1,
                      rb_ready=T, rb_done=T, eT_ready=E0, eT_done=E0, eh_ready=E0, eh_done=E0, ey_ready=E0,
                      ey_done=E0)
        adds = {**norms, **layers}
        sems = {}

        def S(name):
            name = name[:-1] if name[:-1] in adds else name
            if name not in sems:
                sems[name] = ctx.enter_context(nc.semaphore(name))
            return sems[name]

        def count(name, n):
            return S(name), n + (adds[name[:-1]] * int(name[-1]) if name[:-1] in adds else 0)

        tok0_d = nc.dram_tensor("tok0_scratch", (N, D), F32).ap()
        acc0_d = nc.dram_tensor("acc0_scratch", (N, D), F32).ap()
        slot_d = nc.dram_tensor("slot_scratch", (MAXT * C, D), F32).ap()

        X = sb("X", [P, T, D])
        XN = sb("XN", [P, T, D])
        XT = sb("XT", [P, K, N])
        H_lo = rounded("H_lo", [P, T, D])
        H = sb("H", [P, T, D])
        CT = sb("CT", [P, T, N])
        AT = rounded("AT", [P, T, N])
        later = sb("later", [P, T * N])
        H_hi = rounded("H_hi", [P, T, D])
        B1 = sb("B1", [P, 4096])
        W = sb("W", [P, 4, K, D])
        BC = sb("BC", [P, 5, D])
        BG = sb("BG", [P, E1])

        ident = sb("ident", [P, P])
        onescol = sb("onescol", [P, 1])
        ones_b = sb("ones_b", [P, P], BF16)
        tri_b = sb("tri_b", [P, P], BF16)
        zero_b = sb("zero_b", [P, D], BF16)
        zero_f = sb("zero_f", [P, D])
        iota_h = sb("iota_h", [P, N], F16)
        iota_e = sb("iota_e", [P, E1])
        pcol_i = sb("pcol_i", [P, 1], I32)
        pcol = sb("pcol", [P, 1])
        epsc = sb("epsc", [P, 1])

        edge_c = sb("edge_c", [P, 2, P])
        ends = sb("ends", [P, 2, 4])
        gmm = sb("gmm", [NG, 2])
        gov = sb("gov", [NG, 5, T])
        gval = sb("gval", [NG, 2 * T])
        gred = sb("gred", [NG, 2 * T])
        grow = sb("grow", [1, 6, T])
        grow_i = sb("grow_i", [1, 2, T], I32)

        cols_sm = sb("cols_sm", [P, 256])
        BDQ = sb("BDQ", [P, 2 * SLICE])
        BDK = sb("BDK", [P, 2 * SLICE])
        BDV = sb("BDV", [P, 2 * DH])
        GW = sb("GW", [P, K, E0 + E1])
        B2R0 = sb("B2R0", [E0, D])

        st = sb("st", [P, T, 6])
        mv = sb("mv", [P, T, 2])
        sd = sb("sd", [P, T])
        rs = sb("rs", [P, T])
        deg = sb("deg", [P, 2 * T])
        dinv = sb("dinv", [P, T])
        rcnt = sb("rcnt", [P, T])
        kmax = sb("kmax", [P, K])
        ksum = sb("ksum", [P, K])
        krec = sb("krec", [P, K])
        qm = sb("qm", [P, T, HEADS])
        qs = sb("qs", [P, T, HEADS])
        qr = sb("qr", [P, T, HEADS])
        KV = sb("KV", [P, D])

        PR = sb("PR", [P, T, E1])
        pm = sb("pm", [P, T])
        psm = sb("psm", [P, T])
        pr_ = sb("pr_", [P, T])
        sc0 = sb("sc0", [E0, CAP])
        ix0 = sb("ix0", [E0, CAP], U32)
        ixf0 = sb("ixf0", [E0, CAP])
        scT = sb("scT", [CAP, 2 * E0])
        ic0 = sb("ic0", [CAP, E0], I32)
        icur = sb("icur", [CAP, U], I32)
        top8 = sb("top8", [P, T, 8])
        ti8 = sb("ti8", [P, T, 8], U32)
        tif = sb("tif", [P, T, 2])
        slot_f = sb("slot_f", [P, 2, T])
        slot_i = sb("slot_i", [P, 2, T], I32)
        cnti = sb("cnti", [P, E1], I32)
        ecol = sb("ecol", [P, 1])
        trow_i = sb("trow_i", [1, P + 2], I32)

        PS = ctx.enter_context(nc.psum_tensor("PS", [P, 8, 512], F32))

        early = H[:, :, :].rearrange("p a b -> p (a b)")
        iota_i = early[:, 0:N].bitcast(I32)
        edge_i = early[:, N:N + 2 * P].bitcast(I32).rearrange("p (a b) -> p a b", a=2)
        edge_f = early[:, N + 2 * P:N + 4 * P].rearrange("p (a b) -> p a b", a=2)
        dgrp_i = early[0:NG, 2048:2048 + GRP].bitcast(I32)
        rows_sm = early[0:E1, 3072:3584].rearrange("p (a b) -> p a b", a=2)
        ATf = later[:, :]
        CTf = CT[:, :, :].rearrange("p a b -> p (a b)")
        Hf = H[:, :, :].rearrange("p a b -> p (a b)")
        onehot_s = B1[:, 0:2048].bitcast(BF16).rearrange("p (j n) -> p j n", j=4)
        onehot_d = B1[:, 2048:2304].bitcast(BF16).rearrange("p (j n) -> p j n", j=4)
        XM = ATf[:, 0:4096].rearrange("p (c n) -> p c n", c=K)
        V = ATf[:, 4096:8192].rearrange("p (t n) -> p t n", t=T)
        Q = B1[:, :].rearrange("p (t n) -> p t n", t=T)
        OT = B1[:, :].rearrange("p (c n) -> p c n", c=K)
        KTr = XN[:, :, :].rearrange("p a b -> p (a b)").rearrange("p (c n) -> p c n", c=K)
        QT = KTr
        KR = H
        SHT = B1[:, 0:2048].rearrange("p (j n) -> p j n", j=HJ)
        PT = B1[0:E0, 2048:3072]
        PTW = B1[0:E0, 3072:4096]
        O1 = CTf[:, 0:512].rearrange("p (t e) -> p t e", t=T)
        O2 = CTf[:, 512:1024].rearrange("p (t e) -> p t e", t=T)
        MB = CTf[:, 1024:1280].bitcast(BF16).rearrange("p (t e) -> p t e", t=T)
        SWW = CTf[:, 1280:1792].rearrange("p (t e) -> p t e", t=T)
        SL = CTf[:, 1792:2304].rearrange("p (t e) -> p t e", t=T)
        SLT = CTf[:, 2304:2816].rearrange("p (t e) -> p t e", t=T)
        SWT = CTf[0:E1, 2816:3840]
        cntb = CTf[:, 6144:6144 + 6 * E1].rearrange("p (a e) -> p a e", e=E1)
        B2R1 = CTf[0:E1, 6656:6656 + D]
        trow = CTf[0:1, 7168:7168 + P + 1]
        EW = [ATf[:, u * 2048:(u + 1) * 2048] for u in range(U)]
        EW1 = [w[:, 0:1024].rearrange("p (k n) -> p k n", k=K) for w in EW]
        EW2 = [w[:, 1024:2048].rearrange("p (j n) -> p j n", j=HJ) for w in EW]

        def expert_space(f, n):
            g = [f[0:n, u * D:(u + 1) * D] for u in range(U)]
            at = U * D
            gt = [f[:, at + b * K * n:at + (b + 1) * K * n].rearrange("p (k n) -> p k n", k=K) for b in range(2)]
            at += 2 * K * n
            ht = [f[:, at + b * HJ * n:at + (b + 1) * HJ * n].rearrange("p (j n) -> p j n", j=HJ) for b in range(2)]
            return g, gt, ht

        G0, GT0, HT0 = expert_space(Hf, CAP)
        Y0 = [Hf[0:CAP, 2816 + b * D:2816 + (b + 1) * D] for b in range(2)]
        G1, GT1, HT1 = expert_space(Hf, C)
        Y1 = [B1[0:C, u * D:(u + 1) * D] for u in range(U)]
        YG = [CTf[:, 4096 + b * D:4096 + (b + 1) * D] for b in range(4)]
        ZR = CTf[:, 0:4096].rearrange("p (t n) -> p t n", t=T)

        wv = lambda ap: ap.rearrange("(k p) n -> p k n", p=P)
        block = ctx.enter_context(nc.Block())

        @block.sync
        def _(sp):
            for h in range(2):
                sp.dma_start(X[:, 4 * h:4 * h + 4, :], A["x"].rearrange("(t p) d -> p t d", p=P)[:, 4 * h:4 * h + 4, :]
                             ).then_inc(S(f"x_in{h}"), 16)
            for i, n in enumerate(("src", "dst")):
                sp.dma_start(edge_i[:, i, :], A[n].rearrange("(c e) -> c e", e=P)).then_inc(S("edges_in"), 16)
            sp.dma_start(dgrp_i[:, :], A["dst"].rearrange("(g e) -> g e", e=GRP)).then_inc(S("edges_in"), 16)
            sp.dma_start(W[:, 0], wv(A["L0_gnn_W"])).then_inc(S("gnnw_in"), 16)
            for b, n, e in ((0, "L0_ffn_b1", E0), (1, "L1_ffn_b1", E1)):
                sp.dma_start(rows_sm[0:e, b, :], A[n]).then_inc(S("small_in"), 16)
            sp.dma_start(W[:, 1], wv(A["L0_mix_W_in"])).then_inc(S("win_in"), 16)
            for n, at in (("L0_gnn_b", 0), ("L0_mix_b_out", 1), ("L0_ffn_sb2", 2), ("L1_gnn_bias", 3),
                          ("L1_mix_b_proj", 4)):
                sp.dma_start(BC[:, at, :], A[n].partition_broadcast(P)).then_inc(S("bias_in"), 16)
            sp.dma_start(BG[:, :], A["L1_ffn_bg"].partition_broadcast(P)).then_inc(S("bias_in"), 16)
            sp.dma_start(cols_sm[:, 192:196], A["L0_mix_b_in"].rearrange("(c p) -> p c", p=P),
                         allow_slow_non_contiguous=True).then_inc(S("bias_in"), 16)
            sp.dma_start(cols_sm[:, 196:198], A["L0_ffn_sb1"].rearrange("(c p) -> p c", p=P),
                         allow_slow_non_contiguous=True).then_inc(S("bias_in"), 16)
            sp.wait_ge(*count("bd_zero", 3))
            for h in range(2):
                r = slice(h * DH, (h + 1) * DH)
                sp.dma_start(BDQ[r, h * SLICE:(h + 1) * SLICE], A["L0_mix_Wq"]).then_inc(S("bd_in"), 16)
                sp.dma_start(BDK[r, h * SLICE:(h + 1) * SLICE], A["L0_mix_Wk"]).then_inc(S("bd_in"), 16)
                sp.dma_start(BDV[r, h * DH:(h + 1) * DH], A["L0_mix_Wv"]).then_inc(S("bd_in"), 16)
            sp.dma_start(W[:, 2], wv(A["L0_mix_W_out"])).then_inc(S("wout_in"), 16)
            sp.dma_start(GW[:, :, 0:E0], wv(A["L0_ffn_gate_w"])).then_inc(S("gate_in"), 16)
            sp.dma_start(GW[:, :, E0:], wv(A["L1_ffn_Wg"])).then_inc(S("gate_in"), 16)
            sp.dma_start(B2R0[:, :], A["L0_ffn_b2"]).then_inc(S("gate_in"), 16)
            sp.wait_ge(*count("zeros_ready", 2))
            rows = MAXT * C // 4
            for q in range(4):
                sp.dma_start(slot_d[q * rows:(q + 1) * rows].rearrange("(a p) d -> p a d", p=P),
                             zero_f[:, :].unsqueeze(1).to_broadcast([P, rows // P, D])).then_inc(S("slots_zeroed"), 16)
            sp.wait_ge(*count("wT_ready", K))
            sp.dma_start(W[:, 0, 0:2, :].rearrange("p a b -> p (a b)").rearrange("p (k n) -> p k n", k=K),
                         wv(A["L0_ffn_sw1"])).then_inc(S("shared_in"), 16)
            sp.dma_start(W[:, 0, 2:4, :], wv(A["L0_ffn_sw2"])).then_inc(S("shared_in"), 16)
            qkv = A["L1_mix_w_qkv"].rearrange("(k p) n -> p k n", p=P)
            sp.wait_ge(*count("xm_ready", 2 * K))
            sp.dma_start(W[:, 1], qkv[:, :, 0:D]).then_inc(S("wq_in"), 16)
            sp.wait_ge(*count("h_ready0", T))
            sp.dma_start(W[:, 3], wv(A["L1_gnn_wn"])).then_inc(S("wn_in"), 16)
            sp.wait_ge(*count("mix_ready0", T))
            sp.dma_start(W[:, 2], qkv[:, :, 2 * D:3 * D]).then_inc(S("wv_in"), 16)

            sp.wait_ge(*count("xn_ready1", T))
            sp.dma_start(tok0_d.rearrange("(t p) d -> p t d", p=P), XN[:, :, :]).then_inc(S("tok0_out"), 16)

            def load0(i, u):
                e = U * i + u
                sp.dma_start(EW1[u], A["L0_ffn_w1"][ds(e, 1)].rearrange("a (k p) n -> p (a k) n", p=P)
                             ).then_inc(S(f"ew0_in{u}"), 16)
                sp.dma_start(EW2[u], A["L0_ffn_w2"][ds(e, 1)].rearrange("a (k p) n -> p (a k) n", p=P)
                             ).then_inc(S(f"ew0_in{u}"), 16)

            for u in range(U):
                load0(0, u)
            sp.wait_ge(*count("resid0_ready", T))
            sp.dma_start(acc0_d.rearrange("(t p) d -> p t d", p=P), X[:, :, :]).then_inc(S("acc0_out"), 16)
            with sp.Fori(1, E0 // U) as i:
                for u in range(U):
                    sp.wait_ge(*count("ey_ready0", U * i + (u + 1 - U)))
                    load0(i, u)
            sp.wait_ge(*count("scattered0", 16 * E0))
            sp.dma_start(X[:, :, :], acc0_d.rearrange("(t p) d -> p t d", p=P)).then_inc(S("acc0_in"), 16)
            sp.wait_ge(*count("shared_ready", T))
            sp.dma_start(W[:, 0], qkv[:, :, D:2 * D]).then_inc(S("wk_in"), 16)
            sp.wait_ge(*count("h_ready1", T))
            sp.dma_start(W[:, 3], wv(A["L1_gnn_wc"])).then_inc(S("wc_in"), 16)
            sp.wait_ge(*count("q_ready1", T))
            sp.dma_start(W[:, 1], wv(A["L1_mix_w_proj"])).then_inc(S("proj_in"), 16)

            sp.wait_ge(*count("gnn_ready1", T))
            sp.dma_start(B2R1, A["L1_ffn_b2"]).then_inc(S("late_in"), 16)
            sp.dma_start(BC[:, 0, :], A["L1_ffn_gamma"].partition_broadcast(P)).then_inc(S("late_in"), 16)
            sp.dma_start(BC[:, 1, :], A["L1_ffn_beta"].partition_broadcast(P)).then_inc(S("late_in"), 16)

            sp.wait_ge(*count("table_ready", 2))
            turns = sp.value_load(trow_i[0:1, P:P + 1], min_val=3, max_val=MAXT // U)

            def load1(i, u):
                e = sp.value_load(trow_i[0:1, ds(U * i + u, 1)], min_val=0, max_val=E1 - 1)
                sp.dma_start(EW1[u], A["L1_ffn_W1"][ds(e, 1)].rearrange("a (k p) n -> p (a k) n", p=P)
                             ).then_inc(S(f"ew1_in{u}"), 16)
                sp.dma_start(EW2[u], A["L1_ffn_W2"][ds(e, 1)].rearrange("a (k p) n -> p (a k) n", p=P)
                             ).then_inc(S(f"ew1_in{u}"), 16)
                sp.dma_start(G1[u], slot_d[ds((U * i + u) * C, C), :]).then_inc(S(f"ew1_in{u}"), 16)

            def store1(i, u):
                sp.wait_ge(*count("ey_done1", U * i + u + 1))
                sp.dma_start(slot_d[ds((U * i + u) * C, C), :], Y1[u]).then_inc(S(f"y1_out{u}"), 16)

            sp.wait_ge(*count("mix_ready1", T))
            sp.wait_ge(*count("dispatched", 16 * 2 * T))
            for u in range(U):
                load1(0, u)
            with sp.Fori(1, turns) as i:
                for u in range(U):
                    sp.wait_ge(*count("ey_ready1", U * i + (u + 1 - U)))
                    load1(i, u)
                    store1(i - 1, u)
            for u in range(U):
                store1(turns - 1, u)
            for h in range(2):
                sp.wait_ge(*count("out_ready", 4 * (h + 1)))
                sp.dma_start(out.rearrange("(t p) d -> p t d", p=P)[:, 4 * h:4 * h + 4, :],
                             X[:, 4 * h:4 * h + 4, :]).then_inc(S("stored"), 16)
            sp.wait_ge(*count("stored", 32))

        @block.gpsimd
        def _(pool):
            pool.memset(ident[:, :], 0.0).then_inc(S("cst"), 1)
            pool.memset(zero_f[:, :], 0.0).then_inc(S("zeros_ready"), 1)
            pool.memset(zero_b[:, :], 0.0).then_inc(S("zeros_ready"), 1)
            pool.memset(BDQ[:, :], 0.0).then_inc(S("bd_zero"), 1)
            pool.memset(BDK[:, :], 0.0).then_inc(S("bd_zero"), 1)
            pool.memset(BDV[:, :], 0.0).then_inc(S("bd_zero"), 1)
            pool.memset(onescol[:, :], 1.0).then_inc(S("consts"), 1)
            pool.memset(ones_b[:, :], 1.0).then_inc(S("consts"), 1)
            pool.memset(tri_b[:, :], 1.0).then_inc(S("cst"), 1)
            pool.iota(iota_i[:, :], [[1, N]], base=0, channel_multiplier=0).then_inc(S("consts"), 1)
            pool.iota(pcol_i[:, :], [[0, 1]], base=0, channel_multiplier=1).then_inc(S("consts"), 1)
            pool.memset(epsc[:, :], EPS).then_inc(S("consts"), 1)
            pool.wait_ge(*count("cst", 2))
            pool.affine_select(out=ident[:, :], in_=ident[:, :], compare_op=ALU.not_equal, fill=1.0, base=0,
                               pattern=[[-1, P]], channel_multiplier=1).then_inc(S("consts"), 1)
            pool.affine_select(out=tri_b[:, :], in_=tri_b[:, :], compare_op=ALU.is_gt, fill=0.0, base=0,
                               pattern=[[1, P]], channel_multiplier=-1).then_inc(S("consts"), 1)
            pool.wait_ge(*count("gval_ready", 2))
            pool.partition_all_reduce(gred[:, :], gval[:, :], NG, RMAX).then_inc(S("gred_ready"), 1)

            pool.wait_ge(*count("bias_in", 16 * 8))
            for m in range(T):
                pool.wait_ge(*count("h_done0", m + 1))
                pool.tensor_tensor(H[:, m, :], H[:, m, :], BC[:, 0, :], ALU.add).then_inc(S("h_biased"), 1)

            def gather0(i, u):
                e = U * i + u
                pool.tensor_copy(icur[:, u:u + 1], ic0[:, ds(e, 1)]).then_inc(S("icur_set"), 1)
                pool.wait_ge(*count("icur_set", e + 1))
                pool.sem_inc(S("pool_passed"))
                pool.indirect_dma_start(G0[u], None, tok0_d, bass.IndirectOffsetOnAxis(ap=icur[:, u:u + 1], axis=0)
                                        ).then_inc(S(f"g0_in{u}"), 16)

            def scatter0(i, u):
                e = U * i + u
                pool.wait_ge(*count("ey_done0", e + 1))
                pool.sem_inc(S("pool_passed"))
                pool.indirect_dma_start(acc0_d, bass.IndirectOffsetOnAxis(ap=icur[:, u:u + 1], axis=0), Y0[u % 2], None,
                                        compute_op=ALU.add).then_inc(S("scattered0"), 16)
                pool.wait_ge(*count("scattered0", 16 * (e + 1)))

            pool.wait_ge(*count("ic0_ready", 1))
            pool.wait_ge(*count("tok0_out", 16))
            pool.wait_ge(*count("mix_ready0", T))
            for u in range(U):
                gather0(0, u)
            pool.wait_ge(*count("acc0_out", 16))
            with pool.Fori(1, E0 // U) as i:
                for u in range(U):
                    scatter0(i - 1, u)
                    gather0(i, u)
            for u in range(U):
                scatter0(E0 // U - 1, u)

            pool.wait_ge(*count("slot_ready", 2))
            pool.wait_ge(*count("slots_zeroed", 64))
            for t in range(T):
                for c in range(2):
                    pool.indirect_dma_start(slot_d, bass.IndirectOffsetOnAxis(ap=slot_i[:, c, t:t + 1], axis=0),
                                            XN[:, t, :], None).then_inc(S("dispatched"), 16)
            turns = pool.value_load(trow_i[0:1, P:P + 1], min_val=3, max_val=MAXT // U)
            for u in range(U):
                pool.wait_ge(*count(f"y1_out{u}", 16 * turns))
            pool.sem_inc(S("pool_passed"))
            for t in range(T):
                for c in range(2):
                    n = 2 * t + c
                    if n >= 4:
                        pool.wait_ge(*count("combined", n - 3))
                    pool.indirect_dma_start(YG[n % 4], None, slot_d,
                                            bass.IndirectOffsetOnAxis(ap=slot_i[:, c, t:t + 1], axis=0)
                                            ).then_inc(S(f"yg_in{n % 4}"), 16)

        @block.scalar
        def _(act):
            def norm_root(n):
                act.wait_ge(*count(f"var_ready{n}", 1))
                act.activation(sd[:, :], mv[:, :, 1], ACT.Sqrt, bias=epsc[:, 0:1]).then_inc(S(f"sd_ready{n}"), 1)

            def evict_xT(n):
                for i in range(2 * K):
                    act.wait_ge(*count(f"xT_ready{n}", i + 1))
                    act.activation(XT[:, i % K, (i // K) * 512:(i // K + 1) * 512], PS[:, i % 4, :], ACT.Copy
                                   ).then_inc(S(f"xT_done{n}"), 1)

            act.wait_ge(*count("consts", 7))
            norm_root(0)
            for k in range(K):
                act.wait_ge(*count("wT_ready", k + 1))
                act.activation(W[:, 3, k, :], PS[:, 4 + k, :], ACT.Copy).then_inc(S("wT_done"), 1)
            evict_xT(0)
            act.wait_ge(*count("grow_ready", 1))
            for m in range(T):
                act.wait_ge(*count("ct_ready", m + 1))
                for h in range(2):
                    act.activation(CT[:, m, h * 512:(h + 1) * 512], PS[:, 2 * (m % 2) + h, :], ACT.Copy
                                   ).then_inc(S("ct_done"), 1)
                act.wait_ge(*count("h_ready0", m + 1))
                act.activation(H[:, m, :], PS[:, 4 + m % 3, :], ACT.Copy).then_inc(S("h_done0"), 1)
            act.wait_ge(*count("deg_done", 1))
            act.activation(sd[:, :], deg[:, 0:T], ACT.Sqrt).then_inc(S("degroot_ready"), 1)
            act.wait_ge(*count("dinv_ready", 1))
            for m in range(T):
                act.wait_ge(*count("h_biased", m + 1))
                act.activation(H_hi[:, m, :], H[:, m, :], ACT.Copy, scale=dinv[:, m:m + 1]
                               ).then_inc(S("h_rounded"), 1)

            def exp_q(L):
                for t in range(T):
                    w = HEADS * (SLICE if L == 0 else DH)
                    act.wait_ge(*count(f"q_shifted{L}", t + 1))
                    act.activation(Q[:, t, 0:w], Q[:, t, 0:w], ACT.Exp).then_inc(S(f"q_exp{L}"), 1)

            def evict_v(L):
                for m in range(T):
                    act.wait_ge(*count(f"v_ready{L}", m + 1))
                    act.activation(V[:, m, :], PS[:, 4 + m % 4, :], ACT.Copy).then_inc(S(f"v_done{L}"), 1)

            def exp_k(L, g):
                act.wait_ge(*count(f"kmax_ready{L}", g + 1))
                act.activation(KTr[:, g, :], KTr[:, g, :], ACT.Exp, bias=kmax[:, g:g + 1],
                               accum_out=ksum[:, g:g + 1]).then_inc(S(f"k_exp{L}"), 1)

            def evict_kr(L):
                w = HEADS * (SLICE if L == 0 else DH)
                per = 512 // w
                for i in range(T // per):
                    act.wait_ge(*count(f"kr_ready{L}", i + 1))
                    for j in range(per):
                        ins = act.activation(KR[:, i * per + j, 0:w], PS[:, i % 4, j * w:(j + 1) * w], ACT.Copy)
                    ins.then_inc(S(f"kr_done{L}"), 1)

            def evict_qT(L):
                for i in range(2 * (2 if L == 0 else K)):
                    act.wait_ge(*count(f"qT_ready{L}", i + 1))
                    act.activation(QT[:, i // 2, (i % 2) * 512:(i % 2 + 1) * 512], PS[:, 4 + i % 4, :], ACT.Copy
                                   ).then_inc(S(f"qT_done{L}"), 1)

            def evict_oT(L):
                for i in range(2 * K):
                    act.wait_ge(*count(f"oT_ready{L}", i + 1))
                    act.activation(OT[:, i // 2, (i % 2) * 512:(i % 2 + 1) * 512], PS[:, 4 + i % 4, :], ACT.Copy
                                   ).then_inc(S(f"oT_done{L}"), 1)

            def softmax_exp(n):
                act.wait_ge(*count(f"logit_shifted{n}", 1))
                w = (E0, E1)[n]
                act.activation(PR[:, :, 0:w], PR[:, :, 0:w], ACT.Exp).then_inc(S(f"logit_exp{n}"), 1)

            act.wait_ge(*count("bias_in", 16 * 8))
            act.wait_ge(*count("gnn_ready0", T))
            for i in range(2 * K):
                act.wait_ge(*count("xm_ready", i + 1))
                act.activation(XM[:, i // 2, (i % 2) * 512:(i % 2 + 1) * 512], PS[:, 4 + i % 4, :], ACT.Identity,
                               bias=cols_sm[:, 192 + i // 2:193 + i // 2]).then_inc(S("xm_done"), 1)
            for i in range(4):
                act.wait_ge(*count("k_ready0", i + 1))
                act.activation(KTr[:, i // 2, (i % 2) * 512:(i % 2 + 1) * 512], PS[:, i % 4, :], ACT.Copy
                               ).then_inc(S("k_done0"), 1)
            evict_v(0)
            for g in range(2):
                exp_k(0, g)
            exp_q(0)
            evict_kr(0)
            evict_qT(0)
            evict_oT(0)
            norm_root(1)
            evict_xT(1)
            softmax_exp(0)
            for i in range(2 * HJ):
                act.wait_ge(*count("sh_ready", i + 1))
                act.activation(SHT[:, i // 2, (i % 2) * 512:(i % 2 + 1) * 512], PS[:, 4 + i % 4, :],
                               ACT.Gelu_apprx_tanh, bias=cols_sm[:, 196 + i // 2:197 + i // 2]
                               ).then_inc(S("sh_done"), 1)

            def expert(L, i, u, first):
                e = U * i + u
                n, gt, ht = (CAP, GT0, HT0) if L == 0 else (C, GT1, HT1)
                b = u % 2
                act.wait_ge(*count(f"eT_ready{L}", e + 1))
                if not (first and u < 2):
                    act.wait_ge(*count(f"eh_ready{L}", e - 1))
                act.activation(gt[b].rearrange("p k n -> p (k n)"), PS[:, b, 0:K * n], ACT.Copy
                               ).then_inc(S(f"eT_done{L}"), 1)
                act.wait_ge(*count(f"eh_ready{L}", e + 1))
                if not (first and u < 2):
                    act.wait_ge(*count(f"ey_ready{L}", e - 1))
                if L == 1:
                    x = act.value_load(trow_i[0:1, ds(e, 1)], min_val=0, max_val=E1 - 1)
                    bias = [cols_sm[:, ds(x + (32 + j * E1), 1)] for j in range(HJ)]
                else:
                    bias = [cols_sm[:, ds(e + j * E0, 1)] for j in range(HJ)]
                for j in range(HJ):
                    ins = act.activation(ht[b][:, j, :], PS[:, 2 + b, j * n:(j + 1) * n],
                                         ACT.Gelu_apprx_tanh if L == 0 else ACT.Relu, bias=bias[j])
                ins.then_inc(S(f"eh_done{L}"), 1)

            for u in range(U):
                expert(0, 0, u, True)
            with act.Fori(1, E0 // U) as i:
                for u in range(U):
                    expert(0, i, u, False)

            norm_root(2)
            evict_xT(2)
            for m in range(T):
                act.wait_ge(*count("h_ready1", m + 1))
                act.activation(H[:, m, :], PS[:, 4 + m % 4, :], ACT.Copy).then_inc(S("h_done1"), 1)
            for i in range(2 * K):
                act.wait_ge(*count("k_low", i + 1))
                k = KTr[:, i // 2, (i % 2) * 512:(i % 2 + 1) * 512]
                act.activation(k, k, ACT.Exp).then_inc(S("k_elu"), 1)
            evict_v(1)
            for g in range(K):
                exp_k(1, g)
            exp_q(1)
            act.wait_ge(*count("gnn_ready1", T))
            evict_kr(1)
            evict_qT(1)
            evict_oT(1)
            norm_root(3)
            evict_xT(3)
            softmax_exp(1)
            act.wait_ge(*count("table_ready", 2))
            turns = act.value_load(trow_i[0:1, P:P + 1], min_val=3, max_val=MAXT // U)
            for u in range(U):
                expert(1, 0, u, True)
            with act.Fori(1, turns) as i:
                for u in range(U):
                    expert(1, i, u, False)
            norm_root(4)

        @block.tensor
        def _(pe):
            def tr(bank, c0, in_, w=P):
                rows = in_.shape[0]
                return pe.transpose(PS[0:w, bank, c0:c0 + rows], in_, ident[0:rows, 0:rows])

            def transposes(n):
                for i in range(2 * K):
                    half, k = i // K, i % K
                    pe.wait_ge(*count(f"xn_ready{n}", 4 * (half + 1)))
                    if i >= 4:
                        pe.wait_ge(*count(f"xT_done{n}", i - 3))
                    for j in range(4):
                        ins = tr(i % 4, j * P, XN[:, 4 * half + j, k * P:(k + 1) * P])
                    ins.then_inc(S(f"xT_ready{n}"), 1)

            def token_rows(name, base, pairs, done, width=D):
                for m in range(T):
                    if m >= 4:
                        pe.wait_ge(*count(done, m - 3))
                    for n, (left, right) in enumerate(pairs):
                        ins = pe.matmul(PS[:, base + m % 4, 0:width], left[:, m * P:(m + 1) * P], right,
                                        start=(n == 0), stop=(n == len(pairs) - 1))
                    ins.then_inc(S(name), 1)

            pe.wait_ge(*count("consts", 7))
            pe.wait_ge(*count("edge_f_ready", 2))
            pe.wait_ge(*count("small_in", 32))
            tr(0, 0, edge_f[:, 0, :])
            tr(0, P, edge_f[:, 1, :]).then_inc(S("small_ready"), 1)
            for j in range(HJ):
                tr(1, j * E0, rows_sm[0:E0, 0, j * P:(j + 1) * P])
                ins = tr(1, 32 + j * E1, rows_sm[0:E1, 1, j * P:(j + 1) * P])
            ins.then_inc(S("small_ready"), 1)
            pe.wait_ge(*count("gnnw_in", 16))
            for k in range(K):
                for j in range(K):
                    ins = tr(4 + k, j * P, W[:, 0, j, k * P:(k + 1) * P])
                ins.then_inc(S("wT_ready"), 1)
            pe.wait_ge(*count("small_done", 2))
            transposes(0)

            pe.nop().then_inc(S("onehot_free"), 2)
            pe.wait_ge(*count("xT_done0", 2 * K))
            pe.wait_ge(*count("zeros_ready", 2))
            pe.wait_ge(*count("grow_ready", 1))
            pe.wait_ge(*count("wT_done", K))

            def degree_parts(k):
                pe.wait_ge(*count("ct_done", 2 * (k + 1)))
                pe.wait_ge(*count("at_done", k + 1))
                for m in range(T):
                    pe.matmul(PS[:, 7, k * T + m:k * T + m + 1], AT[:, k, m * P:(m + 1) * P].bitcast(F32),
                              onescol[:, :], start=True, stop=True, skip_group_check=True)
                    ins = pe.matmul(PS[:, 7, T * T + k * T + m:T * T + k * T + m + 1], CT[:, k, m * P:(m + 1) * P],
                                    onescol[:, :], start=True, stop=True, skip_group_check=True)
                ins.then_inc(S("deg_ready"), 1)

            start = 0
            for m in range(T):
                if m >= 2:
                    pe.wait_ge(*count("ct_done", 2 * (m - 1)))
                banks = [PS[:, 2 * (m % 2) + h, :] for h in range(2)]
                for h in range(2):
                    pe.matmul(banks[h], zero_b[:, 0:P], zero_b[:, :], start=True, stop=False)
                end = pe.value_load(grow_i[0:1, 1, m:m + 1], min_val=1, max_val=NG * (m + 1))
                with pe.Fori(start, end) as v:
                    for j in range(4):
                        if j % 2 == 0:
                            pe.wait_ge(*count("onehot_ready", v * 2 + (j // 2 + 1)))
                        pe.matmul(banks[0], onehot_d[:, j, :], onehot_s[:, j, 0:512], start=False, stop=False)
                        ins = pe.matmul(banks[1], onehot_d[:, j, :], onehot_s[:, j, 512:1024], start=False, stop=False)
                        if j % 2 == 1:
                            ins.then_inc(S("onehot_free"), 1)
                start = end
                pe.matmul(banks[0], zero_b[:, 0:P], zero_b[:, :], start=False, stop=True)
                pe.matmul(banks[1], zero_b[:, 0:P], zero_b[:, :], start=False, stop=True).then_inc(S("ct_ready"), 1)
                if m >= 3:
                    pe.wait_ge(*count("h_done0", m - 2))
                for k in range(K):
                    ins = pe.matmul(PS[:, 4 + m % 3, :], XT[:, k, m * P:(m + 1) * P], W[:, 3, k, :],
                                    start=(k == 0), stop=(k == K - 1))
                ins.then_inc(S("h_ready0"), 1)
                if m >= 1:
                    degree_parts(m - 1)
            degree_parts(T - 1)
            pe.wait_ge(*count("h_done0", T))
            pe.wait_ge(*count("deg_done", 1))
            for m in range(T):
                if m >= 4:
                    pe.wait_ge(*count("gnn_done0", m - 3))
                for k in range(T):
                    if m == 0:
                        pe.wait_ge(*count("h_split", k + 1))
                    pe.matmul(PS[:, 4 + m % 4, :], AT[:, k, m * P:(m + 1) * P], H_hi[:, k, :],
                              start=(k == 0), stop=False)
                    ins = pe.matmul(PS[:, 4 + m % 4, :], AT[:, k, m * P:(m + 1) * P], H_lo[:, k, :],
                                    start=False, stop=(k == T - 1))
                ins.then_inc(S("gnn_ready0"), 1)

            pe.wait_ge(*count("win_in", 16))
            for i in range(2 * K):
                if i < 4:
                    pe.wait_ge(*count("gnn_done0", T))
                else:
                    pe.wait_ge(*count("xm_done", i - 3))
                for k in range(K):
                    ins = pe.matmul(PS[:, 4 + i % 4, :], W[:, 1, k, (i // 2) * P:(i // 2 + 1) * P],
                                    XT[:, k, (i % 2) * 512:(i % 2 + 1) * 512], start=(k == 0), stop=(k == K - 1))
                ins.then_inc(S("xm_ready"), 1)
            pe.wait_ge(*count("xm_done", 2 * K))
            pe.wait_ge(*count("bd_in", 16 * 6))
            for i in range(4):
                g, half = i // 2, i % 2
                for s in range(2):
                    ins = pe.matmul(PS[s * 64:(s + 1) * 64, i % 4, :], BDK[:, :],
                                    XM[:, 2 * g + s, half * 512:(half + 1) * 512], start=True, stop=True,
                                    skip_group_check=True)
                ins.then_inc(S("k_ready0"), 1)
            for m in range(T):
                if m >= 4:
                    pe.wait_ge(*count("v_done0", m - 3))
                for c in range(K):
                    ins = pe.matmul(PS[:, 4 + m % 4, c * P:(c + 1) * P], XM[:, c, m * P:(m + 1) * P], BDV[:, :],
                                    start=True, stop=True, skip_group_check=True)
                ins.then_inc(S("v_ready0"), 1)
            for m in range(T):
                if m == 0:
                    pe.wait_ge(*count("k_done0", 4))
                if m >= 4:
                    pe.wait_ge(*count("q_done0", m - 3))
                for c in range(K):
                    ins = pe.matmul(PS[:, m % 4, c * 64:(c + 1) * 64], XM[:, c, m * P:(m + 1) * P], BDQ[:, :],
                                    start=True, stop=True, skip_group_check=True)
                ins.then_inc(S("q_ready0"), 1)

            def attend(L):
                groups = 2 if L == 0 else K
                w = groups * P
                per = 512 // w
                pe.wait_ge(*count(f"k_exp{L}", groups))
                pe.wait_ge(*count(f"q_done{L}", T))
                for i in range(T // per):
                    if i >= 4:
                        pe.wait_ge(*count(f"kr_done{L}", i - 3))
                    for j in range(per):
                        for g in range(groups):
                            ins = tr(i % 4, j * w + g * P, KTr[:, g, (i * per + j) * P:(i * per + j + 1) * P])
                    ins.then_inc(S(f"kr_ready{L}"), 1)
                pe.wait_ge(*count(f"kr_done{L}", T // per))
                pe.wait_ge(*count(f"v_done{L}", T))
                for i in range(2 * groups):
                    g, half = i // 2, i % 2
                    pe.wait_ge(*count(f"q_soft{L}", 4 * (half + 1)))
                    if i >= 4:
                        pe.wait_ge(*count(f"qT_done{L}", i - 3))
                    for j in range(4):
                        ins = tr(4 + i % 4, j * P, Q[:, 4 * half + j, g * P:(g + 1) * P])
                    ins.then_inc(S(f"qT_ready{L}"), 1)
                vw = D // groups
                for g in range(groups):
                    for m in range(T):
                        ins = pe.matmul(PS[:, g, 0:vw], KR[:, m, g * P:(g + 1) * P],
                                        V[:, m, g * vw:(g + 1) * vw], start=(m == 0), stop=(m == T - 1))
                    ins.then_inc(S(f"kv_ready{L}"), 1)
                pe.wait_ge(*count(f"kv_done{L}", groups))
                pe.wait_ge(*count(f"qT_done{L}", 2 * groups))
                for i in range(2 * K):
                    c, half = i // 2, i % 2
                    if i >= 4:
                        pe.wait_ge(*count(f"oT_done{L}", i - 3))
                    g, at = (c // 2, (c % 2) * P) if L == 0 else (c, 0)
                    pe.matmul(PS[:, 4 + i % 4, :], KV[:, g * vw + at:g * vw + at + P], QT[:, g, half * 512:(half + 1) * 512],
                              start=True, stop=True).then_inc(S(f"oT_ready{L}"), 1)
                pe.wait_ge(*count(f"oT_done{L}", 2 * K))

            attend(0)
            pe.wait_ge(*count("wout_in", 16))
            token_rows("mix_ready0", 0, [(OT[:, c], W[:, 2, c, :]) for c in range(K)], "mix_done0")

            pe.wait_ge(*count("mix_done0", T))
            transposes(1)
            pe.wait_ge(*count("xT_done1", 2 * K))
            pe.wait_ge(*count("gate_in", 48))
            for m in range(T):
                for k in range(K):
                    ins = pe.matmul(PS[:, 0, m * E0:(m + 1) * E0], XT[:, k, m * P:(m + 1) * P], GW[:, k, 0:E0],
                                    start=(k == 0), stop=(k == K - 1), skip_group_check=True)
            ins.then_inc(S("logit_ready0"), 1)
            pe.wait_ge(*count("shared_in", 32))
            sw1 = W[:, 0, 0:2, :].rearrange("p a b -> p (a b)").rearrange("p (k n) -> p k n", k=K)
            for i in range(2 * HJ):
                j, half = i // 2, i % 2
                for k in range(K):
                    ins = pe.matmul(PS[:, 4 + i % 4, :], sw1[:, k, j * P:(j + 1) * P],
                                    XT[:, k, half * 512:(half + 1) * 512], start=(k == 0), stop=(k == K - 1))
                ins.then_inc(S("sh_ready"), 1)
            pe.wait_ge(*count("probs_ready0", 1))
            for m in range(T):
                ins = tr(m // 4, (m % 4) * P, PR[:, m, 0:E0], E0)
            ins.then_inc(S("pT_ready"), 1)
            pe.wait_ge(*count("sh_done", 2 * HJ))
            for m in range(T):
                if m >= 4:
                    pe.wait_ge(*count("shared_done", m - 3))
                for j in range(HJ):
                    ins = pe.matmul(PS[:, 4 + m % 4, :], SHT[:, j, m * P:(m + 1) * P], W[:, 0, 2 + j, :],
                                    start=(j == 0), stop=(j == HJ - 1))
                ins.then_inc(S("shared_ready"), 1)
            pe.wait_ge(*count("top_ready", 2))
            tr(0, 0, ixf0[:, :], CAP)
            tr(0, E0, sc0[:, :], CAP).then_inc(S("scT_ready"), 1)
            pe.wait_ge(*count("shared_done", T))
            for m in range(T):
                if m >= 4:
                    pe.wait_ge(*count("rb_done0", m - 3))
                pe.matmul(PS[:, 4 + m % 4, :], PTW[:, m * P:(m + 1) * P], B2R0[:, :], start=True, stop=True
                          ).then_inc(S("rb_ready0"), 1)
            pe.wait_ge(*count("rb_done0", T))
            pe.wait_ge(*count("scT_done", 1))

            def expert_T(L, e, u, i):
                n, g = (CAP, G0) if L == 0 else (C, G1)
                if L == 0:
                    pe.wait_ge(*count(f"g0_in{u}", (i + 1) * 16))
                else:
                    pe.wait_ge(*count(f"ew1_in{u}", (i + 1) * 48))
                pe.sem_inc(S("pe_passed"))
                for k in range(K):
                    ins = tr(u % 2, k * n, g[u][:, k * P:(k + 1) * P])
                ins.then_inc(S(f"eT_ready{L}"), 1)

            def expert_h(L, e, u, i):
                n, gt = (CAP, GT0) if L == 0 else (C, GT1)
                b = u % 2
                pe.wait_ge(*count(f"eT_done{L}", e + 1))
                if L == 0:
                    pe.wait_ge(*count(f"ew0_in{u}", (i + 1) * 32))
                for j in range(HJ):
                    for k in range(K):
                        ins = pe.matmul(PS[:, 2 + b, j * n:(j + 1) * n], EW1[u][:, k, j * P:(j + 1) * P], gt[b][:, k, :],
                                        start=(k == 0), stop=(k == K - 1), skip_group_check=True)
                ins.then_inc(S(f"eh_ready{L}"), 1)

            def expert(L, i, u, first=False, last=False):
                e = U * i + u
                n, ht = (CAP, HT0) if L == 0 else (C, HT1)
                b = u % 2
                if not (last and u == U - 1):
                    expert_h(L, e + 1, (u + 1) % U, i + (u + 1) // U)
                if not (last and u >= U - 2):
                    expert_T(L, e + 2, (u + 2) % U, i + (u + 2) // U)
                pe.wait_ge(*count(f"eh_done{L}", e + 1))
                if not (first and u < 2):
                    pe.wait_ge(*count(f"ey_done{L}", e - 1))
                for j in range(HJ):
                    ins = pe.matmul(PS[0:n, 4 + b, :], ht[b][:, j, :], EW2[u][:, j, :],
                                    start=(j == 0), stop=(j == HJ - 1))
                ins.then_inc(S(f"ey_ready{L}"), 1)

            def experts_begin(L):
                expert_T(L, 0, 0, 0)
                expert_h(L, 0, 0, 0)
                expert_T(L, 1, 1, 0)

            experts_begin(0)
            for u in range(U):
                expert(0, 0, u, first=True)
            with pe.Fori(1, E0 // U - 1) as i:
                for u in range(U):
                    expert(0, i, u)
            for u in range(U):
                expert(0, E0 // U - 1, u, last=True)

            transposes(2)
            pe.wait_ge(*count("ey_done0", E0))
            pe.wait_ge(*count("xT_done2", 2 * K))
            pe.wait_ge(*count("wn_in", 16))
            token_rows("h_ready1", 4, [(XT[:, k], W[:, 3, k, :]) for k in range(K)], "h_done1")
            pe.wait_ge(*count("wk_in", 16))
            for i in range(2 * K):
                c, half = i // 2, i % 2
                if i >= 4:
                    pe.wait_ge(*count("k_done1", i - 3))
                for k in range(K):
                    ins = pe.matmul(PS[:, i % 4, :], W[:, 0, k, c * P:(c + 1) * P],
                                    XT[:, k, half * 512:(half + 1) * 512], start=(k == 0), stop=(k == K - 1))
                ins.then_inc(S("k_ready1"), 1)
            pe.wait_ge(*count("h_done1", T))
            pe.wait_ge(*count("wv_in", 16))
            token_rows("v_ready1", 4, [(XT[:, k], W[:, 2, k, :]) for k in range(K)], "v_done1")
            pe.wait_ge(*count("k_done1", 2 * K))
            pe.wait_ge(*count("wq_in", 16))
            token_rows("q_ready1", 0, [(XT[:, k], W[:, 1, k, :]) for k in range(K)], "q_done1")
            pe.wait_ge(*count("v_done1", T))
            token_rows("gnn_ready1", 4, [(CT[:, k], H[:, k, :]) for k in range(T)], "gnn_done1")
            pe.wait_ge(*count("gnn_done1", T))
            attend(1)
            pe.wait_ge(*count("wc_in", 16))
            pe.wait_ge(*count("proj_in", 16))
            token_rows("mix_ready1", 0, [(XT[:, k], W[:, 3, k, :]) for k in range(K)]
                       + [(OT[:, c], W[:, 1, c, :]) for c in range(K)], "mix_done1")

            pe.wait_ge(*count("mix_done1", T))
            transposes(3)
            pe.wait_ge(*count("xT_done3", 2 * K))
            for m in range(T):
                for k in range(K):
                    ins = pe.matmul(PS[:, 0, m * E1:(m + 1) * E1], XT[:, k, m * P:(m + 1) * P], GW[:, k, E0:],
                                    start=(k == 0), stop=(k == K - 1), skip_group_check=True)
            ins.then_inc(S("logit_ready1"), 1)
            pe.wait_ge(*count("mb_ready", 1))
            for m in range(T):
                for q in range(m + 1):
                    pe.matmul(PS[:, 1, m * E1:(m + 1) * E1], tri_b[:, :] if q == m else ones_b[:, :], MB[:, q, :],
                              start=(q == 0), stop=(q == m), skip_group_check=True)
            for q in range(T):
                ins = pe.matmul(PS[:, 2, 0:E1], ones_b[:, :], MB[:, q, :], start=(q == 0), stop=(q == T - 1))
            ins.then_inc(S("place_ready"), 1)
            pe.wait_ge(*count("ecol_ready", 1))
            tr(3, 0, ecol[:, :], 1).then_inc(S("erow_ready"), 1)
            pe.wait_ge(*count("sww_ready", 1))
            for m in range(T):
                ins = tr(4 + m // 4, (m % 4) * P, SWW[:, m, :], E1)
            ins.then_inc(S("swT_ready"), 1)
            pe.wait_ge(*count("swT_done", 2))
            pe.wait_ge(*count("late_in", 48))
            for m in range(T):
                if m >= 2:
                    pe.wait_ge(*count("rb_done1", m - 1))
                pe.matmul(PS[:, 6 + m % 2, :], SWT[:, m * P:(m + 1) * P], B2R1[:, :], start=True, stop=True
                          ).then_inc(S("rb_ready1"), 1)
            pe.wait_ge(*count("table_ready", 2))
            turns = pe.value_load(trow_i[0:1, P:P + 1], min_val=3, max_val=MAXT // U)
            experts_begin(1)
            for u in range(U):
                expert(1, 0, u, first=True)
            with pe.Fori(1, turns - 1) as i:
                for u in range(U):
                    expert(1, i, u)
            for u in range(U):
                expert(1, turns - 1, u, last=True)

        @block.vector
        def _(dve):
            own = [0]

            def step(ins):
                ins.then_inc(S("dve_step"), 1)
                own[0] += 1

            def settle():
                dve.wait_ge(*count("dve_step", own[0]))

            def stats(src):
                for t in range(T):
                    step(dve.bn_stats(st[:, t, :], src[:, t, :]))
                settle()
                for t in range(T):
                    step(dve.bn_aggr(mv[:, t, :], st[:, t, :]))
                settle()

            def norm(n, src, dst, name):
                stats(src)
                dve.engine_nop().then_inc(S(f"var_ready{n}"), 1)
                dve.wait_ge(*count(f"sd_ready{n}", 1))
                step(dve.reciprocal(rs[:, :], sd[:, :]))
                settle()
                for t in range(T):
                    dve.tensor_scalar(dst[:, t, :], src[:, t, :], mv[:, t, 0:1], rs[:, t:t + 1],
                                      ALU.subtract, ALU.mult).then_inc(S(name), 1)

            dve.wait_ge(*count("consts", 7))
            step(dve.tensor_copy(iota_h[:, :], iota_i[:, :]))
            step(dve.tensor_copy(iota_e[:, :], iota_i[:, 0:E1]))
            step(dve.tensor_copy(pcol[:, :], pcol_i[:, :]))
            dve.wait_ge(*count("edges_in", 48))
            for i in range(2):
                dve.tensor_copy(edge_f[:, i, :], edge_i[:, i, :]).then_inc(S("edge_f_ready"), 1)
            step(dve.tensor_reduce(gmm[:, 0:1], dgrp_i[:, :], AX_X, ALU.min))
            step(dve.tensor_reduce(gmm[:, 1:2], dgrp_i[:, :], AX_X, ALU.max))
            settle()
            step(dve.tensor_scalar(gov[:, 0, :], iota_i[0:NG, 0:N:P], gmm[:, 1:2], None, ALU.is_le))
            step(dve.tensor_scalar(gov[:, 1, :], iota_i[0:NG, P - 1:N:P], gmm[:, 0:1], None, ALU.is_ge))
            step(dve.tensor_scalar(gov[:, 3, 0:1], pcol[0:NG, :], -1.0, float(NG), ALU.mult, ALU.add))
            step(dve.tensor_scalar(gov[:, 3, 1:2], pcol[0:NG, :], 1.0, None, ALU.add))
            settle()
            step(dve.tensor_tensor(gov[:, 2, :], gov[:, 0, :], gov[:, 1, :], ALU.mult))
            settle()
            dve.tensor_scalar(gval[:, 0:T], gov[:, 2, :], gov[:, 3, 0:1], None, ALU.mult).then_inc(S("gval_ready"), 1)
            dve.tensor_scalar(gval[:, T:2 * T], gov[:, 2, :], gov[:, 3, 1:2], None, ALU.mult
                              ).then_inc(S("gval_ready"), 1)
            dve.wait_ge(*count("small_ready", 2))
            dve.tensor_copy(edge_c[:, :, :].rearrange("p a b -> p (a b)"), PS[:, 0, 0:2 * P]
                            ).then_inc(S("small_done"), 1)
            dve.tensor_copy(cols_sm[:, 0:160], PS[:, 1, 0:160]).then_inc(S("small_done"), 1)
            dve.wait_ge(*count("small_done", 2))

            for h in range(2):
                dve.wait_ge(*count(f"x_in{h}", 16))
            norm(0, X, XN, "xn_ready0")

            dve.wait_ge(*count("gred_ready", 1))
            step(dve.tensor_scalar(grow[:, 0, :], gred[0:1, 0:T], -1.0, float(NG), ALU.mult, ALU.add))
            settle()
            step(dve.tensor_scalar(grow[:, 1, :], grow[:, 0, :], float(NG - 1), None, ALU.min))
            settle()
            step(dve.tensor_tensor(grow[:, 2, :], gred[0:1, T:2 * T], grow[:, 1, :], ALU.subtract))
            settle()
            step(dve.tensor_scalar(grow[:, 3, :], grow[:, 2, :], 1.0, None, ALU.max))
            step(dve.memset(grow[:, 5, :], 0.0))
            settle()
            step(dve.tensor_tensor_scan(grow[:, 4, :], grow[:, 3, :], grow[:, 5, :], 0.0, ALU.add, ALU.add))
            settle()
            step(dve.tensor_tensor(grow[:, 5, :], grow[:, 4, :], grow[:, 3, :], ALU.subtract))
            step(dve.tensor_copy(grow_i[:, 1, :], grow[:, 4, :]))
            settle()
            step(dve.tensor_tensor(grow[:, 0, :], grow[:, 1, :], grow[:, 5, :], ALU.subtract))
            settle()
            step(dve.tensor_scalar(grow[:, 0, :], grow[:, 0, :], float(SHIFT), None, ALU.add))
            settle()
            dve.tensor_copy(grow_i[:, 0, :], grow[:, 0, :]).then_inc(S("grow_ready"), 1)
            dve.wait_ge(*count("grow_ready", 1))

            def adjacency(m):
                dve.wait_ge(*count("ct_done", 2 * (m + 1)))
                step(dve.tensor_scalar(AT[:, m, :], CT[:, m, :], 1.0, None, ALU.min))
                settle()
                dve.tensor_tensor(AT[:, m, m * P:(m + 1) * P], AT[:, m, m * P:(m + 1) * P].bitcast(F32), ident[:, :],
                                  ALU.max).then_inc(S("at_done"), 1)

            start = 0
            for m in range(T):
                delta = dve.value_load(grow_i[0:1, 0, m:m + 1], min_val=0, max_val=2 * SHIFT)
                end = dve.value_load(grow_i[0:1, 1, m:m + 1], min_val=1, max_val=NG * (m + 1))
                with dve.Fori(start, end) as v:
                    group = nc.s_assert_within(v + delta - SHIFT, 0, NG - 1, skip_runtime_bounds_check_because=
                                               "the table holds only visits to groups that exist")
                    dve.wait_ge(*count("onehot_ready", v * 2))
                    dve.tensor_copy(ends[:, :, :], edge_c[:, :, ds(group * 4, 4)]).then_inc(S("ends_set"), 1)
                    dve.wait_ge(*count("ends_set", v + 1))
                    for j in range(4):
                        if j % 2 == 0:
                            dve.wait_ge(*count("onehot_free", v * 2 + (j // 2 + 1)))
                        dve.tensor_scalar(onehot_d[:, j, :], iota_h[:, m * P:(m + 1) * P], ends[:, 1, j:j + 1],
                                          None, ALU.is_equal)
                        ins = dve.tensor_scalar(onehot_s[:, j, :], iota_h[:, :], ends[:, 0, j:j + 1],
                                                None, ALU.is_equal)
                        if j % 2 == 1:
                            ins.then_inc(S("onehot_ready"), 1)
                start = end
                if m >= 1:
                    adjacency(m - 1)
            adjacency(T - 1)

            dve.wait_ge(*count("deg_ready", T))
            parts = PS[:, 7, 0:2 * T * T].rearrange("p (s k m) -> p s m k", s=2, k=T)
            step(dve.tensor_reduce(deg[:, :].rearrange("p (s m) -> p s m", s=2), parts, AX_X, ALU.add))
            settle()
            dve.tensor_scalar(deg[:, 0:T], deg[:, 0:T], 1e-30, None, ALU.max).then_inc(S("deg_done"), 1)
            step(dve.reciprocal(rcnt[:, :], deg[:, T:2 * T]))
            dve.wait_ge(*count("degroot_ready", 1))
            dve.reciprocal(dinv[:, :], sd[:, :]).then_inc(S("dinv_ready"), 1)
            dve.wait_ge(*count("dinv_ready", 1))
            for m in range(T):
                dve.wait_ge(*count("h_rounded", m + 1))
                dve.scalar_tensor_tensor(H_lo[:, m, :], H[:, m, :], dinv[:, m:m + 1], H_hi[:, m, :].bitcast(F32),
                                         ALU.mult, ALU.subtract).then_inc(S("h_split"), 1)
            for m in range(T):
                dve.wait_ge(*count("gnn_ready0", m + 1))
                dve.scalar_tensor_tensor(X[:, m, :], PS[:, 4 + m % 4, :], dinv[:, m:m + 1], X[:, m, :],
                                         ALU.mult, ALU.add).then_inc(S("gnn_done0"), 1)

            def key_max(L, g):
                step(dve.tensor_reduce(kmax[:, g:g + 1], KTr[:, g, :], AX_X, ALU.max, negate=True))
                settle()
                dve.engine_nop().then_inc(S(f"kmax_ready{L}"), 1)

            def q_rows(L):
                w = SLICE if L == 0 else DH
                for m in range(T):
                    dve.wait_ge(*count(f"q_ready{L}", m + 1))
                    ps = PS[:, m % 4, 0:HEADS * w].rearrange("p (h s) -> p h s", h=HEADS)
                    q = Q[:, m, 0:HEADS * w].rearrange("p (h s) -> p h s", h=HEADS)
                    step(dve.tensor_reduce(qm[:, m, :], ps, AX_X, ALU.max))
                    settle()
                    dve.tensor_tensor(q, ps, qm[:, m, :].unsqueeze(2).to_broadcast([P, HEADS, w]), ALU.subtract
                                      ).then_inc(S(f"q_shifted{L}"), 1)
                    dve.wait_ge(*count(f"q_shifted{L}", m + 1))
                    dve.engine_nop().then_inc(S(f"q_done{L}"), 1)

            def q_soft(L):
                w = SLICE if L == 0 else DH
                for m in range(T):
                    q = Q[:, m, 0:HEADS * w].rearrange("p (h s) -> p h s", h=HEADS)
                    dve.wait_ge(*count(f"q_exp{L}", m + 1))
                    step(dve.tensor_reduce(qs[:, m, :], q, AX_X, ALU.add))
                    settle()
                    step(dve.reciprocal(qr[:, m, :], qs[:, m, :]))
                    settle()
                    dve.tensor_tensor(q, q, qr[:, m, :].unsqueeze(2).to_broadcast([P, HEADS, w]), ALU.mult
                                      ).then_inc(S(f"q_soft{L}"), 1)

            def contexts(L):
                groups, hpg, w = (2, 4, SLICE) if L == 0 else (K, 2, DH)
                dve.wait_ge(*count(f"k_exp{L}", groups))
                step(dve.reciprocal(krec[:, 0:groups], ksum[:, 0:groups]))
                settle()
                for g in range(groups):
                    dve.wait_ge(*count(f"kv_ready{L}", g + 1))
                    for h in range(hpg):
                        r = slice(h * w, (h + 1) * w)
                        ins = dve.tensor_scalar(KV[r, g * (D // groups) + h * DH:g * (D // groups) + (h + 1) * DH], PS[r, g, h * DH:(h + 1) * DH],
                                                krec[r, g:g + 1], None, ALU.mult)
                        if h < hpg - 1:
                            step(ins)
                    settle()
                    ins.then_inc(S(f"kv_done{L}"), 1)

            step(dve.memset(KV[:, :], 0.0))
            settle()
            for g in range(2):
                dve.wait_ge(*count("k_done0", 2 * g + 2))
                key_max(0, g)
            q_rows(0)
            q_soft(0)
            contexts(0)
            for m in range(T):
                dve.wait_ge(*count("mix_ready0", m + 1))
                step(dve.tensor_tensor(X[:, m, :], X[:, m, :], PS[:, m % 4, :], ALU.add))
                settle()
                dve.tensor_tensor(X[:, m, :], X[:, m, :], BC[:, 1, :], ALU.add).then_inc(S("mix_done0"), 1)
            dve.wait_ge(*count("mix_done0", T))
            norm(1, X, XN, "xn_ready1")

            def router_softmax(n):
                w = (E0, E1)[n]
                pr = PR[:, :, 0:w]
                dve.wait_ge(*count(f"logit_ready{n}", 1))
                ps = PS[:, 0, 0:T * w].rearrange("p (t e) -> p t e", t=T)
                if n == 1:
                    step(dve.tensor_tensor(pr, ps, BG[:, :].unsqueeze(1).to_broadcast([P, T, w]), ALU.add))
                    settle()
                    ps = pr
                step(dve.tensor_reduce(pm[:, :], ps, AX_X, ALU.max))
                settle()
                dve.tensor_tensor(pr, ps, pm[:, :].unsqueeze(2).to_broadcast([P, T, w]), ALU.subtract
                                  ).then_inc(S(f"logit_shifted{n}"), 1)
                dve.wait_ge(*count(f"logit_exp{n}", 1))
                step(dve.tensor_reduce(psm[:, :], pr, AX_X, ALU.add))
                settle()
                step(dve.reciprocal(pr_[:, :], psm[:, :]))
                settle()
                dve.tensor_tensor(pr, pr, pr_[:, :].unsqueeze(2).to_broadcast([P, T, w]), ALU.mult
                                  ).then_inc(S(f"probs_ready{n}"), 1)

            router_softmax(0)
            dve.wait_ge(*count("pT_ready", 1))
            both = PS[0:E0, 0:2, :].rearrange("p a b -> p (a b)")
            step(dve.tensor_copy(PT, both))
            step(dve.tensor_copy(PTW, both))
            settle()
            for r in range(CAP // 8):
                s8 = sc0[:, r * 8:(r + 1) * 8]
                step(dve.max(s8, PTW))
                settle()
                step(dve.max_index(ix0[:, r * 8:(r + 1) * 8], s8, PTW))
                settle()
                step(dve.match_replace(PTW, s8, PTW, -1.0))
                settle()
                m = r
                dve.wait_ge(*count("shared_ready", m + 1))
                dve.tensor_tensor(X[:, m, :], X[:, m, :], PS[:, 4 + m % 4, :], ALU.add).then_inc(S("shared_done"), 1)
            step(dve.tensor_scalar(PTW, PTW, 0.0, None, ALU.is_lt))
            dve.tensor_copy(ixf0[:, :], ix0[:, :]).then_inc(S("top_ready"), 1)
            settle()
            dve.tensor_tensor(PTW, PTW, PT, ALU.mult).then_inc(S("top_ready"), 1)
            dve.wait_ge(*count("scT_ready", 1))
            step(dve.tensor_copy(scT[:, :], PS[0:CAP, 0, 0:2 * E0]))
            settle()
            dve.tensor_copy(ic0[:, :], scT[:, 0:E0]).then_inc(S("ic0_ready"), 1)
            dve.engine_nop().then_inc(S("scT_done"), 1)
            dve.wait_ge(*count("shared_done", T))
            for m in range(T):
                dve.wait_ge(*count("rb_ready0", m + 1))
                dve.tensor_tensor(X[:, m, :], X[:, m, :], PS[:, 4 + m % 4, :], ALU.add).then_inc(S("rb_done0"), 1)
            dve.wait_ge(*count("rb_done0", T))
            for m in range(T):
                dve.tensor_tensor(X[:, m, :], X[:, m, :], BC[:, 2, :], ALU.add).then_inc(S("resid0_ready"), 1)

            def expert_out(L, i, u, first):
                e = U * i + u
                dve.wait_ge(*count(f"ey_ready{L}", e + 1))
                if L == 0:
                    if not (first and u < 2):
                        dve.wait_ge(*count("scattered0", 16 * (e - 1)))
                    dve.tensor_scalar(Y0[u % 2], PS[0:CAP, 4 + u % 2, :], scT[:, ds(e + E0, 1)], None, ALU.mult
                                      ).then_inc(S("ey_done0"), 1)
                else:
                    if not first:
                        dve.wait_ge(*count(f"y1_out{u}", 16 * i))
                    dve.tensor_copy(Y1[u], PS[0:C, 4 + u % 2, :]).then_inc(S("ey_done1"), 1)

            for u in range(U):
                expert_out(0, 0, u, True)
            with dve.Fori(1, E0 // U) as i:
                for u in range(U):
                    expert_out(0, i, u, False)

            dve.wait_ge(*count("acc0_in", 16))
            norm(2, X, XN, "xn_ready2")
            dve.wait_ge(*count("xT_done2", 2 * K))
            for i in range(2 * K):
                dve.wait_ge(*count("k_ready1", i + 1))
                k = KTr[:, i // 2, (i % 2) * 512:(i % 2 + 1) * 512]
                dve.tensor_scalar(k, PS[:, i % 4, :], 0.0, None, ALU.min).then_inc(S("k_low"), 1)
                dve.wait_ge(*count("k_elu", i + 1))
                dve.scalar_tensor_tensor(k, PS[:, i % 4, :], 0.0, k, ALU.max, ALU.add).then_inc(S("k_done1"), 1)
            dve.wait_ge(*count("k_done1", 2 * K))
            for g in range(K):
                key_max(1, g)
            q_rows(1)
            for m in range(T):
                dve.wait_ge(*count("gnn_ready1", m + 1))
                dve.scalar_tensor_tensor(X[:, m, :], PS[:, 4 + m % 4, :], rcnt[:, m:m + 1], X[:, m, :],
                                         ALU.mult, ALU.add).then_inc(S("gnn_done1"), 1)
            q_soft(1)
            step(dve.memset(KV[:, :], 0.0))
            step(dve.tensor_tensor(BC[:, 3, :], BC[:, 3, :], BC[:, 4, :], ALU.add))
            settle()
            contexts(1)
            for m in range(T):
                dve.wait_ge(*count("mix_ready1", m + 1))
                step(dve.tensor_tensor(X[:, m, :], X[:, m, :], PS[:, m % 4, :], ALU.add))
                settle()
                dve.tensor_tensor(X[:, m, :], X[:, m, :], BC[:, 3, :], ALU.add).then_inc(S("mix_done1"), 1)
            dve.wait_ge(*count("mix_done1", T))
            norm(3, X, XN, "xn_ready3")
            router_softmax(1)
            dve.wait_ge(*count("probs_ready1", 1))
            for t in range(T):
                step(dve.max(top8[:, t, :], PR[:, t, :]))
            settle()
            for t in range(T):
                step(dve.max_index(ti8[:, t, :], top8[:, t, :], PR[:, t, :]))
            settle()
            step(dve.tensor_copy(tif[:, :, :], ti8[:, :, 0:2]))
            settle()
            for t in range(T):
                step(dve.tensor_scalar(O1[:, t, :], iota_e[:, :], tif[:, t, 0:1], None, ALU.is_equal))
                step(dve.tensor_scalar(O2[:, t, :], iota_e[:, :], tif[:, t, 1:2], None, ALU.is_equal))
            settle()
            dve.tensor_tensor(MB, O1, O2, ALU.add).then_inc(S("mb_ready"), 1)
            for t in range(T):
                step(dve.tensor_scalar(SWW[:, t, :], O1[:, t, :], top8[:, t, 0:1], None, ALU.mult))
            settle()
            for t in range(T):
                ins = dve.scalar_tensor_tensor(SWW[:, t, :], O2[:, t, :], top8[:, t, 1:2], SWW[:, t, :],
                                               ALU.mult, ALU.add)
                if t < T - 1:
                    step(ins)
            settle()
            ins.then_inc(S("sww_ready"), 1)
            dve.wait_ge(*count("place_ready", 1))
            step(dve.tensor_scalar(cntb[:, 0, :], PS[:, 2, 0:E1], float(C - 1), None, ALU.add))
            settle()
            step(dve.tensor_copy(cnti[:, :], cntb[:, 0, :]))
            settle()
            step(dve.tensor_scalar(cnti[:, :], cnti[:, :], C.bit_length() - 1, None, ALU.logical_shift_right))
            step(dve.memset(cntb[:, 5, :], 0.0))
            settle()
            step(dve.tensor_copy(cntb[:, 1, :], cnti[:, :]))
            settle()
            step(dve.tensor_tensor_scan(cntb[:, 2, :], cntb[:, 1, :], cntb[:, 5, :], 0.0, ALU.add, ALU.add))
            settle()
            step(dve.tensor_tensor(cntb[:, 3, :], cntb[:, 2, :], cntb[:, 1, :], ALU.subtract))
            step(dve.tensor_scalar(cntb[:, 0, :], cntb[:, 2, :], pcol[:, 0:1], None, ALU.is_le))
            settle()
            step(dve.tensor_scalar(cntb[:, 4, :], cntb[:, 3, :], float(C), None, ALU.mult))
            dve.tensor_reduce(ecol[:, :], cntb[:, 0, :], AX_X, ALU.add).then_inc(S("ecol_ready"), 1)
            step(dve.tensor_scalar(trow[:, P:P + 1], cntb[0:1, 2, E1 - 1:E1], float(U - 1), None, ALU.add))
            settle()
            step(dve.tensor_copy(trow_i[:, P + 1:P + 2], trow[:, P:P + 1]))
            settle()
            dve.tensor_scalar(trow_i[:, P:P + 1], trow_i[:, P + 1:P + 2], U.bit_length() - 1, None,
                              ALU.logical_shift_right).then_inc(S("table_ready"), 1)
            step(dve.tensor_tensor(SL, PS[:, 1, :].rearrange("p (t e) -> p t e", t=T),
                                   cntb[:, 4, :].unsqueeze(1).to_broadcast([P, T, E1]), ALU.add))
            settle()
            for c, o in enumerate((O1, O2)):
                step(dve.tensor_tensor(SLT, SL, o, ALU.mult))
                settle()
                step(dve.tensor_reduce(slot_f[:, c, :], SLT, AX_X, ALU.add))
                settle()
                dve.tensor_copy(slot_i[:, c, :], slot_f[:, c, :]).then_inc(S("slot_ready"), 1)
            dve.wait_ge(*count("erow_ready", 1))
            step(dve.tensor_scalar(trow[:, 0:P], PS[0:1, 3, 0:P], float(E1 - 1), None, ALU.min))
            settle()
            dve.tensor_copy(trow_i[:, 0:P], trow[:, 0:P]).then_inc(S("table_ready"), 1)
            dve.wait_ge(*count("swT_ready", 1))
            for h in range(2):
                dve.tensor_copy(SWT[:, h * 512:(h + 1) * 512], PS[0:E1, 4 + h, :]).then_inc(S("swT_done"), 1)
            dve.wait_ge(*count("dispatched", 16 * 2 * T))
            for m in range(T):
                dve.wait_ge(*count("rb_ready1", m + 1))
                dve.tensor_tensor(XN[:, m, :], XN[:, m, :], PS[:, 6 + m % 2, :], ALU.add).then_inc(S("rb_done1"), 1)
            dve.wait_ge(*count("rb_done1", T))
            dve.wait_ge(*count("late_in", 48))
            for m in range(T):
                step(dve.tensor_tensor(X[:, m, :], X[:, m, :], BC[:, 1, :], ALU.add))
            turns = dve.value_load(trow_i[0:1, P:P + 1], min_val=3, max_val=MAXT // U)
            for u in range(U):
                expert_out(1, 0, u, True)
            with dve.Fori(1, turns) as i:
                for u in range(U):
                    expert_out(1, i, u, False)
            settle()
            for m in range(T):
                for c in range(2):
                    n = 2 * m + c
                    dve.wait_ge(*count(f"yg_in{n % 4}", 16 * (n // 4 + 1)))
                    dve.scalar_tensor_tensor(XN[:, m, :], YG[n % 4], top8[:, m, c:c + 1], XN[:, m, :],
                                             ALU.mult, ALU.add).then_inc(S("combined"), 1)
                    dve.wait_ge(*count("combined", n + 1))
            norm(4, XN, XN, "zn_ready")
            for m in range(T):
                dve.wait_ge(*count("zn_ready", m + 1))
                step(dve.tensor_tensor(XN[:, m, :], XN[:, m, :], BC[:, 0, :], ALU.mult))
                settle()
                dve.tensor_tensor(X[:, m, :], X[:, m, :], XN[:, m, :], ALU.add).then_inc(S("out_ready"), 1)


_INS = ['x', 'src', 'dst', 'L0_gnn_W', 'L0_gnn_b', 'L0_mix_W_in', 'L0_mix_b_in', 'L0_mix_Wq', 'L0_mix_Wk',
        'L0_mix_Wv', 'L0_mix_W_out', 'L0_mix_b_out', 'L0_ffn_gate_w', 'L0_ffn_w1', 'L0_ffn_b1', 'L0_ffn_w2',
        'L0_ffn_b2', 'L0_ffn_sw1', 'L0_ffn_sb1', 'L0_ffn_sw2', 'L0_ffn_sb2', 'L1_gnn_wc', 'L1_gnn_wn',
        'L1_gnn_bias', 'L1_mix_w_qkv', 'L1_mix_w_proj', 'L1_mix_b_proj', 'L1_ffn_Wg', 'L1_ffn_bg', 'L1_ffn_W1',
        'L1_ffn_b1', 'L1_ffn_W2', 'L1_ffn_b2', 'L1_ffn_gamma', 'L1_ffn_beta']


def kernel(**inputs):
    import numpy as _np
    import concourse.bacc as _bacc
    from concourse import mybir as _mybir
    from concourse.bass_utils import run_bass_kernel_spmd as _run

    nc = _bacc.Bacc("TRN2", target_bir_lowering=False, num_devices=1)
    arrays, aps = {}, {}
    for name in _INS:
        a = _np.ascontiguousarray(inputs[name])
        arrays[f"in_{name}_dram"] = a
        aps[name] = nc.dram_tensor(f"in_{name}_dram", a.shape, _mybir.dt.from_np(a.dtype), kind="ExternalInput").ap()
    out = nc.dram_tensor("out_0_dram", (N, D), _mybir.dt.float32, kind="ExternalOutput").ap()
    build(nc, aps, out)
    r = _run(nc, [arrays], core_ids=[0])
    return r.results[0]["out_0_dram"]
```

```python
from contextlib import ExitStack

import concourse.bass as bass
from concourse import mybir

ALU = mybir.AluOpType
ACT = mybir.ActivationFunctionType
AX_X = mybir.AxisListType.X
F32 = mybir.dt.float32
F32R = mybir.dt.float32r
F16 = mybir.dt.float16
BF16 = mybir.dt.bfloat16
I32 = mybir.dt.int32
U32 = mybir.dt.uint32
RMAX = bass.bass_isa.ReduceOp.max
ds = bass.ds

P = 128
N = 1024
D = 512
NE = 16384
T = N // P
K = D // P
HEADS = 8
DH = D // HEADS
SLICE = 32
GRP = 4 * P
NG = NE // GRP
SHIFT = NG * T
HID = 256
HJ = HID // P
E0 = 16
CAP = N // E0
E1 = 64
C = 80
NC = -(-N // C)
U = 4
MAXT = E1 + (2 * N - E1) // C + U
MAXT -= MAXT % U
EPS = 1e-5
EXACT = 2048


def build(nc, A, out):
    with ExitStack() as ctx:
        def sb(name, shape, dt=F32):
            return ctx.enter_context(nc.sbuf_tensor(name, shape, dt))

        def rounded(name, shape):
            return nc.alloc_sbuf_tensor_at(name, shape, F32R, offset=-(-nc.sbuf_base // 32) * 32)

        norms = dict(var_ready=T, sd_ready=T, xn_ready=T, xT_ready=T, xT_done=T, x_biased=T)
        layers = dict(h_ready=T, h_done=T, gnn_ready=T, gnn_done=T, k_ready=4, k_done=4, v_ready=T, v_done=T,
                      q_ready=T, q_done=T, q_shifted=T, q_exp=T, q_soft=T, kmax_ready=2, k_exp=2, kr_ready=4,
                      kr_done=4, qT_ready=4, qT_done=4, kv_ready=2, kv_done=2, oT_ready=2 * K, oT_done=2 * K,
                      mix_ready=T, mix_done=T, logit_ready=1, logit_shifted=1, logit_exp=1, probs_ready=1,
                      rb_ready=T, rb_done=T, eT_ready=E0, eT_done=E0, eh_ready=E0, eh_done=E0, ey_ready=E0,
                      ey_done=E0)
        rings = {}
        for u in range(U):
            rings[f"ew{u}_in"], rings[f"g{u}_in"] = 32 * (E0 // U), 16 * (E0 // U)
        adds = {**norms, **layers, **rings}
        sems = {}

        def S(name):
            name = name[:-1] if name[:-1] in adds else name
            if name not in sems:
                sems[name] = ctx.enter_context(nc.semaphore(name))
            return sems[name]

        def count(name, n):
            return S(name), n + (adds[name[:-1]] * int(name[-1]) if name[:-1] in adds else 0)

        toks = [nc.dram_tensor(f"tok{L}_scratch", (N, D), F32).ap() for L in range(2)]
        accs = [nc.dram_tensor(f"acc{b}_scratch", (N, D), F32).ap() for b in range(2)]
        chosen_d = nc.dram_tensor("chosen_scratch", (2 * N, D), F32).ap()

        X = sb("X", [P, T, D])
        XN = sb("XN", [P, T, D])
        XT = sb("XT", [P, K, N])
        H_lo = rounded("H_lo", [P, T, D])
        H = sb("H", [P, T, D])
        CT = sb("CT", [P, T, N])
        AT = rounded("AT", [P, T, N])
        later = sb("later", [P, T * N])
        H_hi = rounded("H_hi", [P, T, D])
        B1 = sb("B1", [P, 4096])
        W = sb("W", [P, 4, K, D])
        BC = sb("BC", [P, 5, D])
        BG = sb("BG", [P, E1])

        ident = sb("ident", [P, P])
        onescol = sb("onescol", [P, 1])
        ones_b = sb("ones_b", [P, P], BF16)
        tri_b = sb("tri_b", [P, P], BF16)
        zero_f = sb("zero_f", [P, D])
        zero_b = zero_f[:, 0:D // 2].bitcast(BF16)
        iota_h = sb("iota_h", [P, N], F16)
        iota_e = sb("iota_e", [P, E1])
        pcol_i = sb("pcol_i", [P, 1], I32)
        pcol = sb("pcol", [P, 1])
        epsc = sb("epsc", [P, 1])

        edge_c = sb("edge_c", [P, 2, P])
        ends = sb("ends", [P, 4])
        gmm = sb("gmm", [NG, 2])
        gov = sb("gov", [NG, 5, T])
        gval = sb("gval", [NG, 2 * T])
        gred = sb("gred", [NG, 2 * T])
        grow = sb("grow", [1, 6, T])
        grow_i = sb("grow_i", [1, 2, T], I32)

        cols_sm = sb("cols_sm", [P, 256])
        BDQ = sb("BDQ", [P, 2 * SLICE])
        BDK = sb("BDK", [P, 2 * SLICE])
        BDV = sb("BDV", [P, 2 * DH])
        GW = sb("GW", [P, K, E0 + E1])
        B2R0 = sb("B2R0", [E0, D])

        st = sb("st", [P, T, 6])
        mv = sb("mv", [P, T, 2])
        sd = sb("sd", [P, T])
        rs = sb("rs", [P, T])
        deg = sb("deg", [P, 2 * T])
        dinv = sb("dinv", [P, T])
        most = sb("most", [P, 2])
        most_i = sb("most_i", [1, 1], I32)
        rcnt = sb("rcnt", [P, T])
        kmax = sb("kmax", [P, K])
        ksum = sb("ksum", [P, K])
        krec = sb("krec", [P, K])
        qm = sb("qm", [P, T, HEADS])
        qs = sb("qs", [P, T, HEADS])
        qr = sb("qr", [P, T, HEADS])
        KV = sb("KV", [P, D])

        PR = sb("PR", [P, T, E1])
        pm = sb("pm", [P, T])
        psm = sb("psm", [P, T])
        pr_ = sb("pr_", [P, T])
        sc0 = sb("sc0", [E0, CAP])
        ix0 = sb("ix0", [E0, CAP], U32)
        ixf0 = sb("ixf0", [E0, CAP])
        scT = sb("scT", [CAP, 2 * E0])
        ic0 = sb("ic0", [CAP, E0], I32)
        icur = sb("icur", [P, U], I32)
        iout = sb("iout", [P, U], I32)
        top8 = sb("top8", [P, T, 8])
        ti8 = sb("ti8", [P, T, 8], U32)
        tif = sb("tif", [P, T, 2])
        at = sb("at", [P, 6, 2 * T])
        ids_i = sb("ids_i", [P, 2 * T], I32)
        ids = sb("ids", [P, 2 * T])
        rows_i = sb("rows_i", [C, 2, MAXT], I32)
        limits = sb("limits", [P, NC])
        ecol = sb("ecol", [P, 1])
        trow_i = sb("trow_i", [1, P + 3], I32)

        PS = ctx.enter_context(nc.psum_tensor("PS", [P, 8, 512], F32))

        early = H[:, :, :].rearrange("p a b -> p (a b)")
        iota_i = early[:, 0:N].bitcast(I32)
        edge_i = early[:, N:N + 2 * P].bitcast(I32).rearrange("p (a b) -> p a b", a=2)
        edge_f = early[:, N + 2 * P:N + 4 * P].rearrange("p (a b) -> p a b", a=2)
        dgrp_i = early[0:NG, 2048:2048 + GRP].bitcast(I32)
        rows_sm = early[0:E1, 3072:3584].rearrange("p (a b) -> p a b", a=2)
        ATf = later[:, :]
        CTf = CT[:, :, :].rearrange("p a b -> p (a b)")
        Hf = H[:, :, :].rearrange("p a b -> p (a b)")
        onehot_s = B1[:, 0:2048].bitcast(BF16).rearrange("p (j n) -> p j n", j=4)
        onehot_d = B1[:, 2048:2304].bitcast(BF16).rearrange("p (j n) -> p j n", j=4)
        away = B1[:, 2304:2560].bitcast(BF16).rearrange("p (j n) -> p j n", j=4)
        minus_dst = B1[:, 2560:2564]
        XM = ATf[:, 0:4096].rearrange("p (c n) -> p c n", c=K)
        V = ATf[:, 4096:8192].rearrange("p (t n) -> p t n", t=T)
        Q = B1[:, :].rearrange("p (t n) -> p t n", t=T)
        OT = B1[:, :].rearrange("p (c n) -> p c n", c=K)
        KTr = XN[:, :, :].rearrange("p a b -> p (a b)").rearrange("p (c n) -> p c n", c=K)
        QT = KTr
        KR = H
        SHT = B1[:, 0:2048].rearrange("p (j n) -> p j n", j=HJ)
        PT = B1[0:E0, 2048:3072]
        PTW = B1[0:E0, 3072:4096]
        O1 = CTf[:, 0:512].rearrange("p (t e) -> p t e", t=T)
        O2 = CTf[:, 512:1024].rearrange("p (t e) -> p t e", t=T)
        MB = CTf[:, 1024:1280].bitcast(BF16).rearrange("p (t e) -> p t e", t=T)
        SWW = CTf[:, 1280:1792].rearrange("p (t e) -> p t e", t=T)
        SL = CTf[:, 1792:2304].rearrange("p (t e) -> p t e", t=T)
        SLT = CTf[:, 2304:2816].rearrange("p (t e) -> p t e", t=T)
        SWT = CTf[0:E1, 2816:3840]
        more = Hf[:, 0:E1 * NC].rearrange("p (e c) -> p e c", e=E1)
        cntb = CTf[:, 6144:6144 + 6 * E1].rearrange("p (a e) -> p a e", e=E1)
        B2R1 = CTf[0:E1, 6656:6656 + D]
        trow = CTf[0:1, 7168:7168 + P + 1]
        EW = [ATf[:, u * 2048:(u + 1) * 2048] for u in range(U)]
        EW1 = [w[:, 0:1024].rearrange("p (k n) -> p k n", k=K) for w in EW]
        EW2 = [w[:, 1024:2048].rearrange("p (j n) -> p j n", j=HJ) for w in EW]

        def expert_space(f, n):
            g = [f[0:n, u * D:(u + 1) * D] for u in range(U)]
            at = U * D
            gt = [f[:, at + b * K * n:at + (b + 1) * K * n].rearrange("p (k n) -> p k n", k=K) for b in range(2)]
            at += 2 * K * n
            ht = [f[:, at + b * HJ * n:at + (b + 1) * HJ * n].rearrange("p (j n) -> p j n", j=HJ) for b in range(2)]
            return g, gt, ht

        G0, GT0, HT0 = expert_space(Hf, CAP)
        Y0 = [Hf[0:CAP, 2816 + b * D:2816 + (b + 1) * D] for b in range(2)]
        G1, GT1, HT1 = expert_space(Hf, C)
        Y1 = [B1[0:C, u * D:(u + 1) * D] for u in range(U)]
        YG = [CTf[:, m * 2 * D:(m + 1) * 2 * D].rearrange("p (c n) -> p c n", c=2) for m in range(T)]
        rows = CTf[0:C, 7424:7424 + 3 * MAXT].rearrange("p (a e) -> p a e", e=MAXT)
        place_ge = Hf[:, 1024:1024 + 2 * T * NC].rearrange("p (a c) -> p a c", a=2 * T)
        RB = XT[:, :, :].rearrange("p a b -> p (a b)").rearrange("p (t n) -> p t n", t=T)
        lane_hot = Hf[:, 2048:4096].rearrange("p (a n) -> p a n", a=2 * T)[:, :, 0:C]
        tile_hot = CTf[:, 4096:4096 + 2 * T * MAXT].rearrange("p (a n) -> p a n", a=2 * T)

        def norm_banks(n):
            return (4, 5, 6) if n % 2 else (0, 1, 2, 3)

        wv = lambda ap: ap.rearrange("(k p) n -> p k n", p=P)
        block = ctx.enter_context(nc.Block())

        @block.sync
        def _(sp):
            def rows2(dram, q):
                return dram.rearrange("(t p) d -> p t d", p=P)[:, 2 * q:2 * q + 2, :]

            for q in range(T // 2):
                sp.dma_start(X[:, 2 * q:2 * q + 2, :], rows2(A["x"], q)).then_inc(S(f"x_in{q}"), 16)
            for i, n in enumerate(("src", "dst")):
                sp.dma_start(edge_i[:, i, :], A[n].rearrange("(c e) -> c e", e=P)).then_inc(S("edges_in"), 16)
            sp.dma_start(dgrp_i[:, :], A["dst"].rearrange("(g e) -> g e", e=GRP)).then_inc(S("edges_in"), 16)
            sp.dma_start(W[:, 0], wv(A["L0_gnn_W"])).then_inc(S("gnnw_in"), 16)
            for b, n, e in ((0, "L0_ffn_b1", E0), (1, "L1_ffn_b1", E1)):
                sp.dma_start(rows_sm[0:e, b, :], A[n]).then_inc(S("small_in"), 16)
            sp.dma_start(W[:, 1], wv(A["L0_mix_W_in"])).then_inc(S("win_in"), 16)
            for n, at in (("L0_gnn_b", 0), ("L0_mix_b_out", 1), ("L0_ffn_sb2", 2), ("L1_gnn_bias", 3),
                          ("L1_mix_b_proj", 4)):
                sp.dma_start(BC[:, at, :], A[n].partition_broadcast(P)).then_inc(S("bias_in"), 16)
            sp.dma_start(BG[:, :], A["L1_ffn_bg"].partition_broadcast(P)).then_inc(S("bias_in"), 16)
            sp.dma_start(cols_sm[:, 192:196], A["L0_mix_b_in"].rearrange("(c p) -> p c", p=P),
                         allow_slow_non_contiguous=True).then_inc(S("bias_in"), 16)
            sp.dma_start(cols_sm[:, 196:198], A["L0_ffn_sb1"].rearrange("(c p) -> p c", p=P),
                         allow_slow_non_contiguous=True).then_inc(S("bias_in"), 16)
            sp.wait_ge(*count("bd_zero", 3))
            for h in range(2):
                r = slice(h * DH, (h + 1) * DH)
                sp.dma_start(BDQ[r, h * SLICE:(h + 1) * SLICE], A["L0_mix_Wq"]).then_inc(S("bd_in"), 16)
                sp.dma_start(BDK[r, h * SLICE:(h + 1) * SLICE], A["L0_mix_Wk"]).then_inc(S("bd_in"), 16)
                sp.dma_start(BDV[r, h * DH:(h + 1) * DH], A["L0_mix_Wv"]).then_inc(S("bd_in"), 16)
            sp.dma_start(W[:, 2], wv(A["L0_mix_W_out"])).then_inc(S("wout_in"), 16)
            sp.dma_start(GW[:, :, 0:E0], wv(A["L0_ffn_gate_w"])).then_inc(S("gate_in"), 16)
            sp.dma_start(GW[:, :, E0:], wv(A["L1_ffn_Wg"])).then_inc(S("gate_in"), 16)
            sp.dma_start(B2R0[:, :], A["L0_ffn_b2"]).then_inc(S("gate_in"), 16)
            sp.wait_ge(*count("zeros_ready", 1))
            sp.dma_start(accs[1].rearrange("(t p) d -> p t d", p=P),
                         zero_f[:, :].unsqueeze(1).to_broadcast([P, T, D])).then_inc(S("acc_out"), 16)
            sp.wait_ge(*count("wT_ready", K))
            sp.dma_start(W[:, 0, 0:2, :].rearrange("p a b -> p (a b)").rearrange("p (k n) -> p k n", k=K),
                         wv(A["L0_ffn_sw1"])).then_inc(S("shared_in"), 16)
            sp.dma_start(W[:, 0, 2:4, :], wv(A["L0_ffn_sw2"])).then_inc(S("shared_in"), 16)
            qkv = A["L1_mix_w_qkv"].rearrange("(k p) n -> p k n", p=P)
            sp.wait_ge(*count("xm_ready", 2 * K))
            sp.dma_start(W[:, 1], qkv[:, :, 0:D]).then_inc(S("wq_in"), 16)
            sp.wait_ge(*count("h_ready0", T))
            sp.dma_start(W[:, 3], wv(A["L1_gnn_wn"])).then_inc(S("wn_in"), 16)
            sp.wait_ge(*count("mix_ready0", T))
            sp.dma_start(W[:, 2], qkv[:, :, 2 * D:3 * D]).then_inc(S("wv_in"), 16)

            sp.wait_ge(*count("xn_ready1", T))
            sp.dma_start(toks[0].rearrange("(t p) d -> p t d", p=P), XN[:, :, :]).then_inc(S("tok_out"), 16)

            def load0(i, u):
                e = U * i + u
                sp.dma_start(EW1[u], A["L0_ffn_w1"][ds(e, 1)].rearrange("a (k p) n -> p (a k) n", p=P)
                             ).then_inc(S(f"ew{u}_in0"), 16)
                sp.dma_start(EW2[u], A["L0_ffn_w2"][ds(e, 1)].rearrange("a (k p) n -> p (a k) n", p=P)
                             ).then_inc(S(f"ew{u}_in0"), 16)

            for u in range(U):
                load0(0, u)
            sp.wait_ge(*count("rb_done0", T))
            sp.dma_start(accs[0].rearrange("(t p) d -> p t d", p=P), X[:, :, :]).then_inc(S("acc_out"), 16)
            with sp.Fori(1, E0 // U) as i:
                for u in range(U):
                    sp.wait_ge(*count("ey_ready0", U * i + (u + 1 - U)))
                    load0(i, u)
            for b in range(2):
                sp.wait_ge(*count(f"scattered{b}", 16 * E0 // 2))
            for q in range(T // 2):
                for b, dst in enumerate((X, XN)):
                    sp.dma_start(dst[:, 2 * q:2 * q + 2, :], rows2(accs[b], q)).then_inc(S(f"x_in{q}"), 16)
            sp.wait_ge(*count("shared_ready", T))
            sp.dma_start(W[:, 0], qkv[:, :, D:2 * D]).then_inc(S("wk_in"), 16)
            sp.wait_ge(*count("h_ready1", T))
            sp.dma_start(W[:, 3], wv(A["L1_gnn_wc"])).then_inc(S("wc_in"), 16)
            sp.wait_ge(*count("q_ready1", T))
            sp.dma_start(W[:, 1], wv(A["L1_mix_w_proj"])).then_inc(S("proj_in"), 16)

            sp.wait_ge(*count("gnn_ready1", T))
            sp.dma_start(B2R1, A["L1_ffn_b2"]).then_inc(S("late_in"), 16)
            sp.dma_start(BC[:, 0, :], A["L1_ffn_gamma"].partition_broadcast(P)).then_inc(S("late_in"), 16)
            sp.dma_start(BC[:, 1, :], A["L1_ffn_beta"].partition_broadcast(P)).then_inc(S("late_in"), 16)

            sp.wait_ge(*count("xn_ready3", T))
            sp.dma_start(toks[1].rearrange("(t p) d -> p t d", p=P), XN[:, :, :]).then_inc(S("tok_out"), 16)
            sp.wait_ge(*count("table_ready", 3))
            turns = sp.value_load(trow_i[0:1, P:P + 1], min_val=3, max_val=MAXT // U)

            def load1(i, u):
                e = sp.value_load(trow_i[0:1, ds(U * i + u, 1)], min_val=0, max_val=E1 - 1)
                sp.dma_start(EW1[u], A["L1_ffn_W1"][ds(e, 1)].rearrange("a (k p) n -> p (a k) n", p=P)
                             ).then_inc(S(f"ew{u}_in1"), 16)
                sp.dma_start(EW2[u], A["L1_ffn_W2"][ds(e, 1)].rearrange("a (k p) n -> p (a k) n", p=P)
                             ).then_inc(S(f"ew{u}_in1"), 16)

            sp.wait_ge(*count("mix_ready1", T))
            for u in range(U):
                load1(0, u)
            with sp.Fori(1, turns) as i:
                for u in range(U):
                    sp.wait_ge(*count("ey_ready1", U * i + (u + 1 - U)))
                    load1(i, u)
            for u in range(U):
                sp.wait_ge(*count(f"y1_out{u}", 16 * turns))
            for m in range(T):
                sp.dma_start(YG[m], chosen_d.rearrange("(c t p) d -> p t c d", c=2, p=P)[:, m]
                             ).then_inc(S(f"yg_in{m}"), 16)
            for q in range(T // 2):
                sp.wait_ge(*count("out_ready", 2 * (q + 1)))
                sp.dma_start(rows2(out, q), X[:, 2 * q:2 * q + 2, :]).then_inc(S("stored"), 16)
            sp.wait_ge(*count("stored", 16 * T // 2))

        @block.gpsimd
        def _(pool):
            pool.memset(ident[:, :], 0.0).then_inc(S("cst"), 1)
            pool.memset(zero_f[:, :], 0.0).then_inc(S("zeros_ready"), 1)
            pool.memset(BDQ[:, :], 0.0).then_inc(S("bd_zero"), 1)
            pool.memset(BDK[:, :], 0.0).then_inc(S("bd_zero"), 1)
            pool.memset(BDV[:, :], 0.0).then_inc(S("bd_zero"), 1)
            pool.memset(onescol[:, :], 1.0).then_inc(S("consts"), 1)
            pool.memset(ones_b[:, :], 1.0).then_inc(S("consts"), 1)
            pool.memset(tri_b[:, :], 1.0).then_inc(S("cst"), 1)
            pool.iota(iota_i[:, :], [[1, N]], base=0, channel_multiplier=0).then_inc(S("consts"), 1)
            pool.iota(ids_i[:, :], [[P, 2 * T]], base=1, channel_multiplier=1).then_inc(S("consts"), 1)
            pool.iota(pcol_i[:, :], [[0, 1]], base=0, channel_multiplier=1).then_inc(S("consts"), 1)
            pool.memset(epsc[:, :], EPS).then_inc(S("consts"), 1)
            pool.wait_ge(*count("cst", 2))
            pool.affine_select(out=ident[:, :], in_=ident[:, :], compare_op=ALU.not_equal, fill=1.0, base=0,
                               pattern=[[-1, P]], channel_multiplier=1).then_inc(S("consts"), 1)
            pool.affine_select(out=tri_b[:, :], in_=tri_b[:, :], compare_op=ALU.is_gt, fill=0.0, base=0,
                               pattern=[[1, P]], channel_multiplier=-1).then_inc(S("consts"), 1)
            pool.wait_ge(*count("gval_ready", 2))
            pool.partition_all_reduce(gred[:, :], gval[:, :], NG, RMAX).then_inc(S("gred_ready"), 1)

            def bias(n, row):
                for m in range(T):
                    pool.wait_ge(*count(f"xn_ready{n}", m + 1))
                    pool.tensor_tensor(X[:, m, :], X[:, m, :], BC[:, row, :], ALU.add).then_inc(S(f"x_biased{n}"), 1)

            pool.wait_ge(*count("bias_in", 16 * 8))
            bias(0, 1)
            pool.tensor_tensor(BC[:, 3, :], BC[:, 3, :], BC[:, 4, :], ALU.add).then_inc(S("biases_added"), 1)
            for m in range(T):
                pool.wait_ge(*count("h_done0", m + 1))
                pool.tensor_tensor(H[:, m, :], H[:, m, :], BC[:, 0, :], ALU.add).then_inc(S("h_biased"), 1)

            pool.wait_ge(*count("most_part", 1))
            pool.partition_all_reduce(most[:, 1:2], most[:, 0:1], P, RMAX).then_inc(S("most_all"), 1)
            pool.wait_ge(*count("most_all", 1))
            pool.tensor_copy(most_i[:, :], most[0:1, 1:2]).then_inc(S("most_ready"), 1)
            bias(1, 2)
            for m in range(T):
                pool.wait_ge(*count("x_biased1", m + 1))
                pool.wait_ge(*count("shared_done", m + 1))
                pool.tensor_tensor(X[:, m, :], X[:, m, :], XN[:, m, :], ALU.add).then_inc(S("shared_added"), 1)

            def gather0(i, u):
                e = U * i + u
                pool.tensor_copy(icur[0:CAP, u:u + 1], ic0[:, ds(e, 1)]).then_inc(S("icur_set"), 1)
                pool.wait_ge(*count("icur_set", e + 1))
                pool.sem_inc(S("pool_passed"))
                pool.indirect_dma_start(G0[u], None, toks[0], bass.IndirectOffsetOnAxis(ap=icur[0:CAP, u:u + 1], axis=0)
                                        ).then_inc(S(f"g{u}_in0"), 16)

            def scatter0(i, u):
                e = U * i + u
                b = u % 2
                pool.wait_ge(*count(f"scattered{b}", 16 * (U // 2 * i + u // 2)))
                pool.tensor_copy(iout[0:CAP, u:u + 1], ic0[:, ds(e, 1)]).then_inc(S("iout_set"), 1)
                pool.wait_ge(*count("iout_set", e + 1))
                pool.wait_ge(*count("ey_done0", e + 1))
                pool.sem_inc(S("pool_passed"))
                pool.indirect_dma_start(accs[b], bass.IndirectOffsetOnAxis(ap=iout[0:CAP, u:u + 1], axis=0), Y0[b], None,
                                        compute_op=ALU.add).then_inc(S(f"scattered{b}"), 16)

            pool.wait_ge(*count("ic0_ready", 1))
            pool.wait_ge(*count("tok_out", 16))
            pool.wait_ge(*count("mix_ready0", T))
            for u in range(U):
                gather0(0, u)
            pool.wait_ge(*count("acc_out", 32))
            with pool.Fori(1, E0 // U) as i:
                for u in range(U):
                    scatter0(i - 1, u)
                    gather0(i, u)
            for u in range(U):
                scatter0(E0 // U - 1, u)

            for m in range(T):
                if m == 0:
                    pool.wait_ge(*count("ey_ready0", E0))
                pool.tensor_copy(AT[:, m, :], CT[:, m, :]).then_inc(S("counts_rounded"), 1)
            pool.wait_ge(*count("biases_added", 1))
            bias(2, 3)
            pool.wait_ge(*count("late_in", 48))
            bias(3, 1)

            def gather1(i, u, first=False):
                e = U * i + u
                if not first:
                    pool.wait_ge(*count(f"g{u}_in1", 16 * i))
                    pool.wait_ge(*count("eT_ready1", e + (1 - U)))
                pool.tensor_copy(icur[0:C, u:u + 1], rows_i[:, 0, ds(e, 1)]).then_inc(S("rows_set"), 1)
                pool.wait_ge(*count("rows_set", e + 1))
                pool.sem_inc(S("pool_passed"))
                pool.indirect_dma_start(G1[u], None, toks[1], bass.IndirectOffsetOnAxis(ap=icur[0:C, u:u + 1], axis=0),
                                        bounds_check=N - 1, oob_is_err=False).then_inc(S(f"g{u}_in1"), 16)

            def scatter1(i, u):
                e = U * i + u
                pool.wait_ge(*count(f"y1_out{u}", 16 * i))
                pool.tensor_copy(iout[0:C, u:u + 1], rows_i[:, 1, ds(e, 1)]).then_inc(S("outs_set"), 1)
                pool.wait_ge(*count("outs_set", e + 1))
                pool.wait_ge(*count("ey_done1", e + 1))
                pool.sem_inc(S("pool_passed"))
                pool.indirect_dma_start(chosen_d, bass.IndirectOffsetOnAxis(ap=iout[0:C, u:u + 1], axis=0), Y1[u], None,
                                        bounds_check=2 * N - 1, oob_is_err=False).then_inc(S(f"y1_out{u}"), 16)

            pool.wait_ge(*count("rows_ready", 1))
            pool.wait_ge(*count("table_ready", 3))
            pool.wait_ge(*count("tok_out", 32))
            turns = pool.value_load(trow_i[0:1, P:P + 1], min_val=3, max_val=MAXT // U)
            for u in range(U):
                gather1(0, u, first=True)
            pool.wait_ge(*count("outs_ready", 1))
            with pool.Fori(1, turns) as i:
                for u in range(U):
                    gather1(i, u)
                    scatter1(i - 1, u)
            last = pool.value_load(trow_i[0:1, P + 2:P + 3], min_val=2, max_val=MAXT // U - 1)
            for u in range(U):
                scatter1(last, u)

        @block.scalar
        def _(act):
            def norm_root(n, m):
                act.wait_ge(*count(f"var_ready{n}", m + 1))
                act.activation(sd[:, m:m + 1], mv[:, m, 1:2], ACT.Sqrt, bias=epsc[:, 0:1]).then_inc(S(f"sd_ready{n}"), 1)

            def evict_xT(n, m):
                act.wait_ge(*count(f"xT_ready{n}", m + 1))
                act.activation(XT[:, :, m * P:(m + 1) * P],
                               PS[:, norm_banks(n)[m % len(norm_banks(n))], :].rearrange("p (k n) -> p k n", k=K), ACT.Copy
                               ).then_inc(S(f"xT_done{n}"), 1)

            def norm(n, lag):
                for m in range(T + lag):
                    if m < T:
                        norm_root(n, m)
                    if m >= lag:
                        evict_xT(n, m - lag)

            act.wait_ge(*count("consts", 8))
            for k in range(K):
                act.wait_ge(*count("wT_ready", k + 1))
                act.activation(W[:, 3, k, :], PS[:, 4 + k, :], ACT.Copy).then_inc(S("wT_done"), 1)
            norm(0, 1)
            act.wait_ge(*count("grow_ready", 1))

            def evict_h(m):
                act.wait_ge(*count("h_ready0", m + 1))
                act.activation(H[:, m, :], PS[:, 4 + m % 3, :], ACT.Copy).then_inc(S("h_done0"), 1)

            start = 0
            for m in range(T):
                delta = act.value_load(grow_i[0:1, 0, m:m + 1], min_val=0, max_val=2 * SHIFT)
                end = act.value_load(grow_i[0:1, 1, m:m + 1], min_val=1, max_val=NG * (m + 1))
                with act.Fori(start, end) as v:
                    group = nc.s_assert_within(v + delta - SHIFT, 0, NG - 1, skip_runtime_bounds_check_because=
                                               "the table holds only visits to groups that exist")
                    act.wait_ge(*count("onehot_d_ready", v * 2))
                    act.activation(minus_dst, edge_c[:, 1, ds(group * 4, 4)], ACT.Copy, scale=-1.0
                                   ).then_inc(S("minus_set"), 1)
                    act.wait_ge(*count("minus_set", v + 1))
                    for j in range(4):
                        ins = act.activation(away[:, j, :], iota_h[:, m * P:(m + 1) * P], ACT.Abs,
                                             bias=minus_dst[:, j:j + 1])
                        if j % 2 == 1:
                            ins.then_inc(S("away_set"), 1)
                    for h in range(2):
                        pair = slice(2 * h, 2 * h + 2)
                        act.wait_ge(*count("away_set", v * 2 + (h + 1)))
                        act.wait_ge(*count("onehot_free", v * 2 + (h + 1)))
                        act.activation(onehot_d[:, pair, :], away[:, pair, :], ACT.Relu, bias=onescol[:, 0:1],
                                       scale=-1.0).then_inc(S("onehot_d_ready"), 1)
                start = end
                act.wait_ge(*count("ct_ready", m + 1))
                for h in range(2):
                    act.activation(CT[:, m, h * 512:(h + 1) * 512], PS[:, 2 * (m % 2) + h, :], ACT.Copy
                                   ).then_inc(S("ct_done"), 1)
                if m >= 1:
                    evict_h(m - 1)
            evict_h(T - 1)
            act.wait_ge(*count("deg_done", 1))
            act.activation(sd[:, :], deg[:, 0:T], ACT.Sqrt).then_inc(S("degroot_ready"), 1)
            act.wait_ge(*count("dinv_ready", 1))
            for m in range(T):
                act.wait_ge(*count("h_biased", m + 1))
                act.activation(H_hi[:, m, :], H[:, m, :], ACT.Copy, scale=dinv[:, m:m + 1]
                               ).then_inc(S("h_rounded"), 1)

            def exp_q(L):
                for t in range(T):
                    w = HEADS * (SLICE if L == 0 else DH)
                    act.wait_ge(*count(f"q_shifted{L}", t + 1))
                    act.activation(Q[:, t, 0:w], Q[:, t, 0:w], ACT.Exp).then_inc(S(f"q_exp{L}"), 1)

            def evict_v(L):
                for m in range(T):
                    act.wait_ge(*count(f"v_ready{L}", m + 1))
                    act.activation(V[:, m, :], PS[:, 4 + m % 4, :], ACT.Copy).then_inc(S(f"v_done{L}"), 1)

            def exp_k(L, g):
                act.wait_ge(*count(f"kmax_ready{L}", g + 1))
                act.activation(KTr[:, g, :], KTr[:, g, :], ACT.Exp, bias=kmax[:, g:g + 1],
                               accum_out=ksum[:, g:g + 1]).then_inc(S(f"k_exp{L}"), 1)

            def evict_kr(L):
                w = HEADS * (SLICE if L == 0 else DH)
                per = 512 // w
                for i in range(T // per):
                    act.wait_ge(*count(f"kr_ready{L}", i + 1))
                    for j in range(per):
                        ins = act.activation(KR[:, i * per + j, 0:w], PS[:, i % 4, j * w:(j + 1) * w], ACT.Copy)
                    ins.then_inc(S(f"kr_done{L}"), 1)

            def evict_qT(L):
                for i in range(2 * (2 if L == 0 else K)):
                    act.wait_ge(*count(f"qT_ready{L}", i + 1))
                    act.activation(QT[:, i // 2, (i % 2) * 512:(i % 2 + 1) * 512], PS[:, 4 + i % 4, :], ACT.Copy
                                   ).then_inc(S(f"qT_done{L}"), 1)

            def evict_oT(L):
                for i in range(2 * K):
                    act.wait_ge(*count(f"oT_ready{L}", i + 1))
                    act.activation(OT[:, i // 2, (i % 2) * 512:(i % 2 + 1) * 512], PS[:, 4 + i % 4, :], ACT.Copy
                                   ).then_inc(S(f"oT_done{L}"), 1)

            def softmax_exp(n):
                act.wait_ge(*count(f"logit_shifted{n}", 1))
                w = (E0, E1)[n]
                act.activation(PR[:, :, 0:w], PR[:, :, 0:w], ACT.Exp).then_inc(S(f"logit_exp{n}"), 1)

            act.wait_ge(*count("bias_in", 16 * 8))
            act.wait_ge(*count("gnn_ready0", T))
            for i in range(2 * K):
                act.wait_ge(*count("xm_ready", i + 1))
                act.activation(XM[:, i // 2, (i % 2) * 512:(i % 2 + 1) * 512], PS[:, 4 + i % 4, :], ACT.Identity,
                               bias=cols_sm[:, 192 + i // 2:193 + i // 2]).then_inc(S("xm_done"), 1)
            for i in range(4):
                act.wait_ge(*count("k_ready0", i + 1))
                act.activation(KTr[:, i // 2, (i % 2) * 512:(i % 2 + 1) * 512], PS[:, i % 4, :], ACT.Copy
                               ).then_inc(S("k_done0"), 1)
            for g in range(2):
                exp_k(0, g)
            exp_q(0)
            evict_v(0)
            evict_kr(0)
            evict_qT(0)
            evict_oT(0)
            norm(1, 3)
            softmax_exp(0)
            for i in range(2 * HJ):
                act.wait_ge(*count("sh_ready", i + 1))
                act.activation(SHT[:, i // 2, (i % 2) * 512:(i % 2 + 1) * 512], PS[:, 4 + i % 4, :],
                               ACT.Gelu_apprx_tanh, bias=cols_sm[:, 196 + i // 2:197 + i // 2]
                               ).then_inc(S("sh_done"), 1)

            act.wait_ge(*count("tok_out", 16))
            for m in range(T):
                act.wait_ge(*count("shared_ready", m + 1))
                act.activation(XN[:, m, :], PS[:, 4 + m % 4, :], ACT.Copy).then_inc(S("shared_done"), 1)

            def expert(L, i, u, first):
                e = U * i + u
                n, gt, ht = (CAP, GT0, HT0) if L == 0 else (C, GT1, HT1)
                b = u % 2
                act.wait_ge(*count(f"eT_ready{L}", e + 1))
                if not (first and u < 2):
                    act.wait_ge(*count(f"eh_ready{L}", e - 1))
                act.activation(gt[b].rearrange("p k n -> p (k n)"), PS[:, b, 0:K * n], ACT.Copy
                               ).then_inc(S(f"eT_done{L}"), 1)
                act.wait_ge(*count(f"eh_ready{L}", e + 1))
                if not (first and u < 2):
                    act.wait_ge(*count(f"ey_ready{L}", e - 1))
                if L == 1:
                    x = act.value_load(trow_i[0:1, ds(e, 1)], min_val=0, max_val=E1 - 1)
                    bias = [cols_sm[:, ds(x + (32 + j * E1), 1)] for j in range(HJ)]
                else:
                    bias = [cols_sm[:, ds(e + j * E0, 1)] for j in range(HJ)]
                for j in range(HJ):
                    ins = act.activation(ht[b][:, j, :], PS[:, 2 + b, j * n:(j + 1) * n],
                                         ACT.Gelu_apprx_tanh if L == 0 else ACT.Relu, bias=bias[j])
                ins.then_inc(S(f"eh_done{L}"), 1)

            for u in range(U):
                expert(0, 0, u, True)
            with act.Fori(1, E0 // U) as i:
                for u in range(U):
                    expert(0, i, u, False)

            norm(2, 1)
            for m in range(T):
                act.wait_ge(*count("h_ready1", m + 1))
                act.activation(H_hi[:, m, :], PS[:, 4 + m % 4, :], ACT.Copy).then_inc(S("h1_rounded"), 1)
            for i in range(2 * K):
                act.wait_ge(*count("k_low", i + 1))
                k = KTr[:, i // 2, (i % 2) * 512:(i % 2 + 1) * 512]
                act.activation(k, k, ACT.Exp).then_inc(S("k_elu"), 1)
            for g in range(K):
                exp_k(1, g)
            exp_q(1)
            evict_v(1)
            evict_kr(1)
            evict_qT(1)
            evict_oT(1)
            norm(3, 3)
            softmax_exp(1)
            act.wait_ge(*count("swT_ready", 1))
            for h in range(2):
                act.activation(SWT[:, h * 512:(h + 1) * 512], PS[0:E1, 4 + h, :], ACT.Copy).then_inc(S("swT_done"), 1)
            for m in range(T):
                act.wait_ge(*count("rb_ready1", m + 1))
                act.activation(RB[:, m, :], PS[:, 4 + m % 4, :], ACT.Copy).then_inc(S("rb_done1"), 1)
            act.wait_ge(*count("table_ready", 3))
            turns = act.value_load(trow_i[0:1, P:P + 1], min_val=3, max_val=MAXT // U)
            for u in range(U):
                expert(1, 0, u, True)
            with act.Fori(1, turns) as i:
                for u in range(U):
                    expert(1, i, u, False)
            for m in range(T):
                norm_root(4, m)

        @block.tensor
        def _(pe):
            def tr(bank, c0, in_, w=P):
                rows = in_.shape[0]
                return pe.transpose(PS[0:w, bank, c0:c0 + rows], in_, ident[0:rows, 0:rows])

            def transposes(n, m):
                banks = norm_banks(n)
                pe.wait_ge(*count(f"xn_ready{n}", m + 1))
                if m >= len(banks):
                    pe.wait_ge(*count(f"xT_done{n}", m + 1 - len(banks)))
                bank = banks[m % len(banks)]
                for k in range(K):
                    ins = tr(bank, k * P, XN[:, m, k * P:(k + 1) * P])
                ins.then_inc(S(f"xT_ready{n}"), 1)

            def token_rows(name, base, pairs, done, width=D, norm=None):
                def logits(m):
                    w, at = ((E0, 0), (E1, E0))[norm // 2]
                    pe.wait_ge(*count(f"xT_done{norm}", m + 1))
                    for k in range(K):
                        ins = pe.matmul(PS[:, 7, m * w:(m + 1) * w], XT[:, k, m * P:(m + 1) * P],
                                        GW[:, k, at:at + w], start=(k == 0), stop=(k == K - 1), skip_group_check=True)
                    if m == T - 1:
                        ins.then_inc(S(f"logit_ready{norm // 2}"), 1)

                if norm:
                    pe.wait_ge(*count("gate_in", 48))
                for m in range(T):
                    if m >= 4:
                        pe.wait_ge(*count(done, m - 3))
                    for n, (left, right) in enumerate(pairs):
                        ins = pe.matmul(PS[:, base + m % 4, 0:width], left[:, m * P:(m + 1) * P], right,
                                        start=(n == 0), stop=(n == len(pairs) - 1))
                    ins.then_inc(S(name), 1)
                    if norm and m >= 3:
                        transposes(norm, m - 3)
                    if norm and m >= 4:
                        logits(m - 4)
                if norm:
                    for m in range(T - 3, T):
                        transposes(norm, m)
                        logits(m - 1)
                    logits(T - 1)

            pe.wait_ge(*count("consts", 8))
            pe.wait_ge(*count("edge_f_ready", 2))
            pe.wait_ge(*count("small_in", 32))
            tr(0, 0, edge_f[:, 0, :])
            tr(0, P, edge_f[:, 1, :]).then_inc(S("small_ready"), 1)
            for j in range(HJ):
                tr(1, j * E0, rows_sm[0:E0, 0, j * P:(j + 1) * P])
                ins = tr(1, 32 + j * E1, rows_sm[0:E1, 1, j * P:(j + 1) * P])
            ins.then_inc(S("small_ready"), 1)
            pe.wait_ge(*count("gnnw_in", 16))
            for k in range(K):
                for j in range(K):
                    ins = tr(4 + k, j * P, W[:, 0, j, k * P:(k + 1) * P])
                ins.then_inc(S("wT_ready"), 1)
            pe.wait_ge(*count("small_done", 2))
            for m in range(T):
                transposes(0, m)

            pe.nop().then_inc(S("onehot_free"), 2)
            pe.wait_ge(*count("xT_done0", T))
            pe.wait_ge(*count("zeros_ready", 1))
            pe.wait_ge(*count("grow_ready", 1))
            pe.wait_ge(*count("wT_done", K))

            def degree_parts(k):
                pe.wait_ge(*count("ct_done", 2 * (k + 1)))
                pe.wait_ge(*count("at_done", k + 1))
                for m in range(T):
                    pe.matmul(PS[:, 7, k * T + m:k * T + m + 1], AT[:, k, m * P:(m + 1) * P].bitcast(F32),
                              onescol[:, :], start=True, stop=True, skip_group_check=True)
                    ins = pe.matmul(PS[:, 7, T * T + k * T + m:T * T + k * T + m + 1], CT[:, k, m * P:(m + 1) * P],
                                    onescol[:, :], start=True, stop=True, skip_group_check=True)
                ins.then_inc(S("deg_ready"), 1)

            start = 0
            for m in range(T):
                if m >= 2:
                    pe.wait_ge(*count("ct_done", 2 * (m - 1)))
                banks = [PS[:, 2 * (m % 2) + h, :] for h in range(2)]
                for h in range(2):
                    pe.matmul(banks[h], zero_b[:, 0:P], zero_b, start=True, stop=False)
                end = pe.value_load(grow_i[0:1, 1, m:m + 1], min_val=1, max_val=NG * (m + 1))
                with pe.Fori(start, end) as v:
                    for j in range(4):
                        if j % 2 == 0:
                            pe.wait_ge(*count("onehot_ready", v * 2 + (j // 2 + 1)))
                            pe.wait_ge(*count("onehot_d_ready", v * 2 + (j // 2 + 1)))
                        pe.matmul(banks[0], onehot_d[:, j, :], onehot_s[:, j, 0:512], start=False, stop=False)
                        ins = pe.matmul(banks[1], onehot_d[:, j, :], onehot_s[:, j, 512:1024], start=False, stop=False)
                        if j % 2 == 1:
                            ins.then_inc(S("onehot_free"), 1)
                start = end
                pe.matmul(banks[0], zero_b[:, 0:P], zero_b, start=False, stop=True)
                pe.matmul(banks[1], zero_b[:, 0:P], zero_b, start=False, stop=True).then_inc(S("ct_ready"), 1)
                if m >= 3:
                    pe.wait_ge(*count("h_done0", m - 2))
                for k in range(K):
                    ins = pe.matmul(PS[:, 4 + m % 3, :], XT[:, k, m * P:(m + 1) * P], W[:, 3, k, :],
                                    start=(k == 0), stop=(k == K - 1))
                ins.then_inc(S("h_ready0"), 1)
                if m >= 1:
                    degree_parts(m - 1)
            degree_parts(T - 1)
            pe.wait_ge(*count("h_done0", T))
            pe.wait_ge(*count("deg_done", 1))
            for m in range(T):
                if m >= 4:
                    pe.wait_ge(*count("gnn_done0", m - 3))
                for k in range(T):
                    if m == 0:
                        pe.wait_ge(*count("h_split", k + 1))
                    pe.matmul(PS[:, 4 + m % 4, :], AT[:, k, m * P:(m + 1) * P], H_hi[:, k, :],
                              start=(k == 0), stop=False)
                    ins = pe.matmul(PS[:, 4 + m % 4, :], AT[:, k, m * P:(m + 1) * P], H_lo[:, k, :],
                                    start=False, stop=(k == T - 1))
                ins.then_inc(S("gnn_ready0"), 1)

            pe.wait_ge(*count("win_in", 16))
            for i in range(2 * K):
                if i < 4:
                    pe.wait_ge(*count("gnn_done0", T))
                else:
                    pe.wait_ge(*count("xm_done", i - 3))
                for k in range(K):
                    ins = pe.matmul(PS[:, 4 + i % 4, :], W[:, 1, k, (i // 2) * P:(i // 2 + 1) * P],
                                    XT[:, k, (i % 2) * 512:(i % 2 + 1) * 512], start=(k == 0), stop=(k == K - 1))
                ins.then_inc(S("xm_ready"), 1)
            pe.wait_ge(*count("xm_done", 2 * K))
            pe.wait_ge(*count("bd_in", 16 * 6))
            for i in range(4):
                g, half = i // 2, i % 2
                for s in range(2):
                    ins = pe.matmul(PS[s * 64:(s + 1) * 64, i % 4, :], BDK[:, :],
                                    XM[:, 2 * g + s, half * 512:(half + 1) * 512], start=True, stop=True,
                                    skip_group_check=True)
                ins.then_inc(S("k_ready0"), 1)
            for m in range(T):
                if m == 0:
                    pe.wait_ge(*count("k_done0", 4))
                if m >= 4:
                    pe.wait_ge(*count("q_done0", m - 3))
                for c in range(K):
                    ins = pe.matmul(PS[:, m % 4, c * 64:(c + 1) * 64], XM[:, c, m * P:(m + 1) * P], BDQ[:, :],
                                    start=True, stop=True, skip_group_check=True)
                ins.then_inc(S("q_ready0"), 1)
            for m in range(T):
                if m >= 4:
                    pe.wait_ge(*count("v_done0", m - 3))
                for c in range(K):
                    ins = pe.matmul(PS[:, 4 + m % 4, c * P:(c + 1) * P], XM[:, c, m * P:(m + 1) * P], BDV[:, :],
                                    start=True, stop=True, skip_group_check=True)
                ins.then_inc(S("v_ready0"), 1)

            def attend(L):
                groups = 2 if L == 0 else K
                w = groups * P
                per = 512 // w
                pe.wait_ge(*count(f"k_exp{L}", groups))
                pe.wait_ge(*count(f"q_done{L}", T))
                for i in range(T // per):
                    if i >= 4:
                        pe.wait_ge(*count(f"kr_done{L}", i - 3))
                    for j in range(per):
                        for g in range(groups):
                            ins = tr(i % 4, j * w + g * P, KTr[:, g, (i * per + j) * P:(i * per + j + 1) * P])
                    ins.then_inc(S(f"kr_ready{L}"), 1)
                pe.wait_ge(*count(f"kr_done{L}", T // per))
                pe.wait_ge(*count(f"v_done{L}", T))
                for i in range(2 * groups):
                    g, half = i // 2, i % 2
                    pe.wait_ge(*count(f"q_soft{L}", 4 * (half + 1)))
                    if i >= 4:
                        pe.wait_ge(*count(f"qT_done{L}", i - 3))
                    for j in range(4):
                        ins = tr(4 + i % 4, j * P, Q[:, 4 * half + j, g * P:(g + 1) * P])
                    ins.then_inc(S(f"qT_ready{L}"), 1)
                vw = D // groups
                for g in range(groups):
                    for m in range(T):
                        ins = pe.matmul(PS[:, g, 0:vw], KR[:, m, g * P:(g + 1) * P],
                                        V[:, m, g * vw:(g + 1) * vw], start=(m == 0), stop=(m == T - 1))
                    ins.then_inc(S(f"kv_ready{L}"), 1)
                pe.wait_ge(*count(f"kv_done{L}", groups))
                pe.wait_ge(*count(f"qT_done{L}", 2 * groups))
                for i in range(2 * K):
                    c, half = i // 2, i % 2
                    if i >= 4:
                        pe.wait_ge(*count(f"oT_done{L}", i - 3))
                    g, at = (c // 2, (c % 2) * P) if L == 0 else (c, 0)
                    pe.matmul(PS[:, 4 + i % 4, :], KV[:, g * vw + at:g * vw + at + P], QT[:, g, half * 512:(half + 1) * 512],
                              start=True, stop=True).then_inc(S(f"oT_ready{L}"), 1)
                pe.wait_ge(*count(f"oT_done{L}", 2 * K))

            attend(0)
            pe.wait_ge(*count("wout_in", 16))
            token_rows("mix_ready0", 0, [(OT[:, c], W[:, 2, c, :]) for c in range(K)], "mix_done0",
                       norm=1)

            pe.wait_ge(*count("mix_done0", T))
            pe.wait_ge(*count("xT_done1", T))
            pe.wait_ge(*count("shared_in", 32))
            sw1 = W[:, 0, 0:2, :].rearrange("p a b -> p (a b)").rearrange("p (k n) -> p k n", k=K)
            for i in range(2 * HJ):
                j, half = i // 2, i % 2
                if i == 3:
                    pe.wait_ge(*count("logit_shifted0", 1))
                for k in range(K):
                    ins = pe.matmul(PS[:, 4 + i % 4, :], sw1[:, k, j * P:(j + 1) * P],
                                    XT[:, k, half * 512:(half + 1) * 512], start=(k == 0), stop=(k == K - 1))
                ins.then_inc(S("sh_ready"), 1)
            pe.wait_ge(*count("probs_ready0", 1))
            for m in range(T):
                ins = tr(m // 4, (m % 4) * P, PR[:, m, 0:E0], E0)
            ins.then_inc(S("pT_ready"), 1)
            pe.wait_ge(*count("sh_done", 2 * HJ))
            for m in range(T):
                if m >= 4:
                    pe.wait_ge(*count("shared_done", m - 3))
                for j in range(HJ):
                    ins = pe.matmul(PS[:, 4 + m % 4, :], SHT[:, j, m * P:(m + 1) * P], W[:, 0, 2 + j, :],
                                    start=(j == 0), stop=(j == HJ - 1))
                ins.then_inc(S("shared_ready"), 1)
            pe.wait_ge(*count("top_ready", 2))
            tr(0, 0, ixf0[:, :], CAP)
            tr(0, E0, sc0[:, :], CAP).then_inc(S("scT_ready"), 1)
            pe.wait_ge(*count("shared_done", T))
            for m in range(T):
                if m >= 4:
                    pe.wait_ge(*count("rb_done0", m - 3))
                pe.matmul(PS[:, 4 + m % 4, :], PTW[:, m * P:(m + 1) * P], B2R0[:, :], start=True, stop=True
                          ).then_inc(S("rb_ready0"), 1)
            pe.wait_ge(*count("rb_done0", T))
            pe.wait_ge(*count("scT_done", 1))

            def expert_T(L, e, u, i):
                n, g = (CAP, G0) if L == 0 else (C, G1)
                pe.wait_ge(*count(f"g{u}_in{L}", (i + 1) * 16))
                pe.sem_inc(S("pe_passed"))
                for k in range(K):
                    ins = tr(u % 2, k * n, g[u][:, k * P:(k + 1) * P])
                ins.then_inc(S(f"eT_ready{L}"), 1)

            def expert_h(L, e, u, i):
                n, gt = (CAP, GT0) if L == 0 else (C, GT1)
                b = u % 2
                pe.wait_ge(*count(f"eT_done{L}", e + 1))
                pe.wait_ge(*count(f"ew{u}_in{L}", (i + 1) * 32))
                for j in range(HJ):
                    for k in range(K):
                        ins = pe.matmul(PS[:, 2 + b, j * n:(j + 1) * n], EW1[u][:, k, j * P:(j + 1) * P], gt[b][:, k, :],
                                        start=(k == 0), stop=(k == K - 1), skip_group_check=True)
                ins.then_inc(S(f"eh_ready{L}"), 1)

            def expert(L, i, u, first=False, last=False):
                e = U * i + u
                n, ht = (CAP, HT0) if L == 0 else (C, HT1)
                b = u % 2
                if not (last and u == U - 1):
                    expert_h(L, e + 1, (u + 1) % U, i + (u + 1) // U)
                if not (last and u >= U - 2):
                    expert_T(L, e + 2, (u + 2) % U, i + (u + 2) // U)
                pe.wait_ge(*count(f"eh_done{L}", e + 1))
                if not (first and u < 2):
                    pe.wait_ge(*count(f"ey_done{L}", e - 1))
                for j in range(HJ):
                    ins = pe.matmul(PS[0:n, 4 + b, :], ht[b][:, j, :], EW2[u][:, j, :],
                                    start=(j == 0), stop=(j == HJ - 1))
                ins.then_inc(S(f"ey_ready{L}"), 1)

            def experts_begin(L):
                expert_T(L, 0, 0, 0)
                expert_h(L, 0, 0, 0)
                expert_T(L, 1, 1, 0)

            experts_begin(0)
            for u in range(U):
                expert(0, 0, u, first=True)
            with pe.Fori(1, E0 // U - 1) as i:
                for u in range(U):
                    expert(0, i, u)
            for u in range(U):
                expert(0, E0 // U - 1, u, last=True)

            for m in range(T):
                transposes(2, m)
            pe.wait_ge(*count("ey_done0", E0))
            pe.wait_ge(*count("xT_done2", T))
            pe.wait_ge(*count("wn_in", 16))
            token_rows("h_ready1", 4, [(XT[:, k], W[:, 3, k, :]) for k in range(K)], "h_done1")
            pe.wait_ge(*count("h_done1", T))
            pe.wait_ge(*count("counts_rounded", T))
            pe.wait_ge(*count("most_ready", 1))
            most = pe.value_load(most_i[0:1, 0:1], min_val=0, max_val=NE)
            with pe.If(most <= EXACT):
                token_rows("gnn_ready1", 0, [(AT[:, k], h[:, k, :]) for k in range(T) for h in (H_hi, H_lo)],
                           "gnn_done1")
            with pe.If(most > EXACT):
                token_rows("gnn_ready1", 0, [(CT[:, k], h[:, k, :].bitcast(F32)) for k in range(T)
                                             for h in (H_hi, H_lo)], "gnn_done1")
            pe.wait_ge(*count("gnn_done1", T))
            pe.wait_ge(*count("wk_in", 16))
            for i in range(2 * K):
                c, half = i // 2, i % 2
                if i >= 4:
                    pe.wait_ge(*count("k_done1", i - 3))
                for k in range(K):
                    ins = pe.matmul(PS[:, i % 4, :], W[:, 0, k, c * P:(c + 1) * P],
                                    XT[:, k, half * 512:(half + 1) * 512], start=(k == 0), stop=(k == K - 1))
                ins.then_inc(S("k_ready1"), 1)
            pe.wait_ge(*count("k_done1", 2 * K))
            pe.wait_ge(*count("wq_in", 16))
            token_rows("q_ready1", 0, [(XT[:, k], W[:, 1, k, :]) for k in range(K)], "q_done1")
            pe.wait_ge(*count("wv_in", 16))
            token_rows("v_ready1", 4, [(XT[:, k], W[:, 2, k, :]) for k in range(K)], "v_done1")
            attend(1)
            pe.wait_ge(*count("wc_in", 16))
            pe.wait_ge(*count("proj_in", 16))
            token_rows("mix_ready1", 0, [(XT[:, k], W[:, 3, k, :]) for k in range(K)]
                       + [(OT[:, c], W[:, 1, c, :]) for c in range(K)], "mix_done1", norm=3)

            pe.wait_ge(*count("mix_done1", T))
            pe.wait_ge(*count("xT_done3", T))
            pe.wait_ge(*count("mb_ready", 1))
            for m in range(T):
                for q in range(m + 1):
                    pe.matmul(PS[:, 1, m * E1:(m + 1) * E1], tri_b[:, :] if q == m else ones_b[:, :], MB[:, q, :],
                              start=(q == 0), stop=(q == m), skip_group_check=True)
            for q in range(T):
                ins = pe.matmul(PS[:, 2, 0:E1], ones_b[:, :], MB[:, q, :], start=(q == 0), stop=(q == T - 1))
            ins.then_inc(S("place_ready"), 1)
            pe.wait_ge(*count("ecol_ready", 1))
            tr(3, 0, ecol[:, :], 1).then_inc(S("erow_ready"), 1)
            pe.wait_ge(*count("sww_ready", 1))
            for m in range(T):
                ins = tr(4 + m // 4, (m % 4) * P, SWW[:, m, :], E1)
            ins.then_inc(S("swT_ready"), 1)
            pe.wait_ge(*count("swT_done", 2))
            pe.wait_ge(*count("late_in", 48))
            for m in range(T):
                if m >= 4:
                    pe.wait_ge(*count("rb_done1", m - 3))
                pe.matmul(PS[:, 4 + m % 4, :], SWT[:, m * P:(m + 1) * P], B2R1[:, :], start=True, stop=True
                          ).then_inc(S("rb_ready1"), 1)
            pe.wait_ge(*count("hot_ready", 1))
            for a in range(2 * T):
                ins = pe.matmul(PS[0:C, 0, 0:MAXT], lane_hot[:, a, :], tile_hot[:, a, :], start=(a == 0),
                                stop=(a == 2 * T - 1))
            ins.then_inc(S("rows_summed"), 1)
            pe.wait_ge(*count("table_ready", 3))
            pe.wait_ge(*count("rows_ready", 1))
            pe.wait_ge(*count("rb_done1", T))
            turns = pe.value_load(trow_i[0:1, P:P + 1], min_val=3, max_val=MAXT // U)
            experts_begin(1)
            for u in range(U):
                expert(1, 0, u, first=True)
            with pe.Fori(1, turns - 1) as i:
                for u in range(U):
                    expert(1, i, u)
            for u in range(U):
                expert(1, turns - 1, u, last=True)

        @block.vector
        def _(dve):
            own = [0]

            def step(ins):
                ins.then_inc(S("dve_step"), 1)
                own[0] += 1

            def settle():
                dve.wait_ge(*count("dve_step", own[0]))

            def stats(n, m, src):
                step(dve.bn_stats(st[:, m, :], src[:, m, :]))
                settle()
                dve.bn_aggr(mv[:, m, :], st[:, m, :]).then_inc(S(f"var_ready{n}"), 1)

            def inverse_root(n, m):
                dve.wait_ge(*count(f"sd_ready{n}", m + 1))
                step(dve.reciprocal(rs[:, m:m + 1], sd[:, m:m + 1]))
                settle()

            def norm(n, before):
                for m in range(T + 1):
                    if m < T:
                        before(m)
                        stats(n, m, X)
                    if m >= 1:
                        inverse_root(n, m - 1)
                        dve.tensor_scalar(XN[:, m - 1, :], X[:, m - 1, :], mv[:, m - 1, 0:1], rs[:, m - 1:m],
                                          ALU.subtract, ALU.mult).then_inc(S(f"xn_ready{n}"), 1)

            def input_tile(m):
                if m % 2 == 0:
                    dve.wait_ge(*count(f"x_in{m // 2}", 16))

            def add_mix(L, m):
                dve.wait_ge(*count(f"mix_ready{L}", m + 1))
                dve.tensor_tensor(X[:, m, :], X[:, m, :], PS[:, m % 4, :], ALU.add).then_inc(S(f"mix_done{L}"), 1)
                dve.wait_ge(*count(f"mix_done{L}", m + 1))

            def add_routed(m):
                if m % 2 == 0:
                    dve.wait_ge(*count(f"x_in{m // 2}", 48))
                step(dve.tensor_tensor(X[:, m, :], X[:, m, :], XN[:, m, :], ALU.add))
                settle()

            dve.wait_ge(*count("consts", 8))
            step(dve.tensor_copy(iota_h[:, :], iota_i[:, :]))
            step(dve.tensor_copy(iota_e[:, :], iota_i[:, 0:E1]))
            step(dve.tensor_scalar(limits[:, :], iota_i[:, 0:NC], float(C), None, ALU.mult))
            step(dve.tensor_copy(pcol[:, :], pcol_i[:, :]))
            step(dve.tensor_copy(ids[:, :], ids_i[:, :]))
            dve.wait_ge(*count("edges_in", 48))
            for i in range(2):
                dve.tensor_copy(edge_f[:, i, :], edge_i[:, i, :]).then_inc(S("edge_f_ready"), 1)
            step(dve.tensor_reduce(gmm[:, 0:1], dgrp_i[:, :], AX_X, ALU.min))
            step(dve.tensor_reduce(gmm[:, 1:2], dgrp_i[:, :], AX_X, ALU.max))
            settle()
            step(dve.tensor_scalar(gov[:, 0, :], iota_i[0:NG, 0:N:P], gmm[:, 1:2], None, ALU.is_le))
            step(dve.tensor_scalar(gov[:, 1, :], iota_i[0:NG, P - 1:N:P], gmm[:, 0:1], None, ALU.is_ge))
            step(dve.tensor_scalar(gov[:, 3, 0:1], pcol[0:NG, :], -1.0, float(NG), ALU.mult, ALU.add))
            step(dve.tensor_scalar(gov[:, 3, 1:2], pcol[0:NG, :], 1.0, None, ALU.add))
            settle()
            step(dve.tensor_tensor(gov[:, 2, :], gov[:, 0, :], gov[:, 1, :], ALU.mult))
            settle()
            dve.tensor_scalar(gval[:, 0:T], gov[:, 2, :], gov[:, 3, 0:1], None, ALU.mult).then_inc(S("gval_ready"), 1)
            dve.tensor_scalar(gval[:, T:2 * T], gov[:, 2, :], gov[:, 3, 1:2], None, ALU.mult
                              ).then_inc(S("gval_ready"), 1)
            dve.wait_ge(*count("small_ready", 2))
            dve.tensor_copy(edge_c[:, :, :].rearrange("p a b -> p (a b)"), PS[:, 0, 0:2 * P]
                            ).then_inc(S("small_done"), 1)
            dve.tensor_copy(cols_sm[:, 0:160], PS[:, 1, 0:160]).then_inc(S("small_done"), 1)
            dve.wait_ge(*count("small_done", 2))

            norm(0, input_tile)

            dve.wait_ge(*count("gred_ready", 1))
            step(dve.tensor_scalar(grow[:, 0, :], gred[0:1, 0:T], -1.0, float(NG), ALU.mult, ALU.add))
            settle()
            step(dve.tensor_scalar(grow[:, 1, :], grow[:, 0, :], float(NG - 1), None, ALU.min))
            settle()
            step(dve.tensor_tensor(grow[:, 2, :], gred[0:1, T:2 * T], grow[:, 1, :], ALU.subtract))
            settle()
            step(dve.tensor_scalar(grow[:, 3, :], grow[:, 2, :], 1.0, None, ALU.max))
            step(dve.memset(grow[:, 5, :], 0.0))
            settle()
            step(dve.tensor_tensor_scan(grow[:, 4, :], grow[:, 3, :], grow[:, 5, :], 0.0, ALU.add, ALU.add))
            settle()
            step(dve.tensor_tensor(grow[:, 5, :], grow[:, 4, :], grow[:, 3, :], ALU.subtract))
            step(dve.tensor_copy(grow_i[:, 1, :], grow[:, 4, :]))
            settle()
            step(dve.tensor_tensor(grow[:, 0, :], grow[:, 1, :], grow[:, 5, :], ALU.subtract))
            settle()
            step(dve.tensor_scalar(grow[:, 0, :], grow[:, 0, :], float(SHIFT), None, ALU.add))
            settle()
            dve.tensor_copy(grow_i[:, 0, :], grow[:, 0, :]).then_inc(S("grow_ready"), 1)
            dve.wait_ge(*count("grow_ready", 1))

            def adjacency(m):
                dve.wait_ge(*count("ct_done", 2 * (m + 1)))
                step(dve.tensor_scalar(AT[:, m, :], CT[:, m, :], 1.0, None, ALU.min))
                settle()
                dve.tensor_tensor(AT[:, m, m * P:(m + 1) * P], AT[:, m, m * P:(m + 1) * P].bitcast(F32), ident[:, :],
                                  ALU.max).then_inc(S("at_done"), 1)

            start = 0
            for m in range(T):
                delta = dve.value_load(grow_i[0:1, 0, m:m + 1], min_val=0, max_val=2 * SHIFT)
                end = dve.value_load(grow_i[0:1, 1, m:m + 1], min_val=1, max_val=NG * (m + 1))
                with dve.Fori(start, end) as v:
                    group = nc.s_assert_within(v + delta - SHIFT, 0, NG - 1, skip_runtime_bounds_check_because=
                                               "the table holds only visits to groups that exist")
                    dve.wait_ge(*count("onehot_ready", v * 2))
                    dve.tensor_copy(ends[:, :], edge_c[:, 0, ds(group * 4, 4)]).then_inc(S("ends_set"), 1)
                    dve.wait_ge(*count("ends_set", v + 1))
                    for j in range(4):
                        if j % 2 == 0:
                            dve.wait_ge(*count("onehot_free", v * 2 + (j // 2 + 1)))
                        ins = dve.tensor_scalar(onehot_s[:, j, :], iota_h[:, :], ends[:, j:j + 1],
                                                None, ALU.is_equal)
                        if j % 2 == 1:
                            ins.then_inc(S("onehot_ready"), 1)
                start = end
                if m >= 1:
                    adjacency(m - 1)
            adjacency(T - 1)

            dve.wait_ge(*count("deg_ready", T))
            parts = PS[:, 7, 0:2 * T * T].rearrange("p (s k m) -> p s m k", s=2, k=T)
            step(dve.tensor_reduce(deg[:, :].rearrange("p (s m) -> p s m", s=2), parts, AX_X, ALU.add))
            settle()
            dve.tensor_scalar(deg[:, 0:T], deg[:, 0:T], 1e-30, None, ALU.max).then_inc(S("deg_done"), 1)
            step(dve.reciprocal(rcnt[:, :], deg[:, T:2 * T]))
            dve.wait_ge(*count("degroot_ready", 1))
            dve.reciprocal(dinv[:, :], sd[:, :]).then_inc(S("dinv_ready"), 1)
            dve.wait_ge(*count("dinv_ready", 1))
            for m in range(T):
                dve.wait_ge(*count("h_rounded", m + 1))
                dve.scalar_tensor_tensor(H_lo[:, m, :], H[:, m, :], dinv[:, m:m + 1], H_hi[:, m, :].bitcast(F32),
                                         ALU.mult, ALU.subtract).then_inc(S("h_split"), 1)
            for m in range(T):
                dve.wait_ge(*count("gnn_ready0", m + 1))
                dve.wait_ge(*count("x_biased0", m + 1))
                dve.scalar_tensor_tensor(X[:, m, :], PS[:, 4 + m % 4, :], dinv[:, m:m + 1], X[:, m, :],
                                         ALU.mult, ALU.add).then_inc(S("gnn_done0"), 1)

            step(dve.tensor_reduce(most[:, 0:1], CT[:, :, :].rearrange("p a b -> p (a b)"), AX_X, ALU.max))
            settle()
            dve.engine_nop().then_inc(S("most_part"), 1)

            def key_max(L, g):
                step(dve.tensor_reduce(kmax[:, g:g + 1], KTr[:, g, :], AX_X, ALU.max, negate=True))
                settle()
                dve.engine_nop().then_inc(S(f"kmax_ready{L}"), 1)

            def q_rows(L):
                w = SLICE if L == 0 else DH
                for m in range(T):
                    dve.wait_ge(*count(f"q_ready{L}", m + 1))
                    ps = PS[:, m % 4, 0:HEADS * w].rearrange("p (h s) -> p h s", h=HEADS)
                    q = Q[:, m, 0:HEADS * w].rearrange("p (h s) -> p h s", h=HEADS)
                    step(dve.tensor_reduce(qm[:, m, :], ps, AX_X, ALU.max))
                    settle()
                    dve.tensor_tensor(q, ps, qm[:, m, :].unsqueeze(2).to_broadcast([P, HEADS, w]), ALU.subtract
                                      ).then_inc(S(f"q_shifted{L}"), 1)
                    dve.wait_ge(*count(f"q_shifted{L}", m + 1))
                    dve.engine_nop().then_inc(S(f"q_done{L}"), 1)

            def q_soft(L):
                w = SLICE if L == 0 else DH
                for m in range(T):
                    q = Q[:, m, 0:HEADS * w].rearrange("p (h s) -> p h s", h=HEADS)
                    dve.wait_ge(*count(f"q_exp{L}", m + 1))
                    step(dve.tensor_reduce(qs[:, m, :], q, AX_X, ALU.add))
                    settle()
                    step(dve.reciprocal(qr[:, m, :], qs[:, m, :]))
                    settle()
                    dve.tensor_tensor(q, q, qr[:, m, :].unsqueeze(2).to_broadcast([P, HEADS, w]), ALU.mult
                                      ).then_inc(S(f"q_soft{L}"), 1)

            def contexts(L):
                groups, hpg, w = (2, 4, SLICE) if L == 0 else (K, 2, DH)
                dve.wait_ge(*count(f"k_exp{L}", groups))
                step(dve.reciprocal(krec[:, 0:groups], ksum[:, 0:groups]))
                settle()
                for g in range(groups):
                    dve.wait_ge(*count(f"kv_ready{L}", g + 1))
                    for h in range(hpg):
                        r = slice(h * w, (h + 1) * w)
                        ins = dve.tensor_scalar(KV[r, g * (D // groups) + h * DH:g * (D // groups) + (h + 1) * DH], PS[r, g, h * DH:(h + 1) * DH],
                                                krec[r, g:g + 1], None, ALU.mult)
                        if h < hpg - 1:
                            step(ins)
                    settle()
                    ins.then_inc(S(f"kv_done{L}"), 1)

            step(dve.memset(KV[:, :], 0.0))
            settle()
            for g in range(2):
                dve.wait_ge(*count("k_done0", 2 * g + 2))
                key_max(0, g)
            q_rows(0)
            q_soft(0)
            contexts(0)
            norm(1, lambda m: add_mix(0, m))

            def router_softmax(n):
                w = (E0, E1)[n]
                pr = PR[:, :, 0:w]
                dve.wait_ge(*count(f"logit_ready{n}", 1))
                ps = PS[:, 7, 0:T * w].rearrange("p (t e) -> p t e", t=T)
                if n == 1:
                    step(dve.tensor_tensor(pr, ps, BG[:, :].unsqueeze(1).to_broadcast([P, T, w]), ALU.add))
                    settle()
                    ps = pr
                step(dve.tensor_reduce(pm[:, :], ps, AX_X, ALU.max))
                settle()
                dve.tensor_tensor(pr, ps, pm[:, :].unsqueeze(2).to_broadcast([P, T, w]), ALU.subtract
                                  ).then_inc(S(f"logit_shifted{n}"), 1)
                dve.wait_ge(*count(f"logit_exp{n}", 1))
                step(dve.tensor_reduce(psm[:, :], pr, AX_X, ALU.add))
                settle()
                step(dve.reciprocal(pr_[:, :], psm[:, :]))
                settle()
                dve.tensor_tensor(pr, pr, pr_[:, :].unsqueeze(2).to_broadcast([P, T, w]), ALU.mult
                                  ).then_inc(S(f"probs_ready{n}"), 1)

            router_softmax(0)
            dve.wait_ge(*count("pT_ready", 1))
            both = PS[0:E0, 0:2, :].rearrange("p a b -> p (a b)")
            step(dve.tensor_copy(PT, both))
            step(dve.tensor_copy(PTW, both))
            settle()
            for r in range(CAP // 8):
                s8 = sc0[:, r * 8:(r + 1) * 8]
                step(dve.max(s8, PTW))
                settle()
                step(dve.max_index(ix0[:, r * 8:(r + 1) * 8], s8, PTW))
                settle()
                step(dve.match_replace(PTW, s8, PTW, -1.0))
                settle()
            step(dve.tensor_scalar(PTW, PTW, 0.0, None, ALU.is_lt))
            dve.tensor_copy(ixf0[:, :], ix0[:, :]).then_inc(S("top_ready"), 1)
            settle()
            dve.tensor_tensor(PTW, PTW, PT, ALU.mult).then_inc(S("top_ready"), 1)
            dve.wait_ge(*count("scT_ready", 1))
            step(dve.tensor_copy(scT[:, :], PS[0:CAP, 0, 0:2 * E0]))
            settle()
            dve.tensor_copy(ic0[:, :], scT[:, 0:E0]).then_inc(S("ic0_ready"), 1)
            dve.engine_nop().then_inc(S("scT_done"), 1)
            dve.wait_ge(*count("shared_added", T))
            for m in range(T):
                dve.wait_ge(*count("rb_ready0", m + 1))
                dve.tensor_tensor(X[:, m, :], X[:, m, :], PS[:, 4 + m % 4, :], ALU.add).then_inc(S("rb_done0"), 1)

            def expert_out(L, i, u, first):
                e = U * i + u
                dve.wait_ge(*count(f"ey_ready{L}", e + 1))
                if L == 0:
                    if not (first and u < 2):
                        dve.wait_ge(*count(f"scattered{u % 2}", 16 * (U // 2 * i + u // 2)))
                    dve.tensor_scalar(Y0[u % 2], PS[0:CAP, 4 + u % 2, :], scT[:, ds(e + E0, 1)], None, ALU.mult
                                      ).then_inc(S("ey_done0"), 1)
                else:
                    if not first:
                        dve.wait_ge(*count(f"y1_out{u}", 16 * i))
                    dve.tensor_copy(Y1[u], PS[0:C, 4 + u % 2, :]).then_inc(S("ey_done1"), 1)

            for u in range(U):
                expert_out(0, 0, u, True)
            with dve.Fori(1, E0 // U) as i:
                for u in range(U):
                    expert_out(0, i, u, False)

            norm(2, add_routed)
            for m in range(T):
                dve.wait_ge(*count("h1_rounded", m + 1))
                dve.tensor_tensor(H_lo[:, m, :], PS[:, 4 + m % 4, :], H_hi[:, m, :].bitcast(F32), ALU.subtract
                                  ).then_inc(S("h_done1"), 1)
            for m in range(T):
                dve.wait_ge(*count("gnn_ready1", m + 1))
                dve.wait_ge(*count("x_biased2", m + 1))
                dve.scalar_tensor_tensor(X[:, m, :], PS[:, m % 4, :], rcnt[:, m:m + 1], X[:, m, :],
                                         ALU.mult, ALU.add).then_inc(S("gnn_done1"), 1)
            dve.wait_ge(*count("xT_done2", T))
            for i in range(2 * K):
                dve.wait_ge(*count("k_ready1", i + 1))
                k = KTr[:, i // 2, (i % 2) * 512:(i % 2 + 1) * 512]
                dve.tensor_scalar(k, PS[:, i % 4, :], 0.0, None, ALU.min).then_inc(S("k_low"), 1)
                dve.wait_ge(*count("k_elu", i + 1))
                dve.scalar_tensor_tensor(k, PS[:, i % 4, :], 0.0, k, ALU.max, ALU.add).then_inc(S("k_done1"), 1)
            dve.wait_ge(*count("k_done1", 2 * K))
            for g in range(K):
                key_max(1, g)
            q_rows(1)
            q_soft(1)
            step(dve.memset(KV[:, :], 0.0))
            settle()
            contexts(1)
            norm(3, lambda m: add_mix(1, m))
            router_softmax(1)
            dve.wait_ge(*count("probs_ready1", 1))
            for t in range(T):
                step(dve.max(top8[:, t, :], PR[:, t, :]))
            settle()
            for t in range(T):
                step(dve.max_index(ti8[:, t, :], top8[:, t, :], PR[:, t, :]))
            settle()
            step(dve.tensor_copy(tif[:, :, :], ti8[:, :, 0:2]))
            settle()
            for t in range(T):
                step(dve.tensor_scalar(O1[:, t, :], iota_e[:, :], tif[:, t, 0:1], None, ALU.is_equal))
                step(dve.tensor_scalar(O2[:, t, :], iota_e[:, :], tif[:, t, 1:2], None, ALU.is_equal))
            settle()
            dve.tensor_tensor(MB, O1, O2, ALU.add).then_inc(S("mb_ready"), 1)
            for t in range(T):
                step(dve.tensor_scalar(SWW[:, t, :], O1[:, t, :], top8[:, t, 0:1], None, ALU.mult))
            settle()
            for t in range(T):
                ins = dve.scalar_tensor_tensor(SWW[:, t, :], O2[:, t, :], top8[:, t, 1:2], SWW[:, t, :],
                                               ALU.mult, ALU.add)
                if t < T - 1:
                    step(ins)
            settle()
            ins.then_inc(S("sww_ready"), 1)
            dve.wait_ge(*count("place_ready", 1))
            step(dve.tensor_tensor(more, PS[:, 2, 0:E1].unsqueeze(2).to_broadcast([P, E1, NC]),
                                   limits[:, :].unsqueeze(1).to_broadcast([P, E1, NC]), ALU.is_gt))
            step(dve.memset(cntb[:, 5, :], 0.0))
            settle()
            step(dve.tensor_reduce(cntb[:, 1, :], more, AX_X, ALU.add))
            settle()
            step(dve.tensor_tensor_scan(cntb[:, 2, :], cntb[:, 1, :], cntb[:, 5, :], 0.0, ALU.add, ALU.add))
            settle()
            step(dve.tensor_tensor(cntb[:, 3, :], cntb[:, 2, :], cntb[:, 1, :], ALU.subtract))
            step(dve.tensor_scalar(cntb[:, 0, :], cntb[:, 2, :], pcol[:, 0:1], None, ALU.is_le))
            settle()
            dve.tensor_reduce(ecol[:, :], cntb[:, 0, :], AX_X, ALU.add).then_inc(S("ecol_ready"), 1)
            step(dve.tensor_scalar(trow[:, P:P + 1], cntb[0:1, 2, E1 - 1:E1], float(U - 1), None, ALU.add))
            settle()
            step(dve.tensor_copy(trow_i[:, P + 1:P + 2], trow[:, P:P + 1]))
            settle()
            dve.tensor_scalar(trow_i[:, P:P + 1], trow_i[:, P + 1:P + 2], U.bit_length() - 1, None,
                              ALU.logical_shift_right).then_inc(S("table_ready"), 1)
            step(dve.tensor_scalar(trow_i[:, P + 1:P + 2], trow_i[:, P + 1:P + 2], -float(U), None, ALU.add))
            settle()
            dve.tensor_scalar(trow_i[:, P + 2:P + 3], trow_i[:, P + 1:P + 2], U.bit_length() - 1, None,
                              ALU.logical_shift_right).then_inc(S("table_ready"), 1)
            for c, o in enumerate((O1, O2)):
                step(dve.tensor_tensor(SL, PS[:, 1, :].rearrange("p (t e) -> p t e", t=T), o, ALU.mult))
                step(dve.tensor_tensor(SLT, cntb[:, 3, :].unsqueeze(1).to_broadcast([P, T, E1]), o, ALU.mult))
                settle()
                step(dve.tensor_reduce(at[:, 0, c * T:(c + 1) * T], SL, AX_X, ALU.add))
                step(dve.tensor_reduce(at[:, 1, c * T:(c + 1) * T], SLT, AX_X, ALU.add))
                settle()
            step(dve.tensor_tensor(place_ge, at[:, 0, :].unsqueeze(2).to_broadcast([P, 2 * T, NC]),
                                   limits[:, :].unsqueeze(1).to_broadcast([P, 2 * T, NC]), ALU.is_ge))
            settle()
            step(dve.tensor_reduce(at[:, 2, :], place_ge, AX_X, ALU.add))
            settle()
            step(dve.scalar_tensor_tensor(at[:, 3, :], at[:, 2, :], -1.0, at[:, 1, :], ALU.add, ALU.add))
            step(dve.tensor_scalar(at[:, 5, :], at[:, 2, :], float(-C), float(C), ALU.mult, ALU.add))
            settle()
            step(dve.tensor_tensor(at[:, 4, :], at[:, 0, :], at[:, 5, :], ALU.add))
            settle()
            for a in range(2 * T):
                step(dve.tensor_scalar(lane_hot[:, a, :], iota_h[:, 0:C], at[:, 4, a:a + 1], None, ALU.is_equal))
                step(dve.tensor_scalar(tile_hot[:, a, :], iota_h[:, 0:MAXT], at[:, 3, a:a + 1], ids[:, a:a + 1],
                                       ALU.is_equal, ALU.mult))
            settle()
            dve.engine_nop().then_inc(S("hot_ready"), 1)
            dve.wait_ge(*count("erow_ready", 1))
            step(dve.tensor_scalar(trow[:, 0:P], PS[0:1, 3, 0:P], float(E1 - 1), None, ALU.min))
            settle()
            dve.tensor_copy(trow_i[:, 0:P], trow[:, 0:P]).then_inc(S("table_ready"), 1)
            dve.wait_ge(*count("rows_summed", 1))
            step(dve.tensor_scalar(rows[:, 0, :], PS[0:C, 0, 0:MAXT], 0.0, float(8 * N), ALU.is_equal, ALU.mult))
            settle()
            step(dve.scalar_tensor_tensor(rows[:, 1, :], PS[0:C, 0, 0:MAXT], -1.0, rows[:, 0, :], ALU.add, ALU.add))
            settle()
            step(dve.tensor_scalar(rows[:, 2, :], rows[:, 1, :], float(N), float(-N), ALU.is_ge, ALU.mult))
            settle()
            step(dve.tensor_tensor(rows[:, 0, :], rows[:, 1, :], rows[:, 2, :], ALU.add))
            settle()
            dve.tensor_copy(rows_i[:, 0, :], rows[:, 0, :]).then_inc(S("rows_ready"), 1)
            dve.tensor_copy(rows_i[:, 1, :], rows[:, 1, :]).then_inc(S("outs_ready"), 1)
            dve.wait_ge(*count("tok_out", 32))
            for m in range(T):
                dve.wait_ge(*count("rb_done1", m + 1))
                step(dve.tensor_tensor(XN[:, m, :], XN[:, m, :], RB[:, m, :], ALU.add))
            turns = dve.value_load(trow_i[0:1, P:P + 1], min_val=3, max_val=MAXT // U)
            for u in range(U):
                expert_out(1, 0, u, True)
            with dve.Fori(1, turns) as i:
                for u in range(U):
                    expert_out(1, i, u, False)
            settle()
            def result(m):
                inverse_root(4, m)
                dve.scalar_tensor_tensor(X[:, m, :], XN[:, m, :], rs[:, m:m + 1], X[:, m, :], ALU.mult, ALU.add
                                         ).then_inc(S("out_ready"), 1)

            for m in range(T):
                dve.wait_ge(*count(f"yg_in{m}", 16))
                for c in range(2):
                    step(dve.scalar_tensor_tensor(XN[:, m, :], YG[m][:, c, :], top8[:, m, c:c + 1], XN[:, m, :],
                                                  ALU.mult, ALU.add))
                    settle()
                stats(4, m, XN)
                dve.wait_ge(*count("var_ready4", m + 1))
                step(dve.scalar_tensor_tensor(XN[:, m, :], XN[:, m, :], mv[:, m, 0:1], BC[:, 0, :],
                                              ALU.subtract, ALU.mult))
                if m == 0:
                    dve.wait_ge(*count("x_biased3", T))
                settle()
                result(m)


_INS = ['x', 'src', 'dst', 'L0_gnn_W', 'L0_gnn_b', 'L0_mix_W_in', 'L0_mix_b_in', 'L0_mix_Wq', 'L0_mix_Wk',
        'L0_mix_Wv', 'L0_mix_W_out', 'L0_mix_b_out', 'L0_ffn_gate_w', 'L0_ffn_w1', 'L0_ffn_b1', 'L0_ffn_w2',
        'L0_ffn_b2', 'L0_ffn_sw1', 'L0_ffn_sb1', 'L0_ffn_sw2', 'L0_ffn_sb2', 'L1_gnn_wc', 'L1_gnn_wn',
        'L1_gnn_bias', 'L1_mix_w_qkv', 'L1_mix_w_proj', 'L1_mix_b_proj', 'L1_ffn_Wg', 'L1_ffn_bg', 'L1_ffn_W1',
        'L1_ffn_b1', 'L1_ffn_W2', 'L1_ffn_b2', 'L1_ffn_gamma', 'L1_ffn_beta']


def kernel(**inputs):
    import numpy as _np
    import concourse.bacc as _bacc
    from concourse import mybir as _mybir
    from concourse.bass_utils import run_bass_kernel_spmd as _run

    nc = _bacc.Bacc("TRN2", target_bir_lowering=False, num_devices=1)
    arrays, aps = {}, {}
    for name in _INS:
        a = _np.ascontiguousarray(inputs[name])
        arrays[f"in_{name}_dram"] = a
        aps[name] = nc.dram_tensor(f"in_{name}_dram", a.shape, _mybir.dt.from_np(a.dtype), kind="ExternalInput").ap()
    out = nc.dram_tensor("out_0_dram", (N, D), _mybir.dt.float32, kind="ExternalOutput").ap()
    build(nc, aps, out)
    r = _run(nc, [arrays], core_ids=[0])
    return r.results[0]["out_0_dram"]
```

```python
from contextlib import ExitStack

import concourse.bass as bass
from concourse import mybir

ALU = mybir.AluOpType
ACT = mybir.ActivationFunctionType
AX_X = mybir.AxisListType.X
F32 = mybir.dt.float32
F32R = mybir.dt.float32r
F16 = mybir.dt.float16
BF16 = mybir.dt.bfloat16
I32 = mybir.dt.int32
U32 = mybir.dt.uint32
RMAX = bass.bass_isa.ReduceOp.max
ds = bass.ds

P = 128
N = 1024
D = 512
NE = 16384
T = N // P
K = D // P
HEADS = 8
DH = D // HEADS
SLICE = 32
GRP = 4 * P
NG = NE // GRP
SHIFT = NG * T
HID = 256
HJ = HID // P
E0 = 16
CAP = N // E0
E1 = 64
C = 80
NC = -(-N // C)
U = 4
MAXT = E1 + (2 * N - E1) // C + U
MAXT -= MAXT % U
EPS = 1e-5
EXACT = 2048


def build(nc, A, out):
    with ExitStack() as ctx:
        def sb(name, shape, dt=F32):
            return ctx.enter_context(nc.sbuf_tensor(name, shape, dt))

        def rounded(name, shape):
            return nc.alloc_sbuf_tensor_at(name, shape, F32R, offset=-(-nc.sbuf_base // 32) * 32)

        norms = dict(var_ready=T, sd_ready=T, xn_ready=T, xT_ready=T, xT_done=T, x_biased=T)
        layers = dict(h_ready=T, h_done=T, gnn_ready=T, gnn_done=T, k_ready=4, k_done=4, v_ready=T, v_done=T,
                      q_ready=T, q_done=T, q_shifted=T, q_exp=T, q_soft=T, kmax_ready=2, k_exp=2, kr_ready=4,
                      kr_done=4, qT_ready=4, qT_done=4, kv_ready=2, kv_done=2, oT_ready=2 * K, oT_done=2 * K,
                      oT_rounded=2 * K,
                      mix_ready=T, mix_done=T, logit_ready=1, logit_shifted=1, logit_exp=1, probs_ready=1,
                      rb_ready=T, rb_done=T, eT_ready=E0, eT_done=E0, eh_ready=E0, eh_done=E0, ey_ready=E0,
                      ey_done=E0, h_rounded=T, rows_added=T, rows_scaled=T, icur_set=E0, iout_set=E0)
        rings = {}
        for u in range(U):
            rings[f"ew{u}_in"], rings[f"g{u}_in"] = 32 * (E0 // U), 16 * (E0 // U)
        adds = {**norms, **layers, **rings}
        sems = {}

        def S(name):
            name = name[:-1] if name[:-1] in adds else name
            if name not in sems:
                sems[name] = ctx.enter_context(nc.semaphore(name))
            return sems[name]

        def count(name, n):
            return S(name), n + (adds[name[:-1]] * int(name[-1]) if name[:-1] in adds else 0)

        toks = [nc.dram_tensor(f"tok{L}_scratch", (N, D), F32).ap() for L in range(2)]
        accs = [nc.dram_tensor(f"acc{b}_scratch", (N, D), F32).ap() for b in range(2)]
        chosen_d = nc.dram_tensor("chosen_scratch", (2 * N, D), F32).ap()

        X = sb("X", [P, T, D])
        XT_hi = rounded("XT_hi", [P, K, N])
        XN = sb("XN", [P, T, D])
        XT_lo = rounded("XT_lo", [P, K, N])
        XT = sb("XT", [P, K, N])
        H_lo = rounded("H_lo", [P, T, D])
        H = sb("H", [P, T, D])
        W_hi = rounded("W_hi", [P, 4, K, D])
        CT = sb("CT", [P, T, N])
        AT = rounded("AT", [P, T, N])
        later = sb("later", [P, T * N])
        H_hi = rounded("H_hi", [P, T, D])
        B1 = sb("B1", [P, 4096])
        W_lo = rounded("W_lo", [P, 4, K, D])
        W = sb("W", [P, 4, K, D])
        BC = sb("BC", [P, 5, D])
        BG = sb("BG", [P, E1])

        ident = sb("ident", [P, P])
        onescol = sb("onescol", [P, 1])
        ones_r = sb("ones_r", [P, 2], F32R)
        ones_b = sb("ones_b", [P, P], BF16)
        tri_b = sb("tri_b", [P, P], BF16)
        zero_f = sb("zero_f", [P, D])
        zero_b = zero_f[:, 0:D // 2].bitcast(BF16)
        iota_h = sb("iota_h", [P, N], F16)
        iota_e = sb("iota_e", [P, E1])
        pcol_i = sb("pcol_i", [P, 1], I32)
        pcol = sb("pcol", [P, 1])
        epsc = sb("epsc", [P, 1])

        edge_c = sb("edge_c", [P, 2, P])
        ends = sb("ends", [P, 4])
        gmm = sb("gmm", [NG, 2])
        gov = sb("gov", [NG, 5, T])
        gval = sb("gval", [NG, 2 * T])
        gred = sb("gred", [NG, 2 * T])
        grow = sb("grow", [1, 6, T])
        grow_i = sb("grow_i", [1, 2, T], I32)

        cols_sm = sb("cols_sm", [P, 256])
        BDQ = sb("BDQ", [P, 2 * SLICE])
        BDK = sb("BDK", [P, 2 * SLICE])
        BDV = sb("BDV", [P, 2 * DH])
        GW = sb("GW", [P, K, E0 + E1])
        B2R0 = sb("B2R0", [E0, D])

        st = sb("st", [P, T, 6])
        mv = sb("mv", [P, T, 2])
        sd = sb("sd", [P, T])
        rs = sb("rs", [P, T])
        deg = sb("deg", [P, T])
        dinv = sb("dinv", [P, T])
        most = sb("most", [P, 2])
        most_i = sb("most_i", [1, 1], I32)
        rcnt = sb("rcnt", [P, T])
        kmax = sb("kmax", [P, K])
        ksum = sb("ksum", [P, K])
        krec = sb("krec", [P, K])
        qm = sb("qm", [P, T, HEADS])
        qs = sb("qs", [P, T, HEADS])
        qr = sb("qr", [P, T, HEADS])
        KV = sb("KV", [P, D])

        PR = sb("PR", [P, T, E1])
        pm = sb("pm", [P, T])
        psm = sb("psm", [P, T])
        pr_ = sb("pr_", [P, T])
        sc0 = sb("sc0", [E0, CAP])
        ix0 = sb("ix0", [E0, CAP], U32)
        ixf0 = sb("ixf0", [E0, CAP])
        scT = sb("scT", [CAP, 2 * E0])
        ic0 = sb("ic0", [CAP, E0], I32)
        icur = sb("icur", [P, U], I32)
        iout = sb("iout", [P, U], I32)
        top8 = sb("top8", [P, T, 8])
        ti8 = sb("ti8", [P, T, 8], U32)
        tif = sb("tif", [P, T, 2])
        at = sb("at", [P, 6, 2 * T])
        ids_i = sb("ids_i", [P, 2 * T], I32)
        ids = sb("ids", [P, 2 * T])
        rows_i = sb("rows_i", [C, 2, MAXT], I32)
        limits = sb("limits", [P, NC])
        ecol = sb("ecol", [P, 1])
        trow_i = sb("trow_i", [1, P + 3], I32)

        PS = ctx.enter_context(nc.psum_tensor("PS", [P, 8, 512], F32))

        early = H[:, :, :].rearrange("p a b -> p (a b)")
        iota_i = early[:, 0:N].bitcast(I32)
        edge_i = early[:, N:N + 2 * P].bitcast(I32).rearrange("p (a b) -> p a b", a=2)
        edge_f = early[:, N + 2 * P:N + 4 * P].rearrange("p (a b) -> p a b", a=2)
        dgrp_i = early[0:NG, 2048:2048 + GRP].bitcast(I32)
        rows_sm = early[0:E1, 3072:3584].rearrange("p (a b) -> p a b", a=2)
        ATf = later[:, :]
        CTf = CT[:, :, :].rearrange("p a b -> p (a b)")
        Hf = H[:, :, :].rearrange("p a b -> p (a b)")
        XNf = XN[:, :, :].rearrange("p a b -> p (a b)")
        OT_hi = H_hi[:, :, :].rearrange("p a b -> p (a b)").rearrange("p (c n) -> p c n", c=K)
        OT_lo = AT[:, :, :].rearrange("p a b -> p (a b)")[:, 4096:8192].rearrange("p (c n) -> p c n", c=K)
        splits = (("w1_in", 16, 1, W_lo[:, 3]), ("w2_in", 16, 2, W_lo[:, 3]), ("wk_in", 16, 0, W_hi[:, 0]),
                  ("w1_in", 32, 1, W_hi[:, 1]), ("w2_in", 32, 2, W_hi[:, 2]), ("w3_in", 32, 3, W_hi[:, 3]),
                  ("w1_in", 48, 1, W_hi[:, 1]))
        WIN, WOUT, WK, WQ, WV, WC, WPROJ = range(7)
        normed = (XN, XN, XN, H)
        onehot_s = B1[:, 0:2048].bitcast(BF16).rearrange("p (j n) -> p j n", j=4)
        onehot_d = B1[:, 2048:2304].bitcast(BF16).rearrange("p (j n) -> p j n", j=4)
        away = B1[:, 2304:2560].bitcast(BF16).rearrange("p (j n) -> p j n", j=4)
        minus_dst = B1[:, 2560:2564]
        XM = ATf[:, 0:4096].rearrange("p (c n) -> p c n", c=K)
        V = ATf[:, 4096:8192].rearrange("p (t n) -> p t n", t=T)
        Q = B1[:, :].rearrange("p (t n) -> p t n", t=T)
        KTrs = [f.rearrange("p (c n) -> p c n", c=K) for f in
                (XN[:, :, :].rearrange("p a b -> p (a b)"), ATf[:, 0:4096])]
        KR = H
        SHT = B1[:, 0:2048].rearrange("p (j n) -> p j n", j=HJ)
        PT = B1[0:E0, 2048:3072]
        PTW = B1[0:E0, 3072:4096]
        O1 = CTf[:, 0:512].rearrange("p (t e) -> p t e", t=T)
        O2 = CTf[:, 512:1024].rearrange("p (t e) -> p t e", t=T)
        MB = CTf[:, 1024:1280].bitcast(BF16).rearrange("p (t e) -> p t e", t=T)
        SWW = CTf[:, 1280:1792].rearrange("p (t e) -> p t e", t=T)
        SL = CTf[:, 1792:2304].rearrange("p (t e) -> p t e", t=T)
        SLT = CTf[:, 2304:2816].rearrange("p (t e) -> p t e", t=T)
        SWT = CTf[0:E1, 2816:3840]
        more = XNf[:, 0:E1 * NC].rearrange("p (e c) -> p e c", e=E1)
        cntb = CTf[:, 6144:6144 + 6 * E1].rearrange("p (a e) -> p a e", e=E1)
        B2R1 = CTf[0:E1, 6656:6656 + D]
        trow = CTf[0:1, 7168:7168 + P + 1]
        EW = [ATf[:, u * 2048:(u + 1) * 2048] for u in range(U)]
        EW1 = [w[:, 0:1024].rearrange("p (k n) -> p k n", k=K) for w in EW]
        EW2 = [w[:, 1024:2048].rearrange("p (j n) -> p j n", j=HJ) for w in EW]

        def expert_space(f, n):
            g = [f[0:n, u * D:(u + 1) * D] for u in range(U)]
            at = U * D
            gt = [f[:, at + b * K * n:at + (b + 1) * K * n].rearrange("p (k n) -> p k n", k=K) for b in range(2)]
            at += 2 * K * n
            ht = [f[:, at + b * HJ * n:at + (b + 1) * HJ * n].rearrange("p (j n) -> p j n", j=HJ) for b in range(2)]
            return g, gt, ht

        G0, GT0, HT0 = expert_space(Hf, CAP)
        Y0 = [Hf[0:CAP, 2816 + b * D:2816 + (b + 1) * D] for b in range(2)]
        G1, GT1, HT1 = expert_space(XNf, C)
        Y1 = [B1[0:C, u * D:(u + 1) * D] for u in range(U)]
        YG = [CTf[:, m * 2 * D:(m + 1) * 2 * D].rearrange("p (c n) -> p c n", c=2) for m in range(T)]
        rows = CTf[0:C, 7424:7424 + 3 * MAXT].rearrange("p (a e) -> p a e", e=MAXT)
        place_ge = XNf[:, 1024:1024 + 2 * T * NC].rearrange("p (a c) -> p a c", a=2 * T)
        RB = XT[:, :, :].rearrange("p a b -> p (a b)").rearrange("p (t n) -> p t n", t=T)
        lane_hot = XNf[:, 2048:4096].rearrange("p (a n) -> p a n", a=2 * T)[:, :, 0:C]
        tile_hot = CTf[:, 4096:4096 + 2 * T * MAXT].rearrange("p (a n) -> p a n", a=2 * T)

        def norm_banks(n):
            return (4, 5, 6) if n % 2 else (0, 1, 2, 3)

        wv = lambda ap: ap.rearrange("(k p) n -> p k n", p=P)
        block = ctx.enter_context(nc.Block())

        @block.sync
        def _(sp):
            def rows2(dram, q):
                return dram.rearrange("(t p) d -> p t d", p=P)[:, 2 * q:2 * q + 2, :]

            for q in range(T // 2):
                sp.dma_start(X[:, 2 * q:2 * q + 2, :], rows2(A["x"], q)).then_inc(S(f"x_in{q}"), 16)
            for i, n in enumerate(("src", "dst")):
                sp.dma_start(edge_i[:, i, :], A[n].rearrange("(c e) -> c e", e=P)).then_inc(S("edges_in"), 16)
            sp.dma_start(dgrp_i[:, :], A["dst"].rearrange("(g e) -> g e", e=GRP)).then_inc(S("edges_in"), 16)
            sp.dma_start(W[:, 0], wv(A["L0_gnn_W"])).then_inc(S("gnnw_in"), 16)
            for b, n, e in ((0, "L0_ffn_b1", E0), (1, "L1_ffn_b1", E1)):
                sp.dma_start(rows_sm[0:e, b, :], A[n]).then_inc(S("small_in"), 16)
            sp.dma_start(W[:, 1], wv(A["L0_mix_W_in"])).then_inc(S("w1_in"), 16)
            for n, at in (("L0_gnn_b", 0), ("L0_mix_b_out", 1), ("L0_ffn_sb2", 2), ("L1_gnn_bias", 3),
                          ("L1_mix_b_proj", 4)):
                sp.dma_start(BC[:, at, :], A[n].partition_broadcast(P)).then_inc(S("bias_in"), 16)
            sp.dma_start(BG[:, :], A["L1_ffn_bg"].partition_broadcast(P)).then_inc(S("bias_in"), 16)
            sp.dma_start(cols_sm[:, 192:196], A["L0_mix_b_in"].rearrange("(c p) -> p c", p=P),
                         allow_slow_non_contiguous=True).then_inc(S("bias_in"), 16)
            sp.dma_start(cols_sm[:, 196:198], A["L0_ffn_sb1"].rearrange("(c p) -> p c", p=P),
                         allow_slow_non_contiguous=True).then_inc(S("bias_in"), 16)
            sp.wait_ge(*count("bd_zero", 3))
            for h in range(2):
                r = slice(h * DH, (h + 1) * DH)
                sp.dma_start(BDQ[r, h * SLICE:(h + 1) * SLICE], A["L0_mix_Wq"]).then_inc(S("bd_in"), 16)
                sp.dma_start(BDK[r, h * SLICE:(h + 1) * SLICE], A["L0_mix_Wk"]).then_inc(S("bd_in"), 16)
                sp.dma_start(BDV[r, h * DH:(h + 1) * DH], A["L0_mix_Wv"]).then_inc(S("bd_in"), 16)
            sp.dma_start(W[:, 2], wv(A["L0_mix_W_out"])).then_inc(S("w2_in"), 16)
            sp.dma_start(GW[:, :, 0:E0], wv(A["L0_ffn_gate_w"])).then_inc(S("gate_in"), 16)
            sp.dma_start(GW[:, :, E0:], wv(A["L1_ffn_Wg"])).then_inc(S("gate_in"), 16)
            sp.dma_start(B2R0[:, :], A["L0_ffn_b2"]).then_inc(S("gate_in"), 16)
            sp.wait_ge(*count("zeros_ready", 1))
            sp.dma_start(accs[1].rearrange("(t p) d -> p t d", p=P),
                         zero_f[:, :].unsqueeze(1).to_broadcast([P, T, D])).then_inc(S("acc_out"), 16)
            sp.wait_ge(*count("wT_ready", K))
            sp.dma_start(W[:, 0, 0:2, :].rearrange("p a b -> p (a b)").rearrange("p (k n) -> p k n", k=K),
                         wv(A["L0_ffn_sw1"])).then_inc(S("shared_in"), 16)
            sp.dma_start(W[:, 0, 2:4, :], wv(A["L0_ffn_sw2"])).then_inc(S("shared_in"), 16)
            qkv = A["L1_mix_w_qkv"].rearrange("(k p) n -> p k n", p=P)
            sp.wait_ge(*count("xm_ready", 2 * K))
            sp.dma_start(W[:, 1], qkv[:, :, 0:D]).then_inc(S("w1_in"), 16)
            sp.wait_ge(*count("mix_ready0", T))
            sp.dma_start(W[:, 3], wv(A["L1_gnn_wn"])).then_inc(S("w3_in"), 16)
            sp.dma_start(W[:, 2], qkv[:, :, 2 * D:3 * D]).then_inc(S("w2_in"), 16)

            sp.wait_ge(*count("xn_ready1", T))
            sp.dma_start(toks[0].rearrange("(t p) d -> p t d", p=P), XN[:, :, :]).then_inc(S("tok_out"), 16)

            def load0(i, u):
                e = U * i + u
                sp.dma_start(EW1[u], A["L0_ffn_w1"][ds(e, 1)].rearrange("a (k p) n -> p (a k) n", p=P)
                             ).then_inc(S(f"ew{u}_in0"), 16)
                sp.dma_start(EW2[u], A["L0_ffn_w2"][ds(e, 1)].rearrange("a (k p) n -> p (a k) n", p=P)
                             ).then_inc(S(f"ew{u}_in0"), 16)

            for u in range(U):
                load0(0, u)
            sp.wait_ge(*count("rb_done0", T))
            sp.dma_start(accs[0].rearrange("(t p) d -> p t d", p=P), X[:, :, :]).then_inc(S("acc_out"), 16)
            with sp.Fori(1, E0 // U) as i:
                for u in range(U):
                    sp.wait_ge(*count("ey_ready0", U * i + (u + 1 - U)))
                    load0(i, u)
            for b in range(2):
                sp.wait_ge(*count(f"scattered{b}", 16 * E0 // 2))
            for q in range(T // 2):
                for b, dst in enumerate((X, XN)):
                    sp.dma_start(dst[:, 2 * q:2 * q + 2, :], rows2(accs[b], q)).then_inc(S(f"x_in{q}"), 16)
            sp.wait_ge(*count("shared_ready", T))
            sp.dma_start(W[:, 0], qkv[:, :, D:2 * D]).then_inc(S("wk_in"), 16)
            sp.wait_ge(*count("h_ready1", T))
            sp.dma_start(W[:, 3], wv(A["L1_gnn_wc"])).then_inc(S("w3_in"), 16)
            sp.wait_ge(*count("q_ready1", T))
            sp.dma_start(W[:, 1], wv(A["L1_mix_w_proj"])).then_inc(S("w1_in"), 16)

            sp.wait_ge(*count("mix_ready1", T))
            sp.dma_start(B2R1, A["L1_ffn_b2"]).then_inc(S("late_in"), 16)
            sp.dma_start(BC[:, 0, :], A["L1_ffn_gamma"].partition_broadcast(P)).then_inc(S("late_in"), 16)
            sp.dma_start(BC[:, 1, :], A["L1_ffn_beta"].partition_broadcast(P)).then_inc(S("late_in"), 16)

            sp.wait_ge(*count("xn_ready3", T))
            sp.dma_start(toks[1].rearrange("(t p) d -> p t d", p=P), H[:, :, :]).then_inc(S("tok_out"), 16)
            sp.wait_ge(*count("table_ready", 3))
            turns = sp.value_load(trow_i[0:1, P:P + 1], min_val=3, max_val=MAXT // U)

            def load1(i, u):
                e = sp.value_load(trow_i[0:1, ds(U * i + u, 1)], min_val=0, max_val=E1 - 1)
                sp.dma_start(EW1[u], A["L1_ffn_W1"][ds(e, 1)].rearrange("a (k p) n -> p (a k) n", p=P)
                             ).then_inc(S(f"ew{u}_in1"), 16)
                sp.dma_start(EW2[u], A["L1_ffn_W2"][ds(e, 1)].rearrange("a (k p) n -> p (a k) n", p=P)
                             ).then_inc(S(f"ew{u}_in1"), 16)

            sp.wait_ge(*count("mix_ready1", T))
            for u in range(U):
                load1(0, u)
            with sp.Fori(1, turns) as i:
                for u in range(U):
                    sp.wait_ge(*count("ey_ready1", U * i + (u + 1 - U)))
                    load1(i, u)
            for u in range(U):
                sp.wait_ge(*count(f"y1_out{u}", 16 * turns))
            for m in range(T):
                sp.dma_start(YG[m], chosen_d.rearrange("(c t p) d -> p t c d", c=2, p=P)[:, m]
                             ).then_inc(S(f"yg_in{m}"), 16)
            for q in range(T // 2):
                sp.wait_ge(*count("out_ready", 2 * (q + 1)))
                sp.dma_start(rows2(out, q), X[:, 2 * q:2 * q + 2, :]).then_inc(S("stored"), 16)
            sp.wait_ge(*count("stored", 16 * T // 2))

        @block.gpsimd
        def _(pool):
            pool.memset(ident[:, :], 0.0).then_inc(S("cst"), 1)
            pool.memset(zero_f[:, :], 0.0).then_inc(S("zeros_ready"), 1)
            pool.memset(BDQ[:, :], 0.0).then_inc(S("bd_zero"), 1)
            pool.memset(BDK[:, :], 0.0).then_inc(S("bd_zero"), 1)
            pool.memset(BDV[:, :], 0.0).then_inc(S("bd_zero"), 1)
            pool.memset(onescol[:, :], 1.0).then_inc(S("consts"), 1)
            pool.memset(ones_b[:, :], 1.0).then_inc(S("consts"), 1)
            pool.memset(tri_b[:, :], 1.0).then_inc(S("cst"), 1)
            pool.iota(iota_i[:, :], [[1, N]], base=0, channel_multiplier=0).then_inc(S("consts"), 1)
            pool.iota(ids_i[:, :], [[P, 2 * T]], base=1, channel_multiplier=1).then_inc(S("consts"), 1)
            pool.iota(pcol_i[:, :], [[0, 1]], base=0, channel_multiplier=1).then_inc(S("consts"), 1)
            pool.memset(epsc[:, :], EPS).then_inc(S("consts"), 1)
            pool.wait_ge(*count("cst", 2))
            pool.affine_select(out=ident[:, :], in_=ident[:, :], compare_op=ALU.not_equal, fill=1.0, base=0,
                               pattern=[[-1, P]], channel_multiplier=1).then_inc(S("consts"), 1)
            pool.affine_select(out=tri_b[:, :], in_=tri_b[:, :], compare_op=ALU.is_gt, fill=0.0, base=0,
                               pattern=[[1, P]], channel_multiplier=-1).then_inc(S("consts"), 1)
            pool.wait_ge(*count("gval_ready", 2))
            pool.partition_all_reduce(gred[:, :], gval[:, :], NG, RMAX).then_inc(S("gred_ready"), 1)

            def bias(n, row):
                for m in range(T):
                    pool.wait_ge(*count(f"xn_ready{n}", m + 1))
                    pool.tensor_tensor(X[:, m, :], X[:, m, :], BC[:, row, :], ALU.add).then_inc(S(f"x_biased{n}"), 1)

            pool.wait_ge(*count("bias_in", 16 * 8))
            bias(0, 1)
            pool.tensor_tensor(BC[:, 3, :], BC[:, 3, :], BC[:, 4, :], ALU.add).then_inc(S("biases_added"), 1)
            for m in range(T):
                pool.wait_ge(*count("h_done0", m + 1))
                pool.tensor_tensor(H[:, m, :], H[:, m, :], BC[:, 0, :], ALU.add).then_inc(S("h_biased"), 1)

            bias(1, 2)
            for m in range(T):
                pool.wait_ge(*count("x_biased1", m + 1))
                pool.wait_ge(*count("rows_scaled0", m + 1))
                pool.tensor_tensor(X[:, m, :], X[:, m, :], XN[:, m, :], ALU.add).then_inc(S("rows_added0"), 1)

            def gather0(i, u):
                e = U * i + u
                pool.tensor_copy(icur[0:CAP, u:u + 1], ic0[:, ds(e, 1)]).then_inc(S("icur_set0"), 1)
                pool.wait_ge(*count("icur_set0", e + 1))
                pool.sem_inc(S("pool_passed"))
                pool.indirect_dma_start(G0[u], None, toks[0], bass.IndirectOffsetOnAxis(ap=icur[0:CAP, u:u + 1], axis=0)
                                        ).then_inc(S(f"g{u}_in0"), 16)

            def scatter0(i, u):
                e = U * i + u
                b = u % 2
                pool.wait_ge(*count(f"scattered{b}", 16 * (U // 2 * i + u // 2)))
                pool.tensor_copy(iout[0:CAP, u:u + 1], ic0[:, ds(e, 1)]).then_inc(S("iout_set0"), 1)
                pool.wait_ge(*count("iout_set0", e + 1))
                pool.wait_ge(*count("ey_done0", e + 1))
                pool.sem_inc(S("pool_passed"))
                pool.indirect_dma_start(accs[b], bass.IndirectOffsetOnAxis(ap=iout[0:CAP, u:u + 1], axis=0), Y0[b], None,
                                        compute_op=ALU.add).then_inc(S(f"scattered{b}"), 16)

            pool.wait_ge(*count("ic0_ready", 1))
            pool.wait_ge(*count("tok_out", 16))
            pool.wait_ge(*count("mix_ready0", T))
            for u in range(U):
                gather0(0, u)
            pool.wait_ge(*count("acc_out", 32))
            with pool.Fori(1, E0 // U) as i:
                for u in range(U):
                    scatter0(i - 1, u)
                    gather0(i, u)
            for u in range(U):
                scatter0(E0 // U - 1, u)

            pool.wait_ge(*count("most_part", 1))
            pool.partition_all_reduce(most[:, 1:2], most[:, 0:1], P, RMAX).then_inc(S("most_all"), 1)
            pool.wait_ge(*count("most_all", 1))
            pool.tensor_copy(most_i[:, :], most[0:1, 1:2]).then_inc(S("most_ready"), 1)
            for m in range(T):
                if m == 0:
                    pool.wait_ge(*count("ey_ready0", E0))
                pool.tensor_copy(AT[:, m, :], CT[:, m, :]).then_inc(S("counts_rounded"), 1)
            pool.wait_ge(*count("biases_added", 1))
            bias(2, 3)
            pool.wait_ge(*count("late_in", 48))
            bias(3, 1)

            def gather1(i, u, first=False):
                e = U * i + u
                if not first:
                    pool.wait_ge(*count(f"g{u}_in1", 16 * i))
                    pool.wait_ge(*count("eT_ready1", e + (1 - U)))
                pool.tensor_copy(icur[0:C, u:u + 1], rows_i[:, 0, ds(e, 1)]).then_inc(S("icur_set1"), 1)
                pool.wait_ge(*count("icur_set1", e + 1))
                pool.sem_inc(S("pool_passed"))
                pool.indirect_dma_start(G1[u], None, toks[1], bass.IndirectOffsetOnAxis(ap=icur[0:C, u:u + 1], axis=0),
                                        bounds_check=N - 1, oob_is_err=False).then_inc(S(f"g{u}_in1"), 16)

            def scatter1(i, u):
                e = U * i + u
                pool.wait_ge(*count(f"y1_out{u}", 16 * i))
                pool.tensor_copy(iout[0:C, u:u + 1], rows_i[:, 1, ds(e, 1)]).then_inc(S("iout_set1"), 1)
                pool.wait_ge(*count("iout_set1", e + 1))
                pool.wait_ge(*count("ey_done1", e + 1))
                pool.sem_inc(S("pool_passed"))
                pool.indirect_dma_start(chosen_d, bass.IndirectOffsetOnAxis(ap=iout[0:C, u:u + 1], axis=0), Y1[u], None,
                                        bounds_check=2 * N - 1, oob_is_err=False).then_inc(S(f"y1_out{u}"), 16)

            pool.wait_ge(*count("rows_ready", 1))
            pool.wait_ge(*count("table_ready", 3))
            pool.wait_ge(*count("tok_out", 32))
            turns = pool.value_load(trow_i[0:1, P:P + 1], min_val=3, max_val=MAXT // U)
            for u in range(U):
                gather1(0, u, first=True)
            pool.wait_ge(*count("outs_ready", 1))
            with pool.Fori(1, turns) as i:
                for u in range(U):
                    gather1(i, u)
                    scatter1(i - 1, u)
            last = pool.value_load(trow_i[0:1, P + 2:P + 3], min_val=2, max_val=MAXT // U - 1)
            for u in range(U):
                scatter1(last, u)
            for m in range(T + 3):
                if m < T:
                    pool.wait_ge(*count("rows_scaled1", m + 1))
                    pool.tensor_tensor(H[:, m, :], H[:, m, :], YG[m][:, 0, :], ALU.add).then_inc(S("rows_added1"), 1)
                if m >= 3:
                    pool.wait_ge(*count("result_scaled", m - 2))
                    if m == 3:
                        pool.wait_ge(*count("x_biased3", T))
                    pool.tensor_tensor(X[:, m - 3, :], X[:, m - 3, :], H[:, m - 3, :], ALU.add
                                       ).then_inc(S("out_ready"), 1)

        @block.scalar
        def _(act):
            def norm_root(n, m):
                act.wait_ge(*count(f"var_ready{n}", m + 1))
                act.activation(sd[:, m:m + 1], mv[:, m, 1:2], ACT.Sqrt, bias=epsc[:, 0:1]).then_inc(S(f"sd_ready{n}"), 1)

            def evict_xT(n, m):
                act.wait_ge(*count(f"xT_ready{n}", m + 1))
                act.activation(XT[:, :, m * P:(m + 1) * P],
                               PS[:, norm_banks(n)[m % len(norm_banks(n))], :].rearrange("p (k n) -> p k n", k=K), ACT.Copy
                               ).then_inc(S(f"xT_done{n}"), 1)

            def norm(n, lag):
                for m in range(T + lag):
                    if m < T:
                        norm_root(n, m)
                    if m >= lag:
                        evict_xT(n, m - lag)

            act.wait_ge(*count("consts", 8))
            for k in range(K):
                act.wait_ge(*count("wT_ready", k + 1))
                act.activation(W[:, 3, k, :], PS[:, 4 + k, :], ACT.Copy).then_inc(S("wT_done"), 1)
            norm(0, 1)
            act.wait_ge(*count("grow_ready", 1))

            def evict_block(m):
                act.wait_ge(*count("ct_ready", m + 1))
                for h in range(2):
                    act.activation(CT[:, m, h * 512:(h + 1) * 512], PS[:, 2 * (m % 2) + h, :], ACT.Copy
                                   ).then_inc(S("ct_done"), 1)
                act.wait_ge(*count("h_ready0", m + 1))
                act.activation(H[:, m, :], PS[:, 4 + m % 3, :], ACT.Copy).then_inc(S("h_done0"), 1)

            start = 0
            for m in range(T):
                delta = act.value_load(grow_i[0:1, 0, m:m + 1], min_val=0, max_val=2 * SHIFT)
                end = act.value_load(grow_i[0:1, 1, m:m + 1], min_val=1, max_val=NG * (m + 1))
                with act.Fori(start, end) as v:
                    group = nc.s_assert_within(v + delta - SHIFT, 0, NG - 1, skip_runtime_bounds_check_because=
                                               "the table holds only visits to groups that exist")
                    act.wait_ge(*count("onehot_d_ready", v * 2))
                    act.activation(minus_dst, edge_c[:, 1, ds(group * 4, 4)], ACT.Copy, scale=-1.0
                                   ).then_inc(S("minus_set"), 1)
                    act.wait_ge(*count("minus_set", v + 1))
                    for j in range(4):
                        ins = act.activation(away[:, j, :], iota_h[:, m * P:(m + 1) * P], ACT.Abs,
                                             bias=minus_dst[:, j:j + 1])
                        if j % 2 == 1:
                            ins.then_inc(S("away_set"), 1)
                    for h in range(2):
                        pair = slice(2 * h, 2 * h + 2)
                        act.wait_ge(*count("away_set", v * 2 + (h + 1)))
                        act.wait_ge(*count("onehot_free", v * 2 + (h + 1)))
                        act.activation(onehot_d[:, pair, :], away[:, pair, :], ACT.Relu, bias=onescol[:, 0:1],
                                       scale=-1.0).then_inc(S("onehot_d_ready"), 1)
                start = end
                if m >= 1:
                    evict_block(m - 1)
            evict_block(T - 1)
            act.wait_ge(*count("deg_done", 1))
            act.activation(sd[:, :], deg[:, 0:T], ACT.Sqrt).then_inc(S("degroot_ready"), 1)
            act.wait_ge(*count("dinv_ready", 1))
            for m in range(T):
                act.wait_ge(*count("h_biased", m + 1))
                act.activation(H_hi[:, m, :], H[:, m, :], ACT.Copy, scale=dinv[:, m:m + 1]
                               ).then_inc(S("h_rounded0"), 1)

            def exp_q(L):
                for t in range(T):
                    w = HEADS * (SLICE if L == 0 else DH)
                    act.wait_ge(*count(f"q_shifted{L}", t + 1))
                    act.activation(Q[:, t, 0:w], Q[:, t, 0:w], ACT.Exp).then_inc(S(f"q_exp{L}"), 1)

            def evict_v(L):
                for m in range(T):
                    act.wait_ge(*count(f"v_ready{L}", m + 1))
                    act.activation(V[:, m, :], PS[:, 4 + m % 4, :], ACT.Copy).then_inc(S(f"v_done{L}"), 1)

            def exp_k(L, g):
                act.wait_ge(*count(f"kmax_ready{L}", g + 1))
                act.activation(KTrs[L][:, g, :], KTrs[L][:, g, :], ACT.Exp, bias=kmax[:, g:g + 1],
                               accum_out=ksum[:, g:g + 1]).then_inc(S(f"k_exp{L}"), 1)

            def evict_kr(L):
                w = HEADS * (SLICE if L == 0 else DH)
                per = 512 // w
                for i in range(T // per):
                    act.wait_ge(*count(f"kr_ready{L}", i + 1))
                    for j in range(per):
                        ins = act.activation(KR[:, i * per + j, 0:w], PS[:, i % 4, j * w:(j + 1) * w], ACT.Copy)
                    ins.then_inc(S(f"kr_done{L}"), 1)

            def evict_qT(L):
                for i in range(2 * (2 if L == 0 else K)):
                    act.wait_ge(*count(f"qT_ready{L}", i + 1))
                    act.activation(KTrs[L][:, i // 2, (i % 2) * 512:(i % 2 + 1) * 512], PS[:, 4 + i % 4, :], ACT.Copy
                                   ).then_inc(S(f"qT_done{L}"), 1)

            def evict_oT(L):
                for i in range(2 * K):
                    act.wait_ge(*count(f"oT_ready{L}", i + 1))
                    act.activation(OT_hi[:, i // 2, (i % 2) * 512:(i % 2 + 1) * 512], PS[:, 4 + i % 4, :], ACT.Copy
                                   ).then_inc(S(f"oT_rounded{L}"), 1)

            def softmax_exp(n):
                act.wait_ge(*count(f"logit_shifted{n}", 1))
                w = (E0, E1)[n]
                act.activation(PR[:, :, 0:w], PR[:, :, 0:w], ACT.Exp).then_inc(S(f"logit_exp{n}"), 1)

            def round_tokens():
                for k in range(K):
                    act.activation(XT_hi[:, k, :], XT[:, k, :], ACT.Copy).then_inc(S("xt_rounded"), 1)

            def round_weights(n):
                name, loaded, slot, high = splits[n]
                act.wait_ge(*count(name, loaded))
                for c in range(K):
                    part = slice(c * P, (c + 1) * P)
                    act.activation(high[:, :, part], W[:, slot, :, part], ACT.Copy).then_inc(S("w_rounded"), 1)

            round_tokens()
            round_weights(WIN)
            act.wait_ge(*count("bias_in", 16 * 8))
            act.wait_ge(*count("gnn_ready0", T))
            for i in range(2 * K):
                act.wait_ge(*count("xm_ready", i + 1))
                act.activation(XM[:, i // 2, (i % 2) * 512:(i % 2 + 1) * 512], PS[:, 4 + i % 4, :], ACT.Identity,
                               bias=cols_sm[:, 192 + i // 2:193 + i // 2]).then_inc(S("xm_done"), 1)
            for i in range(4):
                act.wait_ge(*count("k_ready0", i + 1))
                act.activation(KTrs[0][:, i // 2, (i % 2) * 512:(i % 2 + 1) * 512], PS[:, i % 4, :], ACT.Copy
                               ).then_inc(S("k_done0"), 1)
            for g in range(2):
                exp_k(0, g)
            exp_q(0)
            evict_v(0)
            round_weights(WOUT)
            evict_kr(0)
            evict_qT(0)
            evict_oT(0)
            norm(1, 3)
            softmax_exp(0)
            for i in range(2 * HJ):
                act.wait_ge(*count("sh_ready", i + 1))
                act.activation(SHT[:, i // 2, (i % 2) * 512:(i % 2 + 1) * 512], PS[:, 4 + i % 4, :],
                               ACT.Gelu_apprx_tanh, bias=cols_sm[:, 196 + i // 2:197 + i // 2]
                               ).then_inc(S("sh_done"), 1)

            act.wait_ge(*count("tok_out", 16))
            for m in range(T):
                act.wait_ge(*count("shared_ready", m + 1))
                act.activation(XN[:, m, :], PS[:, 4 + m % 4, :], ACT.Copy).then_inc(S("rows_scaled0"), 1)

            def expert(L, i, u, first):
                e = U * i + u
                n, gt, ht = (CAP, GT0, HT0) if L == 0 else (C, GT1, HT1)
                b = u % 2
                act.wait_ge(*count(f"eT_ready{L}", e + 1))
                if not (first and u < 2):
                    act.wait_ge(*count(f"eh_ready{L}", e - 1))
                act.activation(gt[b].rearrange("p k n -> p (k n)"), PS[:, b, 0:K * n], ACT.Copy
                               ).then_inc(S(f"eT_done{L}"), 1)
                act.wait_ge(*count(f"eh_ready{L}", e + 1))
                if not (first and u < 2):
                    act.wait_ge(*count(f"ey_ready{L}", e - 1))
                if L == 1:
                    x = act.value_load(trow_i[0:1, ds(e, 1)], min_val=0, max_val=E1 - 1)
                    bias = [cols_sm[:, ds(x + (32 + j * E1), 1)] for j in range(HJ)]
                else:
                    bias = [cols_sm[:, ds(e + j * E0, 1)] for j in range(HJ)]
                for j in range(HJ):
                    ins = act.activation(ht[b][:, j, :], PS[:, 2 + b, j * n:(j + 1) * n],
                                         ACT.Gelu_apprx_tanh if L == 0 else ACT.Relu, bias=bias[j])
                ins.then_inc(S(f"eh_done{L}"), 1)

            for u in range(U):
                expert(0, 0, u, True)
            with act.Fori(1, E0 // U) as i:
                for u in range(U):
                    expert(0, i, u, False)

            norm(2, 1)
            for m in range(T):
                act.wait_ge(*count("h_ready1", m + 1))
                act.activation(H_hi[:, m, :], PS[:, 4 + m % 4, :], ACT.Copy).then_inc(S("h_rounded1"), 1)
            round_tokens()
            act.wait_ge(*count("gnn_ready1", T))
            round_weights(WK)
            round_weights(WQ)
            for i in range(2 * K):
                act.wait_ge(*count("k_low", i + 1))
                k = KTrs[1][:, i // 2, (i % 2) * 512:(i % 2 + 1) * 512]
                act.activation(k, k, ACT.Exp).then_inc(S("k_elu"), 1)
            round_weights(WV)
            round_weights(WC)
            for g in range(K):
                exp_k(1, g)
            exp_q(1)
            evict_v(1)
            round_weights(WPROJ)
            evict_kr(1)
            evict_qT(1)
            evict_oT(1)
            norm(3, 3)
            softmax_exp(1)
            act.wait_ge(*count("swT_ready", 1))
            for h in range(2):
                act.activation(SWT[:, h * 512:(h + 1) * 512], PS[0:E1, 4 + h, :], ACT.Copy).then_inc(S("swT_done"), 1)
            for m in range(T):
                act.wait_ge(*count("rb_ready1", m + 1))
                act.activation(RB[:, m, :], PS[:, 4 + m % 4, :], ACT.Copy).then_inc(S("rb_done1"), 1)
            act.wait_ge(*count("table_ready", 3))
            turns = act.value_load(trow_i[0:1, P:P + 1], min_val=3, max_val=MAXT // U)
            for u in range(U):
                expert(1, 0, u, True)
            with act.Fori(1, turns) as i:
                for u in range(U):
                    expert(1, i, u, False)
            for m in range(T + 3):
                if m < T:
                    act.wait_ge(*count(f"yg_in{m}", 16))
                    act.activation(YG[m][:, 0, :], YG[m][:, 0, :], ACT.Copy, scale=top8[:, m, 0:1]
                                   ).then_inc(S("rows_scaled1"), 1)
                if 2 <= m < T + 2:
                    norm_root(4, m - 2)
                if m >= 3:
                    act.wait_ge(*count("rs_ready", m - 2))
                    act.activation(H[:, m - 3, :], H[:, m - 3, :], ACT.Copy, scale=rs[:, m - 3:m - 2]
                                   ).then_inc(S("result_scaled"), 1)

        @block.tensor
        def _(pe):
            def tr(bank, c0, in_, w=P):
                rows = in_.shape[0]
                return pe.transpose(PS[0:w, bank, c0:c0 + rows], in_, ident[0:rows, 0:rows])

            def transposes(n, m):
                banks = norm_banks(n)
                pe.wait_ge(*count(f"xn_ready{n}", m + 1))
                if m >= len(banks):
                    pe.wait_ge(*count(f"xT_done{n}", m + 1 - len(banks)))
                bank = banks[m % len(banks)]
                for k in range(K):
                    ins = tr(bank, k * P, normed[n][:, m, k * P:(k + 1) * P])
                ins.then_inc(S(f"xT_ready{n}"), 1)

            def token_rows(name, base, pairs, done, width=D, norm=None):
                def logits(m):
                    w, at = ((E0, 0), (E1, E0))[norm // 2]
                    pe.wait_ge(*count(f"xT_done{norm}", m + 1))
                    for k in range(K):
                        ins = pe.matmul(PS[:, 7, m * w:(m + 1) * w], XT[:, k, m * P:(m + 1) * P],
                                        GW[:, k, at:at + w], start=(k == 0), stop=(k == K - 1), skip_group_check=True)
                    if m == T - 1:
                        ins.then_inc(S(f"logit_ready{norm // 2}"), 1)

                if norm:
                    pe.wait_ge(*count("gate_in", 48))
                for m in range(T):
                    if m >= 4:
                        pe.wait_ge(*count(done, m - 3))
                    for n, (left, right) in enumerate(pairs):
                        ins = pe.matmul(PS[:, base + m % 4, 0:width], left[:, m * P:(m + 1) * P], right,
                                        start=(n == 0), stop=(n == len(pairs) - 1))
                    ins.then_inc(S(name), 1)
                    if norm and m >= 3:
                        transposes(norm, m - 3)
                    if norm and m >= 4:
                        logits(m - 4)
                if norm:
                    for m in range(T - 3, T):
                        transposes(norm, m)
                        logits(m - 1)
                    logits(T - 1)

            def split_pairs(high, low, n):
                _, _, slot, w_high = splits[n]
                return [(x[:, k], w[:, k, :]) for k in range(K)
                        for x, w in ((high, w_high), (low, w_high), (high, W_lo[:, slot]))]

            def channel_rows(name, base, n, done):
                _, _, slot, w_high = splits[n]
                for i in range(2 * K):
                    c, half = i // 2, i % 2
                    pe.wait_ge(*count("w_split", K * n + c + 1))
                    if i >= 4:
                        pe.wait_ge(*count(done, i - 3))
                    parts = [(w[:, k, c * P:(c + 1) * P], x[:, k, half * 512:(half + 1) * 512]) for k in range(K)
                             for w, x in ((w_high, XT_hi), (w_high, XT_lo), (W_lo[:, slot], XT_hi))]
                    for j, (w, x) in enumerate(parts):
                        ins = pe.matmul(PS[:, base + i % 4, :], w, x, start=(j == 0), stop=(j == len(parts) - 1))
                    ins.then_inc(S(name), 1)

            pe.wait_ge(*count("consts", 8))
            pe.wait_ge(*count("edge_f_ready", 2))
            pe.wait_ge(*count("small_in", 32))
            tr(0, 0, edge_f[:, 0, :])
            tr(0, P, edge_f[:, 1, :]).then_inc(S("small_ready"), 1)
            for j in range(HJ):
                tr(1, j * E0, rows_sm[0:E0, 0, j * P:(j + 1) * P])
                ins = tr(1, 32 + j * E1, rows_sm[0:E1, 1, j * P:(j + 1) * P])
            ins.then_inc(S("small_ready"), 1)
            pe.wait_ge(*count("gnnw_in", 16))
            for k in range(K):
                for j in range(K):
                    ins = tr(4 + k, j * P, W[:, 0, j, k * P:(k + 1) * P])
                ins.then_inc(S("wT_ready"), 1)
            pe.wait_ge(*count("small_done", 2))
            for m in range(T):
                transposes(0, m)

            pe.nop().then_inc(S("onehot_free"), 2)
            pe.wait_ge(*count("xT_done0", T))
            pe.wait_ge(*count("zeros_ready", 1))
            pe.wait_ge(*count("grow_ready", 1))
            pe.wait_ge(*count("wT_done", K))

            def degree_parts(k):
                pe.wait_ge(*count("ct_done", 2 * (k + 1)))
                pe.wait_ge(*count("at_done", k + 1))
                for m in range(T):
                    at_ = 2 * (k * T + m)
                    ins = pe.matmul(PS[:, 7, at_:at_ + 2], AT[:, k, m * P:(m + 1) * P], ones_r[:, :], start=True,
                                    stop=True, skip_group_check=True)
                ins.then_inc(S("deg_ready"), 1)

            start = 0
            for m in range(T):
                if m >= 2:
                    pe.wait_ge(*count("ct_done", 2 * (m - 1)))
                banks = [PS[:, 2 * (m % 2) + h, :] for h in range(2)]
                for h in range(2):
                    pe.matmul(banks[h], zero_b[:, 0:P], zero_b, start=True, stop=False)
                end = pe.value_load(grow_i[0:1, 1, m:m + 1], min_val=1, max_val=NG * (m + 1))
                with pe.Fori(start, end) as v:
                    for j in range(4):
                        if j % 2 == 0:
                            pe.wait_ge(*count("onehot_ready", v * 2 + (j // 2 + 1)))
                            pe.wait_ge(*count("onehot_d_ready", v * 2 + (j // 2 + 1)))
                        pe.matmul(banks[0], onehot_d[:, j, :], onehot_s[:, j, 0:512], start=False, stop=False)
                        ins = pe.matmul(banks[1], onehot_d[:, j, :], onehot_s[:, j, 512:1024], start=False, stop=False)
                        if j % 2 == 1:
                            ins.then_inc(S("onehot_free"), 1)
                start = end
                pe.matmul(banks[0], zero_b[:, 0:P], zero_b, start=False, stop=True)
                pe.matmul(banks[1], zero_b[:, 0:P], zero_b, start=False, stop=True).then_inc(S("ct_ready"), 1)
                if m >= 3:
                    pe.wait_ge(*count("h_done0", m - 2))
                for k in range(K):
                    ins = pe.matmul(PS[:, 4 + m % 3, :], XT[:, k, m * P:(m + 1) * P], W[:, 3, k, :],
                                    start=(k == 0), stop=(k == K - 1))
                ins.then_inc(S("h_ready0"), 1)
                if m >= 1:
                    degree_parts(m - 1)
            degree_parts(T - 1)
            pe.wait_ge(*count("h_done0", T))
            pe.wait_ge(*count("deg_done", 1))
            for m in range(T):
                if m >= 4:
                    pe.wait_ge(*count("gnn_done0", m - 3))
                for k in range(T):
                    if m == 0:
                        pe.wait_ge(*count("h_split", k + 1))
                    pe.matmul(PS[:, 4 + m % 4, :], AT[:, k, m * P:(m + 1) * P], H_hi[:, k, :],
                              start=(k == 0), stop=False)
                    ins = pe.matmul(PS[:, 4 + m % 4, :], AT[:, k, m * P:(m + 1) * P], H_lo[:, k, :],
                                    start=False, stop=(k == T - 1))
                ins.then_inc(S("gnn_ready0"), 1)

            pe.wait_ge(*count("xt_split", K))
            pe.wait_ge(*count("gnn_done0", T))
            channel_rows("xm_ready", 4, WIN, "xm_done")
            pe.wait_ge(*count("xm_done", 2 * K))
            pe.wait_ge(*count("bd_in", 16 * 6))
            for i in range(4):
                g, half = i // 2, i % 2
                for s in range(2):
                    ins = pe.matmul(PS[s * 64:(s + 1) * 64, i % 4, :], BDK[:, :],
                                    XM[:, 2 * g + s, half * 512:(half + 1) * 512], start=True, stop=True,
                                    skip_group_check=True)
                ins.then_inc(S("k_ready0"), 1)
            for m in range(T):
                if m == 0:
                    pe.wait_ge(*count("k_done0", 4))
                if m >= 4:
                    pe.wait_ge(*count("q_done0", m - 3))
                for c in range(K):
                    ins = pe.matmul(PS[:, m % 4, c * 64:(c + 1) * 64], XM[:, c, m * P:(m + 1) * P], BDQ[:, :],
                                    start=True, stop=True, skip_group_check=True)
                ins.then_inc(S("q_ready0"), 1)
            for m in range(T):
                if m >= 4:
                    pe.wait_ge(*count("v_done0", m - 3))
                for c in range(K):
                    ins = pe.matmul(PS[:, 4 + m % 4, c * P:(c + 1) * P], XM[:, c, m * P:(m + 1) * P], BDV[:, :],
                                    start=True, stop=True, skip_group_check=True)
                ins.then_inc(S("v_ready0"), 1)

            def attend(L):
                groups = 2 if L == 0 else K
                w = groups * P
                per = 512 // w
                pe.wait_ge(*count(f"k_exp{L}", groups))
                pe.wait_ge(*count(f"q_done{L}", T))
                for i in range(T // per):
                    if i >= 4:
                        pe.wait_ge(*count(f"kr_done{L}", i - 3))
                    for j in range(per):
                        for g in range(groups):
                            ins = tr(i % 4, j * w + g * P, KTrs[L][:, g, (i * per + j) * P:(i * per + j + 1) * P])
                    ins.then_inc(S(f"kr_ready{L}"), 1)
                pe.wait_ge(*count(f"kr_done{L}", T // per))
                pe.wait_ge(*count(f"v_done{L}", T))
                for i in range(2 * groups):
                    g, half = i // 2, i % 2
                    pe.wait_ge(*count(f"q_soft{L}", 4 * (half + 1)))
                    if i >= 4:
                        pe.wait_ge(*count(f"qT_done{L}", i - 3))
                    for j in range(4):
                        ins = tr(4 + i % 4, j * P, Q[:, 4 * half + j, g * P:(g + 1) * P])
                    ins.then_inc(S(f"qT_ready{L}"), 1)
                vw = D // groups
                for g in range(groups):
                    for m in range(T):
                        ins = pe.matmul(PS[:, g, 0:vw], KR[:, m, g * P:(g + 1) * P],
                                        V[:, m, g * vw:(g + 1) * vw], start=(m == 0), stop=(m == T - 1))
                    ins.then_inc(S(f"kv_ready{L}"), 1)
                pe.wait_ge(*count(f"kv_done{L}", groups))
                pe.wait_ge(*count(f"qT_done{L}", 2 * groups))
                for i in range(2 * K):
                    c, half = i // 2, i % 2
                    if i >= 4:
                        pe.wait_ge(*count(f"oT_done{L}", i - 3))
                    g, at = (c // 2, (c % 2) * P) if L == 0 else (c, 0)
                    pe.matmul(PS[:, 4 + i % 4, :], KV[:, g * vw + at:g * vw + at + P], KTrs[L][:, g, half * 512:(half + 1) * 512],
                              start=True, stop=True).then_inc(S(f"oT_ready{L}"), 1)
                pe.wait_ge(*count(f"oT_done{L}", 2 * K))

            attend(0)
            pe.wait_ge(*count("w_split", K * (WOUT + 1)))
            token_rows("mix_ready0", 0, split_pairs(OT_hi, OT_lo, WOUT), "mix_done0",
                       norm=1)

            def edges_by_source(tiles):
                for m in range(T)[tiles]:
                    for k in range(T):
                        ins = pe.matmul(PS[:, 2, m:m + 1], CT[:, k, m * P:(m + 1) * P], onescol[:, :],
                                        start=(k == 0), stop=(k == T - 1), skip_group_check=True)
                if m == T - 1:
                    ins.then_inc(S("deg_ready"), 1)

            pe.wait_ge(*count("mix_done0", T))
            pe.wait_ge(*count("xT_done1", T))
            pe.wait_ge(*count("shared_in", 32))
            sw1 = W[:, 0, 0:2, :].rearrange("p a b -> p (a b)").rearrange("p (k n) -> p k n", k=K)
            for i in range(2 * HJ):
                j, half = i // 2, i % 2
                if i == 2:
                    edges_by_source(slice(0, T // 2))
                    pe.wait_ge(*count("probs_ready0", 1))
                    for m in range(T):
                        ins = tr(m // 4, (m % 4) * P, PR[:, m, 0:E0], E0)
                    ins.then_inc(S("pT_ready"), 1)
                if i == 3:
                    pe.wait_ge(*count("logit_shifted0", 1))
                for k in range(K):
                    ins = pe.matmul(PS[:, 4 + i % 4, :], sw1[:, k, j * P:(j + 1) * P],
                                    XT[:, k, half * 512:(half + 1) * 512], start=(k == 0), stop=(k == K - 1))
                ins.then_inc(S("sh_ready"), 1)
            pe.wait_ge(*count("sh_done", 2 * HJ))
            for m in range(T):
                if m >= 4:
                    pe.wait_ge(*count("rows_scaled0", m - 3))
                for j in range(HJ):
                    ins = pe.matmul(PS[:, 4 + m % 4, :], SHT[:, j, m * P:(m + 1) * P], W[:, 0, 2 + j, :],
                                    start=(j == 0), stop=(j == HJ - 1))
                ins.then_inc(S("shared_ready"), 1)
            edges_by_source(slice(T // 2, T))
            pe.wait_ge(*count("top_ready", 2))
            tr(0, 0, ixf0[:, :], CAP)
            tr(0, E0, sc0[:, :], CAP).then_inc(S("scT_ready"), 1)
            pe.wait_ge(*count("rows_scaled0", T))
            for m in range(T):
                if m >= 4:
                    pe.wait_ge(*count("rb_done0", m - 3))
                pe.matmul(PS[:, 4 + m % 4, :], PTW[:, m * P:(m + 1) * P], B2R0[:, :], start=True, stop=True
                          ).then_inc(S("rb_ready0"), 1)
            pe.wait_ge(*count("rb_done0", T))
            pe.wait_ge(*count("scT_done", 1))
            pe.wait_ge(*count("deg_done", 2))

            def expert_T(L, e, u, i):
                n, g = (CAP, G0) if L == 0 else (C, G1)
                pe.wait_ge(*count(f"g{u}_in{L}", (i + 1) * 16))
                pe.sem_inc(S("pe_passed"))
                for k in range(K):
                    ins = tr(u % 2, k * n, g[u][:, k * P:(k + 1) * P])
                ins.then_inc(S(f"eT_ready{L}"), 1)

            def expert_h(L, e, u, i):
                n, gt = (CAP, GT0) if L == 0 else (C, GT1)
                b = u % 2
                pe.wait_ge(*count(f"eT_done{L}", e + 1))
                pe.wait_ge(*count(f"ew{u}_in{L}", (i + 1) * 32))
                for j in range(HJ):
                    for k in range(K):
                        ins = pe.matmul(PS[:, 2 + b, j * n:(j + 1) * n], EW1[u][:, k, j * P:(j + 1) * P], gt[b][:, k, :],
                                        start=(k == 0), stop=(k == K - 1), skip_group_check=True)
                ins.then_inc(S(f"eh_ready{L}"), 1)

            def expert(L, i, u, first=False, last=False):
                e = U * i + u
                n, ht = (CAP, HT0) if L == 0 else (C, HT1)
                b = u % 2
                if not (last and u == U - 1):
                    expert_h(L, e + 1, (u + 1) % U, i + (u + 1) // U)
                if not (last and u >= U - 2):
                    expert_T(L, e + 2, (u + 2) % U, i + (u + 2) // U)
                pe.wait_ge(*count(f"eh_done{L}", e + 1))
                if not (first and u < 2):
                    pe.wait_ge(*count(f"ey_done{L}", e - 1))
                for j in range(HJ):
                    ins = pe.matmul(PS[0:n, 4 + b, :], ht[b][:, j, :], EW2[u][:, j, :],
                                    start=(j == 0), stop=(j == HJ - 1))
                ins.then_inc(S(f"ey_ready{L}"), 1)

            def experts_begin(L):
                expert_T(L, 0, 0, 0)
                expert_h(L, 0, 0, 0)
                expert_T(L, 1, 1, 0)

            experts_begin(0)
            for u in range(U):
                expert(0, 0, u, first=True)
            with pe.Fori(1, E0 // U - 1) as i:
                for u in range(U):
                    expert(0, i, u)
            for u in range(U):
                expert(0, E0 // U - 1, u, last=True)

            def wn_rows(m):
                pe.wait_ge(*count("xT_done2", m + 1))
                if m >= 4:
                    pe.wait_ge(*count("h_done1", m - 3))
                for k in range(K):
                    ins = pe.matmul(PS[:, 4 + m % 4, :], XT[:, k, m * P:(m + 1) * P], W[:, 3, k, :],
                                    start=(k == 0), stop=(k == K - 1))
                ins.then_inc(S("h_ready1"), 1)

            pe.wait_ge(*count("ey_done0", E0))
            pe.wait_ge(*count("w3_in", 16))
            for m in range(T):
                transposes(2, m)
                if 1 <= m <= 4:
                    wn_rows(m - 1)
            for m in range(4, T):
                wn_rows(m)
            pe.wait_ge(*count("h_done1", T))
            pe.wait_ge(*count("counts_rounded", T))
            pe.wait_ge(*count("most_ready", 1))
            most = pe.value_load(most_i[0:1, 0:1], min_val=0, max_val=NE)
            with pe.If(most <= EXACT):
                token_rows("gnn_ready1", 0, [(AT[:, k], h[:, k, :]) for k in range(T) for h in (H_hi, H_lo)],
                           "gnn_done1")
            with pe.If(most > EXACT):
                token_rows("gnn_ready1", 0, [(CT[:, k], h[:, k, :].bitcast(F32)) for k in range(T)
                                             for h in (H_hi, H_lo)], "gnn_done1")
            pe.wait_ge(*count("gnn_done1", T))
            pe.wait_ge(*count("xt_split", 2 * K))
            channel_rows("k_ready1", 0, WK, "k_done1")
            pe.wait_ge(*count("k_done1", 2 * K))
            pe.wait_ge(*count("w_split", K * (WQ + 1)))
            token_rows("q_ready1", 0, split_pairs(XT_hi, XT_lo, WQ), "q_done1")
            pe.wait_ge(*count("w_split", K * (WV + 1)))
            token_rows("v_ready1", 4, split_pairs(XT_hi, XT_lo, WV), "v_done1")
            attend(1)
            pe.wait_ge(*count("w_split", K * (WPROJ + 1)))
            token_rows("mix_ready1", 0, split_pairs(XT_hi, XT_lo, WC)
                       + split_pairs(OT_hi, OT_lo, WPROJ), "mix_done1", norm=3)

            pe.wait_ge(*count("mix_done1", T))
            pe.wait_ge(*count("xT_done3", T))
            pe.wait_ge(*count("mb_ready", 1))
            for m in range(T):
                for q in range(m + 1):
                    pe.matmul(PS[:, 1, m * E1:(m + 1) * E1], tri_b[:, :] if q == m else ones_b[:, :], MB[:, q, :],
                              start=(q == 0), stop=(q == m), skip_group_check=True)
            for q in range(T):
                ins = pe.matmul(PS[:, 2, 0:E1], ones_b[:, :], MB[:, q, :], start=(q == 0), stop=(q == T - 1))
            ins.then_inc(S("place_ready"), 1)
            pe.wait_ge(*count("ecol_ready", 1))
            tr(3, 0, ecol[:, :], 1).then_inc(S("erow_ready"), 1)
            pe.wait_ge(*count("sww_ready", 1))
            for m in range(T):
                ins = tr(4 + m // 4, (m % 4) * P, SWW[:, m, :], E1)
            ins.then_inc(S("swT_ready"), 1)
            pe.wait_ge(*count("swT_done", 2))
            pe.wait_ge(*count("late_in", 48))
            for m in range(T):
                if m >= 4:
                    pe.wait_ge(*count("rb_done1", m - 3))
                pe.matmul(PS[:, 4 + m % 4, :], SWT[:, m * P:(m + 1) * P], B2R1[:, :], start=True, stop=True
                          ).then_inc(S("rb_ready1"), 1)
            pe.wait_ge(*count("hot_ready", 1))
            for a in range(2 * T):
                ins = pe.matmul(PS[0:C, 0, 0:MAXT], lane_hot[:, a, :], tile_hot[:, a, :], start=(a == 0),
                                stop=(a == 2 * T - 1))
            ins.then_inc(S("rows_summed"), 1)
            pe.wait_ge(*count("table_ready", 3))
            pe.wait_ge(*count("rows_ready", 1))
            pe.wait_ge(*count("rb_done1", T))
            turns = pe.value_load(trow_i[0:1, P:P + 1], min_val=3, max_val=MAXT // U)
            experts_begin(1)
            for u in range(U):
                expert(1, 0, u, first=True)
            with pe.Fori(1, turns - 1) as i:
                for u in range(U):
                    expert(1, i, u)
            for u in range(U):
                expert(1, turns - 1, u, last=True)

        @block.vector
        def _(dve):
            own = [0]

            def step(ins):
                ins.then_inc(S("dve_step"), 1)
                own[0] += 1

            def settle():
                dve.wait_ge(*count("dve_step", own[0]))

            def stats(n, m, src):
                step(dve.bn_stats(st[:, m, :], src[:, m, :]))
                settle()
                dve.bn_aggr(mv[:, m, :], st[:, m, :]).then_inc(S(f"var_ready{n}"), 1)

            def inverse_root(n, m):
                dve.wait_ge(*count(f"sd_ready{n}", m + 1))
                step(dve.reciprocal(rs[:, m:m + 1], sd[:, m:m + 1]))
                settle()

            def norm(n, before):
                for m in range(T + 1):
                    if m < T:
                        before(m)
                        stats(n, m, X)
                    if m >= 1:
                        inverse_root(n, m - 1)
                        dve.tensor_scalar(normed[n][:, m - 1, :], X[:, m - 1, :], mv[:, m - 1, 0:1], rs[:, m - 1:m],
                                          ALU.subtract, ALU.mult).then_inc(S(f"xn_ready{n}"), 1)

            def input_tile(m):
                if m % 2 == 0:
                    dve.wait_ge(*count(f"x_in{m // 2}", 16))

            def add_mix(L, m):
                dve.wait_ge(*count(f"mix_ready{L}", m + 1))
                dve.tensor_tensor(X[:, m, :], X[:, m, :], PS[:, m % 4, :], ALU.add).then_inc(S(f"mix_done{L}"), 1)
                dve.wait_ge(*count(f"mix_done{L}", m + 1))

            def add_routed(m):
                if m % 2 == 0:
                    dve.wait_ge(*count(f"x_in{m // 2}", 48))
                step(dve.tensor_tensor(X[:, m, :], X[:, m, :], XN[:, m, :], ALU.add))
                settle()

            dve.wait_ge(*count("consts", 8))
            step(dve.tensor_copy(iota_h[:, :], iota_i[:, :]))
            step(dve.tensor_copy(iota_e[:, :], iota_i[:, 0:E1]))
            step(dve.tensor_scalar(limits[:, :], iota_i[:, 0:NC], float(C), None, ALU.mult))
            step(dve.tensor_copy(pcol[:, :], pcol_i[:, :]))
            step(dve.tensor_copy(ids[:, :], ids_i[:, :]))
            step(dve.tensor_scalar(ones_r[:, :], iota_i[:, 0:2], 0.0, 1.0, ALU.mult, ALU.add))
            dve.wait_ge(*count("edges_in", 48))
            for i in range(2):
                dve.tensor_copy(edge_f[:, i, :], edge_i[:, i, :]).then_inc(S("edge_f_ready"), 1)
            step(dve.tensor_reduce(gmm[:, 0:1], dgrp_i[:, :], AX_X, ALU.min))
            step(dve.tensor_reduce(gmm[:, 1:2], dgrp_i[:, :], AX_X, ALU.max))
            settle()
            step(dve.tensor_scalar(gov[:, 0, :], iota_i[0:NG, 0:N:P], gmm[:, 1:2], None, ALU.is_le))
            step(dve.tensor_scalar(gov[:, 1, :], iota_i[0:NG, P - 1:N:P], gmm[:, 0:1], None, ALU.is_ge))
            step(dve.tensor_scalar(gov[:, 3, 0:1], pcol[0:NG, :], -1.0, float(NG), ALU.mult, ALU.add))
            step(dve.tensor_scalar(gov[:, 3, 1:2], pcol[0:NG, :], 1.0, None, ALU.add))
            settle()
            step(dve.tensor_tensor(gov[:, 2, :], gov[:, 0, :], gov[:, 1, :], ALU.mult))
            settle()
            dve.tensor_scalar(gval[:, 0:T], gov[:, 2, :], gov[:, 3, 0:1], None, ALU.mult).then_inc(S("gval_ready"), 1)
            dve.tensor_scalar(gval[:, T:2 * T], gov[:, 2, :], gov[:, 3, 1:2], None, ALU.mult
                              ).then_inc(S("gval_ready"), 1)
            dve.wait_ge(*count("small_ready", 2))
            dve.tensor_copy(edge_c[:, :, :].rearrange("p a b -> p (a b)"), PS[:, 0, 0:2 * P]
                            ).then_inc(S("small_done"), 1)
            dve.tensor_copy(cols_sm[:, 0:160], PS[:, 1, 0:160]).then_inc(S("small_done"), 1)
            dve.wait_ge(*count("small_done", 2))

            norm(0, input_tile)

            dve.wait_ge(*count("gred_ready", 1))
            step(dve.tensor_scalar(grow[:, 0, :], gred[0:1, 0:T], -1.0, float(NG), ALU.mult, ALU.add))
            settle()
            step(dve.tensor_scalar(grow[:, 1, :], grow[:, 0, :], float(NG - 1), None, ALU.min))
            settle()
            step(dve.tensor_tensor(grow[:, 2, :], gred[0:1, T:2 * T], grow[:, 1, :], ALU.subtract))
            settle()
            step(dve.tensor_scalar(grow[:, 3, :], grow[:, 2, :], 1.0, None, ALU.max))
            step(dve.memset(grow[:, 5, :], 0.0))
            settle()
            step(dve.tensor_tensor_scan(grow[:, 4, :], grow[:, 3, :], grow[:, 5, :], 0.0, ALU.add, ALU.add))
            settle()
            step(dve.tensor_tensor(grow[:, 5, :], grow[:, 4, :], grow[:, 3, :], ALU.subtract))
            step(dve.tensor_copy(grow_i[:, 1, :], grow[:, 4, :]))
            settle()
            step(dve.tensor_tensor(grow[:, 0, :], grow[:, 1, :], grow[:, 5, :], ALU.subtract))
            settle()
            step(dve.tensor_scalar(grow[:, 0, :], grow[:, 0, :], float(SHIFT), None, ALU.add))
            settle()
            dve.tensor_copy(grow_i[:, 0, :], grow[:, 0, :]).then_inc(S("grow_ready"), 1)
            dve.wait_ge(*count("grow_ready", 1))

            def adjacency(m):
                dve.wait_ge(*count("ct_done", 2 * (m + 1)))
                step(dve.tensor_scalar(AT[:, m, :], CT[:, m, :], 1.0, None, ALU.min))
                settle()
                dve.tensor_tensor(AT[:, m, m * P:(m + 1) * P], AT[:, m, m * P:(m + 1) * P].bitcast(F32), ident[:, :],
                                  ALU.max).then_inc(S("at_done"), 1)

            start = 0
            for m in range(T):
                delta = dve.value_load(grow_i[0:1, 0, m:m + 1], min_val=0, max_val=2 * SHIFT)
                end = dve.value_load(grow_i[0:1, 1, m:m + 1], min_val=1, max_val=NG * (m + 1))
                with dve.Fori(start, end) as v:
                    group = nc.s_assert_within(v + delta - SHIFT, 0, NG - 1, skip_runtime_bounds_check_because=
                                               "the table holds only visits to groups that exist")
                    dve.wait_ge(*count("onehot_ready", v * 2))
                    dve.tensor_copy(ends[:, :], edge_c[:, 0, ds(group * 4, 4)]).then_inc(S("ends_set"), 1)
                    dve.wait_ge(*count("ends_set", v + 1))
                    for j in range(4):
                        if j % 2 == 0:
                            dve.wait_ge(*count("onehot_free", v * 2 + (j // 2 + 1)))
                        ins = dve.tensor_scalar(onehot_s[:, j, :], iota_h[:, :], ends[:, j:j + 1],
                                                None, ALU.is_equal)
                        if j % 2 == 1:
                            ins.then_inc(S("onehot_ready"), 1)
                start = end
                if m >= 1:
                    adjacency(m - 1)
            adjacency(T - 1)

            dve.wait_ge(*count("deg_ready", T))
            step(dve.tensor_reduce(deg[:, 0:T], PS[:, 7, 0:2 * T * T].rearrange("p (k m c) -> p c m k", k=T, c=2)[:, 0],
                                   AX_X, ALU.add))
            settle()
            dve.tensor_scalar(deg[:, 0:T], deg[:, 0:T], 1e-30, None, ALU.max).then_inc(S("deg_done"), 1)
            dve.wait_ge(*count("degroot_ready", 1))
            dve.reciprocal(dinv[:, :], sd[:, :]).then_inc(S("dinv_ready"), 1)
            dve.wait_ge(*count("dinv_ready", 1))
            for m in range(T):
                dve.wait_ge(*count("h_rounded0", m + 1))
                dve.scalar_tensor_tensor(H_lo[:, m, :], H[:, m, :], dinv[:, m:m + 1], H_hi[:, m, :].bitcast(F32),
                                         ALU.mult, ALU.subtract).then_inc(S("h_split"), 1)
            def split_tokens(L):
                dve.wait_ge(*count(f"h_ready{L}", T))
                for k in range(K):
                    dve.wait_ge(*count("xt_rounded", K * L + k + 1))
                    dve.tensor_tensor(XT_lo[:, k, :], XT[:, k, :], XT_hi[:, k, :].bitcast(F32), ALU.subtract
                                      ).then_inc(S("xt_split"), 1)

            def split_weights(n):
                _, _, slot, high = splits[n]
                for c in range(K):
                    part = slice(c * P, (c + 1) * P)
                    dve.wait_ge(*count("w_rounded", K * n + c + 1))
                    dve.tensor_tensor(W_lo[:, slot, :, part], W[:, slot, :, part], high[:, :, part].bitcast(F32),
                                      ALU.subtract).then_inc(S("w_split"), 1)

            def split_oT(L):
                for i in range(2 * K):
                    at_ = (slice(None), i // 2, slice((i % 2) * 512, (i % 2 + 1) * 512))
                    dve.wait_ge(*count(f"oT_rounded{L}", i + 1))
                    dve.tensor_tensor(OT_lo[at_], PS[:, 4 + i % 4, :], OT_hi[at_].bitcast(F32), ALU.subtract
                                      ).then_inc(S(f"oT_done{L}"), 1)

            split_tokens(0)
            split_weights(WIN)
            for m in range(T):
                dve.wait_ge(*count("gnn_ready0", m + 1))
                dve.wait_ge(*count("x_biased0", m + 1))
                dve.scalar_tensor_tensor(X[:, m, :], PS[:, 4 + m % 4, :], dinv[:, m:m + 1], X[:, m, :],
                                         ALU.mult, ALU.add).then_inc(S("gnn_done0"), 1)

            def key_max(L, g):
                step(dve.tensor_reduce(kmax[:, g:g + 1], KTrs[L][:, g, :], AX_X, ALU.max, negate=True))
                settle()
                dve.engine_nop().then_inc(S(f"kmax_ready{L}"), 1)

            def q_rows(L):
                w = SLICE if L == 0 else DH
                for m in range(T):
                    dve.wait_ge(*count(f"q_ready{L}", m + 1))
                    ps = PS[:, m % 4, 0:HEADS * w].rearrange("p (h s) -> p h s", h=HEADS)
                    q = Q[:, m, 0:HEADS * w].rearrange("p (h s) -> p h s", h=HEADS)
                    step(dve.tensor_reduce(qm[:, m, :], ps, AX_X, ALU.max))
                    settle()
                    dve.tensor_tensor(q, ps, qm[:, m, :].unsqueeze(2).to_broadcast([P, HEADS, w]), ALU.subtract
                                      ).then_inc(S(f"q_shifted{L}"), 1)
                    dve.wait_ge(*count(f"q_shifted{L}", m + 1))
                    dve.engine_nop().then_inc(S(f"q_done{L}"), 1)

            def q_soft(L):
                w = SLICE if L == 0 else DH
                for m in range(T):
                    q = Q[:, m, 0:HEADS * w].rearrange("p (h s) -> p h s", h=HEADS)
                    dve.wait_ge(*count(f"q_exp{L}", m + 1))
                    step(dve.tensor_reduce(qs[:, m, :], q, AX_X, ALU.add))
                    settle()
                    step(dve.reciprocal(qr[:, m, :], qs[:, m, :]))
                    settle()
                    dve.tensor_tensor(q, q, qr[:, m, :].unsqueeze(2).to_broadcast([P, HEADS, w]), ALU.mult
                                      ).then_inc(S(f"q_soft{L}"), 1)

            def contexts(L):
                groups, hpg, w = (2, 4, SLICE) if L == 0 else (K, 2, DH)
                dve.wait_ge(*count(f"k_exp{L}", groups))
                step(dve.reciprocal(krec[:, 0:groups], ksum[:, 0:groups]))
                settle()
                for g in range(groups):
                    dve.wait_ge(*count(f"kv_ready{L}", g + 1))
                    for h in range(hpg):
                        r = slice(h * w, (h + 1) * w)
                        ins = dve.tensor_scalar(KV[r, g * (D // groups) + h * DH:g * (D // groups) + (h + 1) * DH], PS[r, g, h * DH:(h + 1) * DH],
                                                krec[r, g:g + 1], None, ALU.mult)
                        if h < hpg - 1:
                            step(ins)
                    settle()
                    ins.then_inc(S(f"kv_done{L}"), 1)

            step(dve.memset(KV[:, :], 0.0))
            settle()
            for g in range(2):
                dve.wait_ge(*count("k_done0", 2 * g + 2))
                key_max(0, g)
            q_rows(0)
            q_soft(0)
            split_weights(WOUT)
            contexts(0)
            split_oT(0)
            norm(1, lambda m: add_mix(0, m))

            def router_softmax(n):
                w = (E0, E1)[n]
                pr = PR[:, :, 0:w]
                dve.wait_ge(*count(f"logit_ready{n}", 1))
                ps = PS[:, 7, 0:T * w].rearrange("p (t e) -> p t e", t=T)
                if n == 1:
                    step(dve.tensor_tensor(pr, ps, BG[:, :].unsqueeze(1).to_broadcast([P, T, w]), ALU.add))
                    settle()
                    ps = pr
                step(dve.tensor_reduce(pm[:, :], ps, AX_X, ALU.max))
                settle()
                dve.tensor_tensor(pr, ps, pm[:, :].unsqueeze(2).to_broadcast([P, T, w]), ALU.subtract
                                  ).then_inc(S(f"logit_shifted{n}"), 1)
                dve.wait_ge(*count(f"logit_exp{n}", 1))
                step(dve.tensor_reduce(psm[:, :], pr, AX_X, ALU.add))
                settle()
                step(dve.reciprocal(pr_[:, :], psm[:, :]))
                settle()
                dve.tensor_tensor(pr, pr, pr_[:, :].unsqueeze(2).to_broadcast([P, T, w]), ALU.mult
                                  ).then_inc(S(f"probs_ready{n}"), 1)

            router_softmax(0)
            dve.wait_ge(*count("pT_ready", 1))
            both = PS[0:E0, 0:2, :].rearrange("p a b -> p (a b)")
            step(dve.tensor_copy(PT, both))
            step(dve.tensor_copy(PTW, both))
            settle()
            for r in range(CAP // 8):
                s8 = sc0[:, r * 8:(r + 1) * 8]
                step(dve.max(s8, PTW))
                settle()
                step(dve.max_index(ix0[:, r * 8:(r + 1) * 8], s8, PTW))
                settle()
                step(dve.match_replace(PTW, s8, PTW, -1.0))
                settle()
            step(dve.tensor_scalar(PTW, PTW, 0.0, None, ALU.is_lt))
            dve.tensor_copy(ixf0[:, :], ix0[:, :]).then_inc(S("top_ready"), 1)
            settle()
            dve.tensor_tensor(PTW, PTW, PT, ALU.mult).then_inc(S("top_ready"), 1)
            dve.wait_ge(*count("deg_ready", T + 1))
            dve.reciprocal(rcnt[:, :], PS[:, 2, 0:T]).then_inc(S("deg_done"), 1)
            dve.wait_ge(*count("scT_ready", 1))
            step(dve.tensor_copy(scT[:, :], PS[0:CAP, 0, 0:2 * E0]))
            settle()
            dve.tensor_copy(ic0[:, :], scT[:, 0:E0]).then_inc(S("ic0_ready"), 1)
            dve.engine_nop().then_inc(S("scT_done"), 1)
            dve.wait_ge(*count("rows_added0", T))
            for m in range(T):
                dve.wait_ge(*count("rb_ready0", m + 1))
                dve.tensor_tensor(X[:, m, :], X[:, m, :], PS[:, 4 + m % 4, :], ALU.add).then_inc(S("rb_done0"), 1)

            step(dve.tensor_reduce(most[:, 0:1], CT[:, :, :].rearrange("p a b -> p (a b)"), AX_X, ALU.max))
            settle()
            dve.engine_nop().then_inc(S("most_part"), 1)

            def expert_out(L, i, u, first):
                e = U * i + u
                dve.wait_ge(*count(f"ey_ready{L}", e + 1))
                if L == 0:
                    if not (first and u < 2):
                        dve.wait_ge(*count(f"scattered{u % 2}", 16 * (U // 2 * i + u // 2)))
                    dve.tensor_scalar(Y0[u % 2], PS[0:CAP, 4 + u % 2, :], scT[:, ds(e + E0, 1)], None, ALU.mult
                                      ).then_inc(S("ey_done0"), 1)
                else:
                    if not first:
                        dve.wait_ge(*count(f"y1_out{u}", 16 * i))
                    dve.tensor_copy(Y1[u], PS[0:C, 4 + u % 2, :]).then_inc(S("ey_done1"), 1)

            for u in range(U):
                expert_out(0, 0, u, True)
            with dve.Fori(1, E0 // U) as i:
                for u in range(U):
                    expert_out(0, i, u, False)

            norm(2, add_routed)
            for m in range(T):
                dve.wait_ge(*count("h_rounded1", m + 1))
                dve.tensor_tensor(H_lo[:, m, :], PS[:, 4 + m % 4, :], H_hi[:, m, :].bitcast(F32), ALU.subtract
                                  ).then_inc(S("h_done1"), 1)
            split_tokens(1)
            for m in range(T):
                dve.wait_ge(*count("gnn_ready1", m + 1))
                dve.wait_ge(*count("x_biased2", m + 1))
                dve.scalar_tensor_tensor(X[:, m, :], PS[:, m % 4, :], rcnt[:, m:m + 1], X[:, m, :],
                                         ALU.mult, ALU.add).then_inc(S("gnn_done1"), 1)
            split_weights(WK)
            split_weights(WQ)
            for i in range(2 * K):
                dve.wait_ge(*count("k_ready1", i + 1))
                k = KTrs[1][:, i // 2, (i % 2) * 512:(i % 2 + 1) * 512]
                dve.tensor_scalar(k, PS[:, i % 4, :], 0.0, None, ALU.min).then_inc(S("k_low"), 1)
                dve.wait_ge(*count("k_elu", i + 1))
                dve.scalar_tensor_tensor(k, PS[:, i % 4, :], 0.0, k, ALU.max, ALU.add).then_inc(S("k_done1"), 1)
            split_weights(WV)
            split_weights(WC)
            dve.wait_ge(*count("k_done1", 2 * K))
            for g in range(K):
                key_max(1, g)
            q_rows(1)
            q_soft(1)
            split_weights(WPROJ)
            step(dve.memset(KV[:, :], 0.0))
            settle()
            contexts(1)
            split_oT(1)
            norm(3, lambda m: add_mix(1, m))
            router_softmax(1)
            dve.wait_ge(*count("probs_ready1", 1))
            for t in range(T):
                step(dve.max(top8[:, t, :], PR[:, t, :]))
            settle()
            for t in range(T):
                step(dve.max_index(ti8[:, t, :], top8[:, t, :], PR[:, t, :]))
            settle()
            step(dve.tensor_copy(tif[:, :, :], ti8[:, :, 0:2]))
            settle()
            for t in range(T):
                step(dve.tensor_scalar(O1[:, t, :], iota_e[:, :], tif[:, t, 0:1], None, ALU.is_equal))
                step(dve.tensor_scalar(O2[:, t, :], iota_e[:, :], tif[:, t, 1:2], None, ALU.is_equal))
            settle()
            dve.tensor_tensor(MB, O1, O2, ALU.add).then_inc(S("mb_ready"), 1)
            for t in range(T):
                step(dve.tensor_scalar(SWW[:, t, :], O1[:, t, :], top8[:, t, 0:1], None, ALU.mult))
            settle()
            for t in range(T):
                ins = dve.scalar_tensor_tensor(SWW[:, t, :], O2[:, t, :], top8[:, t, 1:2], SWW[:, t, :],
                                               ALU.mult, ALU.add)
                if t < T - 1:
                    step(ins)
            settle()
            ins.then_inc(S("sww_ready"), 1)
            dve.wait_ge(*count("place_ready", 1))
            step(dve.tensor_tensor(more, PS[:, 2, 0:E1].unsqueeze(2).to_broadcast([P, E1, NC]),
                                   limits[:, :].unsqueeze(1).to_broadcast([P, E1, NC]), ALU.is_gt))
            step(dve.memset(cntb[:, 5, :], 0.0))
            settle()
            step(dve.tensor_reduce(cntb[:, 1, :], more, AX_X, ALU.add))
            settle()
            step(dve.tensor_tensor_scan(cntb[:, 2, :], cntb[:, 1, :], cntb[:, 5, :], 0.0, ALU.add, ALU.add))
            settle()
            step(dve.tensor_tensor(cntb[:, 3, :], cntb[:, 2, :], cntb[:, 1, :], ALU.subtract))
            step(dve.tensor_scalar(cntb[:, 0, :], cntb[:, 2, :], pcol[:, 0:1], None, ALU.is_le))
            settle()
            dve.tensor_reduce(ecol[:, :], cntb[:, 0, :], AX_X, ALU.add).then_inc(S("ecol_ready"), 1)
            step(dve.tensor_scalar(trow[:, P:P + 1], cntb[0:1, 2, E1 - 1:E1], float(U - 1), None, ALU.add))
            settle()
            step(dve.tensor_copy(trow_i[:, P + 1:P + 2], trow[:, P:P + 1]))
            settle()
            dve.tensor_scalar(trow_i[:, P:P + 1], trow_i[:, P + 1:P + 2], U.bit_length() - 1, None,
                              ALU.logical_shift_right).then_inc(S("table_ready"), 1)
            step(dve.tensor_scalar(trow_i[:, P + 1:P + 2], trow_i[:, P + 1:P + 2], -float(U), None, ALU.add))
            settle()
            dve.tensor_scalar(trow_i[:, P + 2:P + 3], trow_i[:, P + 1:P + 2], U.bit_length() - 1, None,
                              ALU.logical_shift_right).then_inc(S("table_ready"), 1)
            for c, o in enumerate((O1, O2)):
                step(dve.tensor_tensor(SL, PS[:, 1, :].rearrange("p (t e) -> p t e", t=T), o, ALU.mult))
                step(dve.tensor_tensor(SLT, cntb[:, 3, :].unsqueeze(1).to_broadcast([P, T, E1]), o, ALU.mult))
                settle()
                step(dve.tensor_reduce(at[:, 0, c * T:(c + 1) * T], SL, AX_X, ALU.add))
                step(dve.tensor_reduce(at[:, 1, c * T:(c + 1) * T], SLT, AX_X, ALU.add))
                settle()
            step(dve.tensor_tensor(place_ge, at[:, 0, :].unsqueeze(2).to_broadcast([P, 2 * T, NC]),
                                   limits[:, :].unsqueeze(1).to_broadcast([P, 2 * T, NC]), ALU.is_ge))
            settle()
            step(dve.tensor_reduce(at[:, 2, :], place_ge, AX_X, ALU.add))
            settle()
            step(dve.scalar_tensor_tensor(at[:, 3, :], at[:, 2, :], -1.0, at[:, 1, :], ALU.add, ALU.add))
            step(dve.tensor_scalar(at[:, 5, :], at[:, 2, :], float(-C), float(C), ALU.mult, ALU.add))
            settle()
            step(dve.tensor_tensor(at[:, 4, :], at[:, 0, :], at[:, 5, :], ALU.add))
            settle()
            for a in range(2 * T):
                step(dve.tensor_scalar(lane_hot[:, a, :], iota_h[:, 0:C], at[:, 4, a:a + 1], None, ALU.is_equal))
                step(dve.tensor_scalar(tile_hot[:, a, :], iota_h[:, 0:MAXT], at[:, 3, a:a + 1], ids[:, a:a + 1],
                                       ALU.is_equal, ALU.mult))
            settle()
            dve.engine_nop().then_inc(S("hot_ready"), 1)
            dve.wait_ge(*count("erow_ready", 1))
            step(dve.tensor_scalar(trow[:, 0:P], PS[0:1, 3, 0:P], float(E1 - 1), None, ALU.min))
            settle()
            dve.tensor_copy(trow_i[:, 0:P], trow[:, 0:P]).then_inc(S("table_ready"), 1)
            dve.wait_ge(*count("rows_summed", 1))
            step(dve.tensor_scalar(rows[:, 0, :], PS[0:C, 0, 0:MAXT], 0.0, float(8 * N), ALU.is_equal, ALU.mult))
            settle()
            step(dve.scalar_tensor_tensor(rows[:, 1, :], PS[0:C, 0, 0:MAXT], -1.0, rows[:, 0, :], ALU.add, ALU.add))
            settle()
            step(dve.tensor_scalar(rows[:, 2, :], rows[:, 1, :], float(N), float(-N), ALU.is_ge, ALU.mult))
            settle()
            step(dve.tensor_tensor(rows[:, 0, :], rows[:, 1, :], rows[:, 2, :], ALU.add))
            settle()
            dve.tensor_copy(rows_i[:, 0, :], rows[:, 0, :]).then_inc(S("rows_ready"), 1)
            dve.tensor_copy(rows_i[:, 1, :], rows[:, 1, :]).then_inc(S("outs_ready"), 1)
            dve.wait_ge(*count("tok_out", 32))
            for m in range(T):
                dve.wait_ge(*count("rb_done1", m + 1))
                step(dve.tensor_tensor(H[:, m, :], H[:, m, :], RB[:, m, :], ALU.add))
            turns = dve.value_load(trow_i[0:1, P:P + 1], min_val=3, max_val=MAXT // U)
            for u in range(U):
                expert_out(1, 0, u, True)
            with dve.Fori(1, turns) as i:
                for u in range(U):
                    expert_out(1, i, u, False)
            settle()
            for m in range(T):
                dve.wait_ge(*count("rows_added1", m + 1))
                step(dve.scalar_tensor_tensor(H[:, m, :], YG[m][:, 1, :], top8[:, m, 1:2], H[:, m, :],
                                              ALU.mult, ALU.add))
                settle()
                stats(4, m, H)
                dve.wait_ge(*count("var_ready4", m + 1))
                step(dve.scalar_tensor_tensor(H[:, m, :], H[:, m, :], mv[:, m, 0:1], BC[:, 0, :],
                                              ALU.subtract, ALU.mult))
                settle()
                dve.wait_ge(*count("sd_ready4", m + 1))
                dve.reciprocal(rs[:, m:m + 1], sd[:, m:m + 1]).then_inc(S("rs_ready"), 1)


_INS = ['x', 'src', 'dst', 'L0_gnn_W', 'L0_gnn_b', 'L0_mix_W_in', 'L0_mix_b_in', 'L0_mix_Wq', 'L0_mix_Wk',
        'L0_mix_Wv', 'L0_mix_W_out', 'L0_mix_b_out', 'L0_ffn_gate_w', 'L0_ffn_w1', 'L0_ffn_b1', 'L0_ffn_w2',
        'L0_ffn_b2', 'L0_ffn_sw1', 'L0_ffn_sb1', 'L0_ffn_sw2', 'L0_ffn_sb2', 'L1_gnn_wc', 'L1_gnn_wn',
        'L1_gnn_bias', 'L1_mix_w_qkv', 'L1_mix_w_proj', 'L1_mix_b_proj', 'L1_ffn_Wg', 'L1_ffn_bg', 'L1_ffn_W1',
        'L1_ffn_b1', 'L1_ffn_W2', 'L1_ffn_b2', 'L1_ffn_gamma', 'L1_ffn_beta']


def kernel(**inputs):
    import numpy as _np
    import concourse.bacc as _bacc
    from concourse import mybir as _mybir
    from concourse.bass_utils import run_bass_kernel_spmd as _run

    nc = _bacc.Bacc("TRN2", target_bir_lowering=False, num_devices=1)
    arrays, aps = {}, {}
    for name in _INS:
        a = _np.ascontiguousarray(inputs[name])
        arrays[f"in_{name}_dram"] = a
        aps[name] = nc.dram_tensor(f"in_{name}_dram", a.shape, _mybir.dt.from_np(a.dtype), kind="ExternalInput").ap()
    out = nc.dram_tensor("out_0_dram", (N, D), _mybir.dt.float32, kind="ExternalOutput").ap()
    build(nc, aps, out)
    r = _run(nc, [arrays], core_ids=[0])
    return r.results[0]["out_0_dram"]
```
